# Optimizing a Trainium2 kernel written in Bass

```python
import numpy as np
import jax
import jax.numpy as jnp

def _softmax(x, axis=-1):
    return jax.nn.softmax(x, axis=axis)

def _gelu(x):
    return jax.nn.gelu(x, approximate=True)

def _silu(x):
    return jax.nn.silu(x)

def _sigmoid(x):
    return jax.nn.sigmoid(x)

def _layernorm(x, axis=-1, eps=1e-05):
    m = jnp.mean(x, axis=axis, keepdims=True)
    v = jnp.var(x, axis=axis, keepdims=True)
    return (x - m) / jnp.sqrt(v + eps)

def _scatter_add(tgt, idx, src, axis=0):
    return tgt.at[idx].add(src)

def _segment_sum(src, seg, n):
    return jax.ops.segment_sum(src, seg, n)
kernel_name = 'mk_audio_tower_d1_tok_audfeat512_r4_3a6343'

def setup_inputs(seed: int=0):
    np.random.seed(seed)
    _w = jnp.asarray

    def _rec_inputs():
        import jax
        import jax.numpy as jnp
        _rk = jax.random.key(seed)
        x = 7.22013e-05 + 1.00017 * jax.random.normal(jax.random.fold_in(_rk, 1), (32, 250, 128), jnp.float32)
        return x
    x = _rec_inputs()

    def _L0_tok_setup():
        import jax, jax.numpy as jnp
        import numpy as np
        H = 8
        TOP_FRAC = 0.2
        EPS = 1e-05

        def _layernorm(x, g, b):
            mu = jnp.mean(x, axis=-1, keepdims=True)
            var = jnp.mean((x - mu) ** 2, axis=-1, keepdims=True)
            return (x - mu) * jax.lax.rsqrt(var + EPS) * g + b
        key = jax.random.key(seed)
        ks = jax.random.split(key, 8)
        B, L, D, F = (8, 512, 128, 512)
        s = 0.02
        return {'x': jax.random.normal(ks[0], (B, L, D), jnp.float32), 'q_w': jax.random.normal(ks[1], (D, D), jnp.float32) * s, 'q_b': jnp.zeros((D,), jnp.float32), 'k_w': jax.random.normal(ks[2], (D, D), jnp.float32) * s, 'k_b': jnp.zeros((D,), jnp.float32), 'v_w': jax.random.normal(ks[3], (D, D), jnp.float32) * s, 'v_b': jnp.zeros((D,), jnp.float32), 'o_w': jax.random.normal(ks[4], (D, D), jnp.float32) * s, 'o_b': jnp.zeros((D,), jnp.float32), 'ln1_g': jnp.ones((D,), jnp.float32), 'ln1_b': jnp.zeros((D,), jnp.float32), 'f1_w': jax.random.normal(ks[5], (D, F), jnp.float32) * s, 'f1_b': jnp.zeros((F,), jnp.float32), 'f2_w': jax.random.normal(ks[6], (F, D), jnp.float32) * s, 'f2_b': jnp.zeros((D,), jnp.float32), 'ln2_g': jnp.ones((D,), jnp.float32), 'ln2_b': jnp.zeros((D,), jnp.float32), 'conv_w': jax.random.normal(ks[7], (D, D, 3), jnp.float32) * s, 'conv_b': jnp.zeros((D,), jnp.float32)}
    _L0_tok_all = _L0_tok_setup()
    _L0_tok_in = {k: v for k, v in _L0_tok_all.items() if k in ('q_w', 'q_b', 'k_w', 'k_b', 'v_w', 'v_b', 'o_w', 'o_b', 'ln1_g', 'ln1_b', 'f1_w', 'f1_b', 'f2_w', 'f2_b', 'ln2_g', 'ln2_b', 'conv_w', 'conv_b')}
    del _L0_tok_all

    def _L0_attn_setup():
        import jax, jax.numpy as jnp
        import numpy as np
        DIM = 128
        HEADS = 8
        HD = DIM // HEADS
        WIN = 64
        HALF = WIN // 2

        def _sliding_window_attn(q, k, v):
            B, H, S, Dh = q.shape
            scale = Dh ** (-0.5)
            pos = jnp.arange(S)
            offsets = list(range(-HALF, HALF + 1))
            scores = []
            for o in offsets:
                k_sh = jnp.roll(k, -o, axis=2)
                s = jnp.einsum('bhsd,bhsd->bhs', q, k_sh) * scale
                valid = (pos + o >= 0) & (pos + o < S)
                s = jnp.where(valid[None, None, :], s, -jnp.inf)
                scores.append(s)
            scores = jnp.stack(scores, axis=-1)
            p = jax.nn.softmax(scores, axis=-1)
            out = jnp.zeros_like(q)
            for idx, o in enumerate(offsets):
                out = out + p[..., idx:idx + 1] * jnp.roll(v, -o, axis=2)
            return out
        key = jax.random.key(seed)
        k0, k1, k2 = jax.random.split(key, 3)
        x = jax.random.normal(k0, (4, 1024, DIM), dtype=jnp.float32)
        W_qkv = jax.random.normal(k1, (DIM, 3 * DIM), dtype=jnp.float32) * 0.02
        b_qkv = jnp.zeros((3 * DIM,), dtype=jnp.float32)
        W_proj = jax.random.normal(k2, (DIM, DIM), dtype=jnp.float32) * 0.02
        b_proj = jnp.zeros((DIM,), dtype=jnp.float32)
        return {'x': x, 'W_qkv': W_qkv, 'b_qkv': b_qkv, 'W_proj': W_proj, 'b_proj': b_proj}
    _L0_attn_all = _L0_attn_setup()
    _L0_attn_in = {k: v for k, v in _L0_attn_all.items() if k in ('W_qkv', 'b_qkv', 'W_proj', 'b_proj')}
    del _L0_attn_all

    def _L0_ffn_setup():
        import jax, jax.numpy as jnp
        import numpy as np
        MARK_AX, OP_ADD, OP_SUB = (0, 1, 2)
        ALU_LO, ALU_HI = (16, 32)
        AX_CARRY_LO, AX_CARRY_HI = (48, 64)
        OPCODE_BASE = 80
        OUTPUT_LO, OUTPUT_HI, CARRY = (128, 144, 160)
        NIB_A, NIB_B, OP_START = (0, 1, 10)
        RESULT, CARRY_OUT = (100, 101)
        GE_POS, GE_DIM = (8, 160)
        OPC_ADD, OPC_SUB = (25, 26)
        B, S, D = (8, 1024, 128)

        def _decode_nibble(x, base):
            return jnp.argmax(x[..., base:base + 16] > 0.5, axis=-1).astype(x.dtype)

        def _pipeline(h, W, b):
            for i in range(3):
                h = jnp.einsum('bspd,od->bspo', h, W[i]) + b[i]
                if i < 2:
                    h = jax.nn.relu(h)
            return h
        key = jax.random.key(seed)
        kx, k1, k2, k3, k4 = jax.random.split(key, 5)
        x_bd = jax.random.uniform(kx, (B, S, D), dtype=jnp.float32)
        Wa = jax.random.normal(k1, (3, GE_DIM, GE_DIM), dtype=jnp.float32) * 0.05
        ba = jax.random.normal(k2, (3, GE_DIM), dtype=jnp.float32) * 0.05
        Ws = jax.random.normal(k3, (3, GE_DIM, GE_DIM), dtype=jnp.float32) * 0.05
        bs = jax.random.normal(k4, (3, GE_DIM), dtype=jnp.float32) * 0.05
        return {'x_bd': x_bd, 'Wa': Wa, 'ba': ba, 'Ws': Ws, 'bs': bs}
    _L0_ffn_all = _L0_ffn_setup()
    _L0_ffn_in = {k: v for k, v in _L0_ffn_all.items() if k in ('Wa', 'ba', 'Ws', 'bs')}
    del _L0_ffn_all
    return {'x': x, 'L0_tok_q_w': _L0_tok_in['q_w'], 'L0_tok_q_b': _L0_tok_in['q_b'], 'L0_tok_k_w': _L0_tok_in['k_w'], 'L0_tok_k_b': _L0_tok_in['k_b'], 'L0_tok_v_w': _L0_tok_in['v_w'], 'L0_tok_v_b': _L0_tok_in['v_b'], 'L0_tok_o_w': _L0_tok_in['o_w'], 'L0_tok_o_b': _L0_tok_in['o_b'], 'L0_tok_ln1_g': _L0_tok_in['ln1_g'], 'L0_tok_ln1_b': _L0_tok_in['ln1_b'], 'L0_tok_f1_w': _L0_tok_in['f1_w'], 'L0_tok_f1_b': _L0_tok_in['f1_b'], 'L0_tok_f2_w': _L0_tok_in['f2_w'], 'L0_tok_f2_b': _L0_tok_in['f2_b'], 'L0_tok_ln2_g': _L0_tok_in['ln2_g'], 'L0_tok_ln2_b': _L0_tok_in['ln2_b'], 'L0_tok_conv_w': _L0_tok_in['conv_w'], 'L0_tok_conv_b': _L0_tok_in['conv_b'], 'L0_attn_W_qkv': _L0_attn_in['W_qkv'], 'L0_attn_b_qkv': _L0_attn_in['b_qkv'], 'L0_attn_W_proj': _L0_attn_in['W_proj'], 'L0_attn_b_proj': _L0_attn_in['b_proj'], 'L0_ffn_Wa': _L0_ffn_in['Wa'], 'L0_ffn_ba': _L0_ffn_in['ba'], 'L0_ffn_Ws': _L0_ffn_in['Ws'], 'L0_ffn_bs': _L0_ffn_in['bs']}

def reference(x, L0_tok_q_w, L0_tok_q_b, L0_tok_k_w, L0_tok_k_b, L0_tok_v_w, L0_tok_v_b, L0_tok_o_w, L0_tok_o_b, L0_tok_ln1_g, L0_tok_ln1_b, L0_tok_f1_w, L0_tok_f1_b, L0_tok_f2_w, L0_tok_f2_b, L0_tok_ln2_g, L0_tok_ln2_b, L0_tok_conv_w, L0_tok_conv_b, L0_attn_W_qkv, L0_attn_b_qkv, L0_attn_W_proj, L0_attn_b_proj, L0_ffn_Wa, L0_ffn_ba, L0_ffn_Ws, L0_ffn_bs):
    import jax
    import jax.numpy as jnp

    def _L0_tok_ref(x, q_w, q_b, k_w, k_b, v_w, v_b, o_w, o_b, ln1_g, ln1_b, f1_w, f1_b, f2_w, f2_b, ln2_g, ln2_b, conv_w, conv_b):
        import jax, jax.numpy as jnp
        import numpy as np
        H = 8
        TOP_FRAC = 0.2
        EPS = 1e-05

        def _layernorm(x, g, b):
            mu = jnp.mean(x, axis=-1, keepdims=True)
            var = jnp.mean((x - mu) ** 2, axis=-1, keepdims=True)
            return (x - mu) * jax.lax.rsqrt(var + EPS) * g + b
        B, L, D = x.shape
        hd = D // H
        scale = hd ** (-0.5)
        k_top = max(1, int(L * TOP_FRAC))

        def split_heads(t):
            return t.reshape(B, L, H, hd).transpose(0, 2, 1, 3)
        q = split_heads(x @ q_w + q_b)
        k = split_heads(x @ k_w + k_b)
        v = split_heads(x @ v_w + v_b)
        q_norm = jnp.sum(q * q, axis=-1)
        _, top_idx = jax.lax.top_k(q_norm, k_top)
        bi = jnp.arange(B)[:, None, None]
        hi = jnp.arange(H)[None, :, None]
        mask = jnp.zeros((B, H, L), bool).at[bi, hi, top_idx].set(True)
        q = q * mask[..., None]
        scores = jnp.einsum('bhld,bhmd->bhlm', q, k) * scale
        probs = jax.nn.softmax(scores, axis=-1)
        attn = jnp.einsum('bhlm,bhmd->bhld', probs, v)
        attn = attn.transpose(0, 2, 1, 3).reshape(B, L, D)
        attn_out = attn @ o_w + o_b
        h1 = _layernorm(x + attn_out, ln1_g, ln1_b)
        ff = jax.nn.relu(h1 @ f1_w + f1_b) @ f2_w + f2_b
        h2 = _layernorm(h1 + ff, ln2_g, ln2_b)
        fused = h2 + attn_out
        y = fused.transpose(0, 2, 1)
        y = jax.lax.conv_general_dilated(y, conv_w, window_strides=(1,), padding=[(1, 1)], dimension_numbers=('NCH', 'OIH', 'NCH')) + conv_b[None, :, None]
        y = jax.nn.relu(y)
        y = y.reshape(B, D, L // 2, 2).max(axis=-1)
        return y.transpose(0, 2, 1)

    def _L0_attn_ref(x, W_qkv, b_qkv, W_proj, b_proj):
        import jax, jax.numpy as jnp
        import numpy as np
        DIM = 128
        HEADS = 8
        HD = DIM // HEADS
        WIN = 64
        HALF = WIN // 2

        def _sliding_window_attn(q, k, v):
            B, H, S, Dh = q.shape
            scale = Dh ** (-0.5)
            pos = jnp.arange(S)
            offsets = list(range(-HALF, HALF + 1))
            scores = []
            for o in offsets:
                k_sh = jnp.roll(k, -o, axis=2)
                s = jnp.einsum('bhsd,bhsd->bhs', q, k_sh) * scale
                valid = (pos + o >= 0) & (pos + o < S)
                s = jnp.where(valid[None, None, :], s, -jnp.inf)
                scores.append(s)
            scores = jnp.stack(scores, axis=-1)
            p = jax.nn.softmax(scores, axis=-1)
            out = jnp.zeros_like(q)
            for idx, o in enumerate(offsets):
                out = out + p[..., idx:idx + 1] * jnp.roll(v, -o, axis=2)
            return out
        B, S, _ = x.shape
        qkv = (x @ W_qkv + b_qkv).reshape(B, S, 3, HEADS, HD)
        qkv = jnp.transpose(qkv, (2, 0, 3, 1, 4))
        q, k, v = (qkv[0], qkv[1], qkv[2])
        attn = _sliding_window_attn(q, k, v)
        attn = jnp.transpose(attn, (0, 2, 1, 3)).reshape(B, S, DIM)
        return attn @ W_proj + b_proj

    def _L0_ffn_ref(x_bd, Wa, ba, Ws, bs):
        import jax, jax.numpy as jnp
        import numpy as np
        MARK_AX, OP_ADD, OP_SUB = (0, 1, 2)
        ALU_LO, ALU_HI = (16, 32)
        AX_CARRY_LO, AX_CARRY_HI = (48, 64)
        OPCODE_BASE = 80
        OUTPUT_LO, OUTPUT_HI, CARRY = (128, 144, 160)
        NIB_A, NIB_B, OP_START = (0, 1, 10)
        RESULT, CARRY_OUT = (100, 101)
        GE_POS, GE_DIM = (8, 160)
        OPC_ADD, OPC_SUB = (25, 26)
        B, S, D = (8, 1024, 128)

        def _decode_nibble(x, base):
            return jnp.argmax(x[..., base:base + 16] > 0.5, axis=-1).astype(x.dtype)

        def _pipeline(h, W, b):
            for i in range(3):
                h = jnp.einsum('bspd,od->bspo', h, W[i]) + b[i]
                if i < 2:
                    h = jax.nn.relu(h)
            return h
        x = x_bd
        Bsz, seq, _ = x.shape
        x_ge = jnp.zeros((Bsz, seq, GE_POS, GE_DIM), dtype=x.dtype)
        x_ge = x_ge.at[..., 0, NIB_A].set(_decode_nibble(x, ALU_LO))
        x_ge = x_ge.at[..., 1, NIB_A].set(_decode_nibble(x, ALU_HI))
        x_ge = x_ge.at[..., 0, NIB_B].set(_decode_nibble(x, AX_CARRY_LO))
        x_ge = x_ge.at[..., 1, NIB_B].set(_decode_nibble(x, AX_CARRY_HI))
        x_ge = x_ge.at[..., :, OP_START + OPC_ADD].set(x[..., OPCODE_BASE + OPC_ADD][..., None])
        x_ge = x_ge.at[..., :, OP_START + OPC_SUB].set(x[..., OPCODE_BASE + OPC_SUB][..., None])
        mark = x[..., MARK_AX] > 0.5
        m_add = mark & (x[..., OP_ADD] > 0.5)
        m_sub = mark & ~(x[..., OP_ADD] > 0.5) & (x[..., OP_SUB] > 0.5)
        active = (m_add | m_sub).astype(x.dtype)
        y_add = _pipeline(x_ge, Wa, ba)
        y_sub = _pipeline(x_ge, Ws, bs)
        y = jnp.where(m_add[..., None, None], y_add, jnp.where(m_sub[..., None, None], y_sub, x_ge))
        res_lo = jnp.clip(jnp.round(y[..., 0, RESULT]), 0, 15).astype(jnp.int32)
        res_hi = jnp.clip(jnp.round(y[..., 1, RESULT]), 0, 15).astype(jnp.int32)
        oh_lo = jax.nn.one_hot(res_lo, 16, dtype=x.dtype) * active[..., None]
        oh_hi = jax.nn.one_hot(res_hi, 16, dtype=x.dtype) * active[..., None]
        carry = (jnp.round(y[..., 1, CARRY_OUT]) > 0.5).astype(x.dtype) * active
        out = x
        out = out.at[..., OUTPUT_LO:OUTPUT_LO + 16].add(2.0 * oh_lo)
        out = out.at[..., OUTPUT_HI:OUTPUT_HI + 16].add(2.0 * oh_hi)
        out = out.at[..., CARRY].add(carry)
        return out
    h = _L0_tok_ref(x, L0_tok_q_w, L0_tok_q_b, L0_tok_k_w, L0_tok_k_b, L0_tok_v_w, L0_tok_v_b, L0_tok_o_w, L0_tok_o_b, L0_tok_ln1_g, L0_tok_ln1_b, L0_tok_f1_w, L0_tok_f1_b, L0_tok_f2_w, L0_tok_f2_b, L0_tok_ln2_g, L0_tok_ln2_b, L0_tok_conv_w, L0_tok_conv_b)
    h = h + _L0_attn_ref(_layernorm(h, axis=-1), L0_attn_W_qkv, L0_attn_b_qkv, L0_attn_W_proj, L0_attn_b_proj)
    h = h + _L0_ffn_ref(_layernorm(h, axis=-1), L0_ffn_Wa, L0_ffn_ba, L0_ffn_Ws, L0_ffn_bs)
    return h

_drawn_inputs = setup_inputs


def setup_inputs(seed=0):
    import zlib

    import numpy as np

    out = dict(_drawn_inputs(seed))
    spreads = {'L0_tok_q_b': (0.0, 0.8),
     'L0_tok_k_b': (0.0, 0.8),
     'L0_tok_v_b': (0.0, 0.1),
     'L0_tok_o_b': (0.0, 0.1),
     'L0_tok_ln1_g': (1.0, 0.2),
     'L0_tok_ln1_b': (0.0, 0.1),
     'L0_tok_f1_b': (0.0, 0.1),
     'L0_tok_f2_b': (0.0, 0.1),
     'L0_tok_ln2_g': (1.0, 0.2),
     'L0_tok_ln2_b': (0.0, 0.1),
     'L0_tok_conv_b': (0.0, 0.1),
     'L0_attn_b_qkv': (0.0, 0.1),
     'L0_attn_b_proj': (0.0, 0.1)}
    factors = {'L0_tok_q_w': 8.0, 'L0_tok_k_w': 8.0, 'L0_tok_v_w': 8.0}
    for name, (base, spread) in spreads.items():
        noise = np.random.default_rng([zlib.crc32(name.encode()), seed]).standard_normal(out[name].shape)
        drawn = base * np.exp(spread * noise) if base else spread * noise
        out[name] = jnp.asarray(drawn.astype(out[name].dtype))
    for name, factor in factors.items():
        out[name] = (out[name] * factor).astype(out[name].dtype)
    return out
```

```python
from contextlib import ExitStack

import numpy as np
import concourse.bass as bass
from concourse import mybir

F32 = mybir.dt.float32
BF16 = mybir.dt.bfloat16
ALU = mybir.AluOpType
ACT = mybir.ActivationFunctionType
AX = mybir.AxisListType.X

B, L, D, H, F = 32, 250, 128, 8, 512
HD = D // H
LH = L // 2
KTOP = L // 5
NPAIR = B // 2
HC = H // 2
CW = 2 * HD
ROWS = 2 * KTOP
HALF = 32
EPS = 1e-5
SCALE = HD ** -0.5
OFF = -3.0e38

CONST = {}
WEIGHT = {}


def _columns(table, *sizes):
    at = 0
    for name, n in sizes:
        table[name] = slice(at, at + n)
        at += n
    return at


NCONST = _columns(CONST, ("ident", 128), ("qmask", 2 * ROWS), ("omask", ROWS), ("kmask", 4), ("sidx", 1),
                  ("siota", KTOP * H), ("band", 4 * LH), ("parity", 2), ("eps", 1), ("ones", CW))
NWEIGHT = _columns(WEIGHT, ("q", D), ("k", D), ("v", D), ("o", D), ("f1", F), ("f2", F), ("conv", 3 * D),
                   ("wq", D), ("wk", D), ("wv", D), ("wp", D))
COLS = ["k_b", "v_b", "ln1_g", "ln1_b", "f1_0", "f1_1", "f1_2", "f1_3", "conv_b", "wq_b", "wk_b"]
RWS = ["q_b", "o_b", "ln1_g", "ln1_b", "f2_b", "ln2_g", "ln2_b", "wv_b", "wp_b"]


def constants():
    c = np.zeros((128, NCONST), np.float32)
    p = np.arange(128)
    c[:, CONST["ident"]] = np.eye(128)
    j = np.arange(ROWS)
    own = (p[:, None] % CW) // HD == j[None, :] % 2
    qm = np.stack([own & ((p[:, None] % 64) // CW == cc) for cc in range(2)], 1)
    c[:, CONST["qmask"]] = (qm * SCALE).reshape(128, -1)
    c[:, CONST["omask"]] = own
    c[:, CONST["kmask"]] = ((p[:, None] % 64) // HD == np.arange(4)[None, :]) * SCALE
    c[:, CONST["sidx"]] = (p // 2 + 1)[:, None]
    c[:, CONST["siota"]] = np.repeat(np.arange(1, KTOP + 1), H)[None, :]
    away = np.abs(p[:, None] - np.arange(LH)[None, :]) > HALF
    c[:, CONST["band"]] = np.tile(np.where(away, OFF, 0.0), (1, 4))
    c[:, CONST["parity"]] = (p[:, None] % CW) // HD == np.arange(2)[None, :]
    c[:, CONST["eps"]] = EPS
    c[:, CONST["ones"]] = 1.0
    return c


def wait(eng, sem, value):
    if isinstance(value, int) and value <= 0:
        return
    eng.wait_ge(sem, value)


def within(u, lo, hi):
    return not isinstance(u, int) or lo <= u < hi


def steps(eng, slot, first, lo, hi, last):
    for u in range(first, lo):
        slot(u // 2, u % 2)
    with eng.Fori(lo // 2, (hi + 1) // 2) as h:
        slot(h, 0)
        slot(h, 1)
    for u in range(hi + 1, last + 1):
        slot(u // 2, u % 2)


def shift(h, p, k):
    h, p = h + (p + k) // 2, (p + k) % 2
    return 2 * h + p, h, p


def program(nc, xT, xtok, weights, consts, cols, rows, key_dram, out):
    with ExitStack() as ctx:
        def sb(name, shape, dt=F32):
            return ctx.enter_context(nc.sbuf_tensor(name, shape, dt))

        S = {
            "nc": nc, "xT": xT, "xtok": xtok, "key_dram": key_dram, "out": out,
            "weights_dram": weights, "consts_dram": consts, "cols_dram": cols, "rows_dram": rows,
            "w": sb("w", [128, NWEIGHT]), "c": sb("c", [128, NCONST]),
            "cols": sb("vec_cols", [128, len(COLS)]), "rows": sb("vec_rows", [128, len(RWS), D]),
            "banks": [ctx.enter_context(nc.psum_tensor(f"bank{i}", [128, 512], F32)) for i in range(8)],
            "xneg": sb("xneg", [128, B]), "meanv": sb("meanv", [128, B]),
        }
        S["n3T_all"] = sb("n3T_all", [128, B * LH])
        S["z_all"] = sb("z_all", [LH, B, D])
        S["attn_all"] = sb("attn_all", [128, B * L])
        with ExitStack() as early:
            S["q_all"] = early.enter_context(nc.sbuf_tensor("q_all", [LH, B * 2 * D], F32))
            S["key_all"] = early.enter_context(nc.sbuf_tensor("key_all", [LH, 2, B, H], F32))
            measure_and_select(S)
            topk_attention(S)
        ffn_conv(S)
        window_attention(S)


def measure_and_select(S):
    nc, w, c, cols, rows, banks = (S[k] for k in ("nc", "w", "c", "cols", "rows", "banks"))
    q_all, key_all, xneg, meanv = (S[k] for k in ("q_all", "key_all", "xneg", "meanv"))
    W = L + 8
    with ExitStack() as ctx:
        def sb(name, shape, dt=F32):
            return ctx.enter_context(nc.sbuf_tensor(name, shape, dt))

        def sem(name):
            return ctx.enter_context(nc.semaphore(name))

        xa = [sb(f"xa{p}", [128, 2 * L]) for p in range(2)]
        sq = [sb(f"sq{p}", [LH, 4 * D]) for p in range(2)]
        norm_all = sb("norm_all", [LH, 2, B, H])
        xsum = sb("xsum", [128, B])
        work = [[sb(f"work{g}{i}", [128, W]) for i in range(2)] for g in range(2)]
        top8 = [sb(f"top8_{g}", [128, 8]) for g in range(2)]
        chosen = [sb(f"chosen{g}", [128, L]) for g in range(2)]
        prefix = [sb(f"prefix{g}", [128, L]) for g in range(2)]
        zeros = sb("zeros", [128, L])
        key = [sb(f"key{g}", [128, L]) for g in range(2)]
        key16 = [sb(f"key16_{g}", [128, L], BF16) for g in range(2)]

        params_in = [sem(f"m_params{i}") for i in range(4)]
        x_in = [sem(f"m_x_in{p}") for p in range(2)]
        q_ready, q_done, xsum_done = sem("m_q_ready"), sem("m_q_done"), sem("m_xsum_done")
        sq_done, norm_done = sem("m_sq_done"), sem("m_norm_done")
        mean_ready, norm_t_ready, key_t_ready = sem("m_mean_ready"), sem("m_norm_t_ready"), sem("m_key_t_ready")
        select, key_stored, key_ready, key_t_done = sem("m_select"), sem("m_key_stored"), sem("m_key_ready"), sem("m_key_t_done")
        ident = c[:, CONST["ident"]]
        block = ctx.enter_context(nc.Block())

        @block.sync
        def _(sp):
            sp.dma_start(w[:, :], S["weights_dram"]).then_inc(params_in[0], 16)

            def slot(h, p):
                t, _, _ = shift(h, p, 0)
                wait(sp, q_ready, t - 1)
                wait(sp, xsum_done, t - 1)
                sp.dma_start(xa[p][:, :], S["xT"][:, bass.ds(t * 2 * L, 2 * L)]).then_inc(x_in[p], 16)

            steps(sp, slot, 0, 2, NPAIR - 1, NPAIR - 1)
            for g in range(2):
                sp.wait_ge(key_ready, g + 1)
                sp.dma_start(S["key_dram"][128 * g:128 * g + 128, :], key16[g][:, :]).then_inc(key_stored, 16)
            sp.wait_ge(key_stored, 32)

        @block.scalar
        def _(act):
            act.dma_start(rows[:, :, :].rearrange("p a b -> p (a b)"),
                          S["rows_dram"].partition_broadcast(128)).then_inc(params_in[1], 16)
            act.dma_start(c[:, :], S["consts_dram"]).then_inc(params_in[2], 16)
            act.dma_start(cols[:, :], S["cols_dram"]).then_inc(params_in[3], 16)

            def slot(h, p):
                t, _, _ = shift(h, p, 0)
                wait(act, q_done, t + 1)
                wait(act, norm_done, t - 1)
                nc.scalar.activation(sq[p][:, :], q_all[:, bass.ds(t * 4 * D, 4 * D)], ACT.Square).then_inc(sq_done, 1)

            steps(act, slot, 0, 2, NPAIR - 1, NPAIR - 1)

        @block.tensor
        def _(pe):
            pe.wait_ge(params_in[0], 16)

            def slot(h, p):
                t, half, _ = shift(h, p, 0)
                pe.wait_ge(x_in[p], 16 * half + 16)
                wait(pe, q_done, t - 1)
                for j in range(4):
                    last = nc.tensor.matmul(banks[p][0:LH, D * j:D * j + D], xa[p][:, LH * j:LH * j + LH],
                                            w[:, WEIGHT["q"]], start=True, stop=True)
                last.then_inc(q_ready, 1)

            steps(pe, slot, 0, 2, NPAIR - 1, NPAIR - 1)
            pe.wait_ge(xsum_done, NPAIR)
            nc.tensor.matmul(banks[2][:, 0:B], w[:, WEIGHT["v"]], xsum[:, :], start=True, stop=True).then_inc(mean_ready, 1)
            pe.wait_ge(params_in[2], 16)
            pe.wait_ge(norm_done, NPAIR)
            for g in range(2):
                for lt in range(2):
                    last = nc.tensor.transpose(banks[3 + g][:, LH * lt:LH * lt + LH],
                                               norm_all[:, lt, 16 * g:16 * g + 16, :].rearrange("p b h -> p (b h)"),
                                               ident[0:LH, 0:LH])
                last.then_inc(norm_t_ready, 1)
            for g in range(2):
                pe.wait_ge(key_ready, g + 1)
                for lt in range(2):
                    last = nc.tensor.transpose(banks[5 + g][0:LH, D * lt:D * lt + D], key[g][:, LH * lt:LH * lt + LH], ident)
                last.then_inc(key_t_ready, 1)

        @block.vector
        def _(dve):
            dve.wait_ge(params_in[1], 16)

            def slot(h, p):
                t, half, _ = shift(h, p, 0)
                dve.wait_ge(q_ready, t + 1)
                nc.vector.tensor_tensor(q_all[:, bass.ds(t * 4 * D, 4 * D)].rearrange("p (a b) -> p a b", b=D),
                                        banks[p][0:LH, :].rearrange("p (a b) -> p a b", b=D),
                                        rows[0:LH, RWS.index("q_b"):RWS.index("q_b") + 1, :].to_broadcast([LH, 4, D]),
                                        ALU.add).then_inc(q_done, 1)
                dve.wait_ge(x_in[p], 16 * half + 16)
                nc.vector.reduce_sum(xsum[:, bass.ds(t * 2, 2)], xa[p][:, :].rearrange("p (b l) -> p b l", b=2),
                                     axis=AX).then_inc(xsum_done, 1)
                wait(dve, sq_done, t + 1)
                nc.vector.reduce_sum(norm_all[:, :, bass.ds(t * 2, 2), :].rearrange("p l b h -> p b l h"),
                                     sq[p][:, :].rearrange("p (b l h d) -> p b l h d", b=2, l=2, h=H),
                                     axis=AX).then_inc(norm_done, 1)

            steps(dve, slot, 0, 2, NPAIR - 1, NPAIR - 1)

            n = [0]

            def link(ins):
                n[0] += 1
                ins.then_inc(select, 1)

            def joined():
                dve.wait_ge(select, n[0])

            link(nc.vector.memset(zeros[:, :], 0.0))
            for g in range(2):
                link(nc.vector.memset(work[g][0][:, L:W], -2.0))
            dve.wait_ge(mean_ready, 1)
            dve.wait_ge(params_in[3], 16)
            dve.wait_ge(xsum_done, NPAIR)
            nc.vector.tensor_scalar(meanv[:, :], banks[2][:, 0:B], 1.0 / L, cols[:, COLS.index("v_b"):COLS.index("v_b") + 1],
                                    ALU.mult, ALU.add)
            nc.vector.tensor_scalar_mul(xneg[:, :], xsum[:, :], -1.0 / L)
            for g in range(2):
                dve.wait_ge(norm_t_ready, g + 1)
                link(nc.vector.tensor_copy(work[g][0][:, 0:L], banks[3 + g][:, 0:L]))
            joined()
            rounds = (KTOP + 7) // 8
            for r in range(rounds):
                for g in range(2):
                    link(nc.vector.max(top8[g][:, :], work[g][r % 2][:, 0:L]))
                joined()
                if r == rounds - 1:
                    for g in range(2):
                        link(nc.vector.memset(top8[g][:, KTOP - 8 * r:8], -2.0))
                    joined()
                for g in range(2):
                    link(nc.vector.match_replace(work[g][(r + 1) % 2][:, :], top8[g][:, :], work[g][r % 2][:, :], -1.0))
                joined()
            end = rounds % 2
            for g in range(2):
                link(nc.vector.tensor_scalar(chosen[g][:, :], work[g][end][:, 0:L], -1.0, None, ALU.is_equal))
            joined()
            for g in range(2):
                link(nc.vector.tensor_tensor_scan(prefix[g][:, :], chosen[g][:, :], zeros[:, :], 0.0, ALU.add, ALU.add))
            joined()
            for g in range(2):
                link(nc.vector.tensor_tensor(key[g][:, :], prefix[g][:, :], chosen[g][:, :], ALU.mult))
            joined()
            for g in range(2):
                nc.vector.tensor_copy(key16[g][:, :], key[g][:, :]).then_inc(key_ready, 1)
            for g in range(2):
                dve.wait_ge(key_t_ready, g + 1)
                nc.vector.tensor_copy(key_all[:, :, 16 * g:16 * g + 16, :],
                                      banks[5 + g][0:LH, 0:2 * D].rearrange("p (l b h) -> p l b h", l=2, h=H)).then_inc(key_t_done, 1)


def topk_attention(S):
    nc, w, c, cols, banks = (S[k] for k in ("nc", "w", "c", "cols", "banks"))
    q_all, key_all, xneg, meanv, attn_all = (S[k] for k in ("q_all", "key_all", "xneg", "meanv", "attn_all"))
    with ExitStack() as ctx:
        def sb(name, shape, dt=F32):
            return ctx.enter_context(nc.sbuf_tensor(name, shape, dt))

        def sem(name):
            return ctx.enter_context(nc.semaphore(name))

        def pair(name, shape, dt=F32):
            return [sb(f"{name}{p}", shape, dt) for p in range(2)]

        x1 = pair("x1_", [128, L])
        xc = pair("xc_", [128, L])
        q1 = pair("q1_", [LH, 2, D])
        keyb = pair("keyb_", [ROWS, HC, L], BF16)
        pick = pair("pick_", [LH, 2, KTOP, H])
        put = pair("put_", [ROWS, HC, L])
        qsel = pair("qsel_", [128, 2, ROWS])
        kT = pair("kT_", [128, L])
        v1 = pair("v1_", [LH, 2, D])
        negmax = pair("negmax_", [ROWS, HC])
        rowsum = pair("rowsum_", [ROWS, HC])
        rinv = pair("rinv_", [ROWS, HC])
        probs = pair("probs_", [ROWS, HC, L])
        probsT = sb("probsT", [LH, 2, HC, ROWS])
        oT = sb("oT", [128, ROWS])
        osel = pair("osel_", [ROWS, HC, CW])

        x_in = [sem(f"a_x_in{p}") for p in range(2)]
        q_in = [sem(f"a_q_in{p}") for p in range(2)]
        key_in = [sem(f"a_key_in{p}") for p in range(2)]
        xc_done, kv_ready, kT_done, v_done = sem("a_xc_done"), sem("a_kv_ready"), sem("a_kT_done"), sem("a_v_done")
        pick_done, gathered, qsel_done = sem("a_pick_done"), sem("a_gathered"), sem("a_qsel_done")
        scores0, scores1, max_done, exp_done = sem("a_scores0"), sem("a_scores1"), sem("a_max_done"), sem("a_exp_done")
        rinv_done, pT_ready, pT0_done, pT1_done = sem("a_rinv_done"), sem("a_pT_ready"), sem("a_pT0_done"), sem("a_pT1_done")
        pv_ready, oT_done, o_ready, osel_done = sem("a_pv_ready"), sem("a_oT_done"), sem("a_o_ready"), sem("a_osel_done")
        put_done, scattered, attn_done = sem("a_put_done"), sem("a_scattered"), sem("a_attn_done")

        s_bank, t_bank, kv_bank, g_bank, o_bank, a_bank = banks[0:2], banks[2:4], banks[4], banks[5], banks[6], banks[7]
        ident = c[:, CONST["ident"]]
        RUN = (-2, 4, B - 3, B + 1)
        block = ctx.enter_context(nc.Block())

        @block.sync
        def _(sp):
            def slot(h, p):
                v, _, _ = shift(h, p, 0)
                wait(sp, kv_ready, v - 1)
                wait(sp, xc_done, v - 1)
                sp.dma_start(x1[p][:, :], S["xT"][:, bass.ds(v * L, L)]).then_inc(x_in[p], 16)
                wait(sp, gathered, v - 1)
                sp.dma_start(q1[p][:, :, :].rearrange("p a b -> p (a b)"),
                             q_all[:, bass.ds(v * 2 * D, 2 * D)]).then_inc(q_in[p], 16)
                wait(sp, put_done, v - 1)
                for hh in range(2):
                    src = S["key_dram"].rearrange("(b c hh) l -> b hh c l", c=HC, hh=2)[bass.ds(v, 1), hh, :, :]
                    sp.dma_start(keyb[p][hh:ROWS:2, :, :], src.to_broadcast([KTOP, HC, L])).then_inc(key_in[p], 16)

            steps(sp, slot, 0, 4, B - 1, B - 1)

        @block.gpsimd
        def _(pool):
            def slot(h, p):
                v, half, _ = shift(h, p, 0)
                pool.wait_ge(x_in[p], 16 * half + 16)
                wait(pool, kv_ready, v)
                nc.gpsimd.tensor_tensor(xc[p][:, :], x1[p][:, :], xneg[:, bass.ds(v, 1)].to_broadcast([128, L]), ALU.add).then_inc(xc_done, 1)

            steps(pool, slot, 0, 4, B - 1, B - 1)

        @block.tensor
        def _(pe):
            def slot(h, p):
                u, _, _ = shift(h, p, 0)
                u1, h1, p1 = shift(h, p, 1)
                um, _, pm = shift(h, p, -1)
                if within(u, 0, B):
                    pe.wait_ge(qsel_done, u + 1)
                    pe.wait_ge(kT_done, u + 1)
                    wait(pe, exp_done, 4 * u)
                    for ch in (0, 2, 1, 3):
                        r, cc = ch // 2, ch % 2
                        ins = nc.tensor.matmul(s_bank[r][0:ROWS, L * cc:L * cc + L], qsel[p][64 * r:64 * r + 64, cc, :],
                                               kT[p][64 * r:64 * r + 64, :], start=True, stop=True)
                        if cc:
                            ins.then_inc((scores0, scores1)[r], 1)
                if within(u, 2, B + 2):
                    wait(pe, oT_done, u - 1)
                    wait(pe, osel_done, u - 2)
                    nc.tensor.transpose(o_bank[0:ROWS, 128:256], oT[:, :], ident).then_inc(o_ready, 1)
                if within(u, 1, B + 1):
                    wait(pe, exp_done, 4 * u)
                    wait(pe, pT0_done, u - 1)
                    wait(pe, pT1_done, u - 1)
                    for lt in range(2):
                        for ch in range(HC):
                            ins = nc.tensor.transpose(t_bank[lt][0:LH, ROWS * ch:ROWS * ch + ROWS],
                                                      probs[pm][:, ch, LH * lt:LH * lt + LH], ident[0:ROWS, 0:ROWS])
                        ins.then_inc(pT_ready, 1)
                if within(u, -1, B):
                    wait(pe, kT_done, u + 1)
                    wait(pe, v_done, u)
                    if within(u, -1, B - 1):
                        pe.wait_ge(x_in[p1], 16 * h1 + 16)
                        ins = nc.tensor.matmul(kv_bank[:, 0:L], w[:, WEIGHT["k"]], x1[p1][:, :], start=True, stop=True)
                    if within(u, 0, B):
                        pe.wait_ge(xc_done, u + 1)
                        for lt in range(2):
                            ins = nc.tensor.matmul(kv_bank[0:LH, 256 + D * lt:256 + D * lt + D],
                                                   xc[p][:, LH * lt:LH * lt + LH], w[:, WEIGHT["v"]], start=True, stop=True)
                    ins.then_inc(kv_ready, 1)
                if within(u, 2, B + 2):
                    wait(pe, osel_done, u - 1)
                    wait(pe, put_done, u - 1)
                    wait(pe, attn_done, u - 2)
                    for ch in range(HC):
                        ins = nc.tensor.matmul(a_bank[CW * ch:CW * ch + CW, 0:L], osel[p][:, ch, :], put[p][:, ch, :],
                                               start=True, stop=True)
                    ins.then_inc(scattered, 1)
                if within(u, -1, B - 1):
                    pe.wait_ge(q_in[p1], 16 * h1 + 16)
                    pe.wait_ge(pick_done, u + 2)
                    wait(pe, qsel_done, u + 1)
                    for lt in range(2):
                        for ch in range(HC):
                            ins = nc.tensor.matmul(g_bank[CW * ch:CW * ch + CW, 0:ROWS], q1[p1][:, lt, CW * ch:CW * ch + CW],
                                                   pick[p1][:, lt, :, 2 * ch:2 * ch + 2], start=lt == 0, stop=lt == 1)
                    ins.then_inc(gathered, 1)
                if within(u, 1, B + 1):
                    pe.wait_ge(pT0_done, u)
                    pe.wait_ge(pT1_done, u)
                    pe.wait_ge(v_done, u)
                    wait(pe, oT_done, u - 1)
                    wait(pe, osel_done, u - 1)
                    for lt in range(2):
                        for ch in range(HC):
                            ins = nc.tensor.matmul(o_bank[CW * ch:CW * ch + CW, 0:ROWS], v1[pm][:, lt, CW * ch:CW * ch + CW],
                                                   probsT[:, lt, ch, :], start=lt == 0, stop=lt == 1)
                    ins.then_inc(pv_ready, 1)

            steps(pe, slot, *RUN)

        @block.vector
        def _(dve):
            def slot(h, p):
                u, hf, _ = shift(h, p, 0)
                u2, _, p2 = shift(h, p, 2)
                _, _, p1 = shift(h, p, 1)
                _, _, pm = shift(h, p, -1)
                if within(u, 0, B):
                    for r in range(2):
                        dve.wait_ge((scores0, scores1)[r], u + 1)
                        nc.vector.tensor_reduce(negmax[p][:, 2 * r:2 * r + 2],
                                                s_bank[r][0:ROWS, 0:2 * L].rearrange("p (c l) -> p c l", c=2),
                                                AX, ALU.max, negate=True).then_inc(max_done, 1)
                if within(u, 1, B + 1):
                    dve.wait_ge(exp_done, 4 * u)
                    wait(dve, osel_done, u - 2)
                    nc.vector.reciprocal(rinv[pm][:, :], rowsum[pm][:, :]).then_inc(rinv_done, 1)
                if within(u, 2, B + 2):
                    dve.wait_ge(o_ready, u - 1)
                    dve.wait_ge(rinv_done, u - 1)
                    wait(dve, scattered, u - 3)
                    nc.vector.tensor_tensor(osel[p][:, :, :], o_bank[0:ROWS, 128:256].rearrange("p (c f) -> p c f", c=HC),
                                            rinv[p][:, :].unsqueeze(2).to_broadcast([ROWS, HC, CW]), ALU.mult).then_inc(osel_done, 1)
                if within(u, 1, B + 1):
                    dve.wait_ge(pT_ready, 2 * u - 1)
                    wait(dve, pv_ready, u - 1)
                    nc.vector.tensor_copy(probsT[:, 0, :, :].rearrange("p c s -> p (c s)"), t_bank[0][0:LH, 0:HC * ROWS]).then_inc(pT0_done, 1)
                if within(u, -2, B - 2):
                    wait(dve, gathered, u + 1)
                    nc.vector.tensor_tensor(pick[p2][:, :, :, :],
                                            c[0:LH, CONST["siota"]].rearrange("p (s h) -> p s h", h=H).unsqueeze(1).to_broadcast([LH, 2, KTOP, H]),
                                            key_all[:, :, bass.ds(u2, 1), :].to_broadcast([LH, 2, KTOP, H]),
                                            ALU.is_equal).then_inc(pick_done, 1)
                if within(u, 0, B):
                    dve.wait_ge(key_in[p], 32 * hf + 32)
                    wait(dve, scattered, u - 1)
                    nc.vector.tensor_scalar(put[p][:, :, :], keyb[p][:, :, :], c[0:ROWS, CONST["sidx"]], None,
                                            ALU.is_equal).then_inc(put_done, 1)
                if within(u, -1, B - 1):
                    dve.wait_ge(gathered, u + 2)
                    wait(dve, scores1, u)
                    nc.vector.tensor_tensor(qsel[p1][:, :, :], g_bank[:, 0:ROWS].unsqueeze(1).to_broadcast([128, 2, ROWS]),
                                            c[:, CONST["qmask"]].rearrange("p (c s) -> p c s", c=2), ALU.mult).then_inc(qsel_done, 1)
                if within(u, 1, B + 1):
                    dve.wait_ge(pv_ready, u)
                    wait(dve, o_ready, u - 1)
                    nc.vector.tensor_tensor(oT[:, :], o_bank[:, 0:ROWS], c[:, CONST["omask"]], ALU.mult).then_inc(oT_done, 1)

            steps(dve, slot, *RUN)

        @block.scalar
        def _(act):
            def slot(h, p):
                u, _, _ = shift(h, p, 0)
                _, _, p1 = shift(h, p, 1)
                um2, _, _ = shift(h, p, -2)
                if within(u, 0, B):
                    wait(act, rinv_done, u - 1)
                    wait(act, pT_ready, 2 * u - 2)
                    for ch in range(HC):
                        if ch % 2 == 0:
                            act.wait_ge(max_done, 2 * u + 1 + ch // 2)
                        nc.scalar.activation(probs[p][:, ch, :], s_bank[ch // 2][0:ROWS, L * (ch % 2):L * (ch % 2) + L], ACT.Exp,
                                             bias=negmax[p][:, ch:ch + 1], accum_out=rowsum[p][:, ch:ch + 1]).then_inc(exp_done, 1)
                if within(u, 1, B + 1):
                    act.wait_ge(pT_ready, 2 * u)
                    wait(act, pv_ready, u - 1)
                    nc.scalar.activation(probsT[:, 1, :, :].rearrange("p c s -> p (c s)"), t_bank[1][0:LH, 0:HC * ROWS], ACT.Copy).then_inc(pT1_done, 1)
                if within(u, -1, B):
                    act.wait_ge(kv_ready, u + 2)
                if within(u, -1, B - 1):
                    wait(act, scores1, u)
                    nc.scalar.activation(kT[p1][:, :], kv_bank[:, 0:L], ACT.Identity,
                                         bias=cols[:, COLS.index("k_b"):COLS.index("k_b") + 1]).then_inc(kT_done, 1)
                if within(u, 0, B):
                    wait(act, pv_ready, u - 1)
                    nc.scalar.activation(v1[p][:, :, :].rearrange("p a b -> p (a b)"), kv_bank[0:LH, 256:512], ACT.Copy).then_inc(v_done, 1)
                if within(u, 2, B + 2):
                    act.wait_ge(scattered, u - 1)
                    nc.scalar.activation(attn_all[:, bass.ds(um2 * L, L)], a_bank[:, 0:L], ACT.Identity,
                                         bias=meanv[:, bass.ds(um2, 1)]).then_inc(attn_done, 1)

            steps(act, slot, *RUN)


def ffn_conv(S):
    nc, w, c, cols, rows, banks = (S[k] for k in ("nc", "w", "c", "cols", "rows", "banks"))
    attn_all, n3T_all, z_all = (S[k] for k in ("attn_all", "n3T_all", "z_all"))
    with ExitStack() as ctx:
        def sb(name, shape, dt=F32):
            return ctx.enter_context(nc.sbuf_tensor(name, shape, dt))

        def sem(name):
            return ctx.enter_context(nc.semaphore(name))

        def pair(name, shape, dt=F32):
            return [sb(f"{name}{p}", shape, dt) for p in range(2)]

        attn = pair("attn_", [128, 2 * L])
        xt = pair("xt_", [LH, 4, D])
        ao = pair("ao_", [LH, 4, D])
        aob = pair("aob_", [LH, 4, D])
        t1 = sb("t1", [LH, 4, D])
        n1 = sb("n1", [LH, 4, D])
        hb = pair("hb_", [LH, 4, D])
        h1T = pair("h1T_", [128, 2 * L])
        hid = sb("hid", [128, 4, 2 * L])
        t2 = sb("t2", [LH, 4, D])
        n2 = sb("n2", [LH, 4, D])
        fused = sb("fused", [LH, 4, D])
        yin = sb("yin", [128, 2, L + 2])
        ymax = sb("ymax", [128, 2 * LH])
        h0T = sb("h0T", [128, 2 * LH])
        h0 = sb("h0", [LH, 2, D])
        n3 = sb("n3", [LH, 2, D])
        gate = sb("gate", [1, 1])
        biases = sb("biases", [LH, D])
        st = [sb(f"st{i}", [LH, n, 6]) for i, n in enumerate((4, 4, 2))]
        mv = [sb(f"mv{i}", [LH, n, 2]) for i, n in enumerate((4, 4, 2))]
        sd = [sb(f"sd{i}", [LH, n]) for i, n in enumerate((4, 4, 2))]
        rstd = [sb(f"rstd{i}", [LH, n]) for i, n in enumerate((4, 4, 2))]

        at_in = [sem(f"f_attn_in{p}") for p in range(2)]
        x_in = [sem(f"f_x_in{p}") for p in range(2)]
        ready = sem("f_ready")
        ao_ready, ao_done, t1_done, aob_done = sem("f_ao_ready"), sem("f_ao_done"), sem("f_t1_done"), sem("f_aob_done")
        bn, aggr, sd_done, rs_done, norm = ([sem(f"f_{k}{i}") for i in range(3)] for k in ("bn", "aggr", "sd", "rstd", "norm"))
        n1T_ready, h1T_done, hb_mul, hb_done = sem("f_n1T_ready"), sem("f_h1T_done"), sem("f_hb_mul"), sem("f_hb_done")
        f1_ready, hid_done, f2_ready, t2_done = sem("f_f1_ready"), sem("f_hid_done"), sem("f_f2_ready"), sem("f_t2_done")
        fu_mul, fused_done, fT_ready, yin_done = sem("f_fu_mul"), sem("f_fused_done"), sem("f_fT_ready"), sem("f_yin_done")
        conv_ready, max_done, h0T_done, h0_ready = sem("f_conv_ready"), sem("f_max_done"), sem("f_h0T_done"), sem("f_h0_ready")
        h0_done, h0b_done, n3T_ready, n3T_done = sem("f_h0_done"), sem("f_h0b_done"), sem("f_n3T_ready"), sem("f_n3T_done")

        f_bank, ao_bank, f2_bank, n1_bank, fu_bank, cv_bank, h_bank = banks[0:2], banks[2], banks[3], banks[4], banks[5], banks[6], banks[7]
        ident = c[:, CONST["ident"]]
        NP = NPAIR
        RUN = (-1, 4, NP - 3, NP + 1)

        def row(name, n):
            i = RWS.index(name)
            return rows[0:LH, i:i + 1, :].to_broadcast([LH, n, D])

        def col(name):
            i = COLS.index(name)
            return cols[:, i:i + 1]

        def tok(bank, n=4):
            return bank[0:LH, 0:n * D].rearrange("p (a b) -> p a b", b=D)

        block = ctx.enter_context(nc.Block())

        @block.sync
        def _(sp):
            def slot(h, p):
                t, _, _ = shift(h, p, 0)
                wait(sp, ao_ready, t - 1)
                sp.dma_start(attn[p][:, :], attn_all[:, bass.ds(t * 2 * L, 2 * L)]).then_inc(at_in[p], 16)
                wait(sp, t1_done, t - 1)
                sp.dma_start(xt[p][:, :, :], S["xtok"][:, bass.ds(t * 4, 4), :]).then_inc(x_in[p], 16)

            steps(sp, slot, 0, 2, NP - 1, NP - 1)

        @block.tensor
        def _(pe):
            def slot(h, p):
                t, _, _ = shift(h, p, 0)
                _, hn, pn = shift(h, p, 1)
                if within(t, 0, NP):
                    pe.wait_ge(h1T_done, t + 1)
                    for k in range(4):
                        wait(pe, hid_done, 4 * t + k - 1)
                        nc.tensor.matmul(f_bank[k % 2][:, 0:2 * L], w[:, WEIGHT["f1"].start + 128 * k:WEIGHT["f1"].start + 128 * k + 128],
                                         h1T[p][:, :], start=True, stop=True).then_inc(f1_ready, 1)
                if within(t, -1, NP - 1):
                    pe.wait_ge(at_in[pn], 16 * hn + 16)
                    wait(pe, ao_done, t + 1)
                    for j in range(4):
                        ins = nc.tensor.matmul(ao_bank[0:LH, D * j:D * j + D], attn[pn][:, LH * j:LH * j + LH], w[:, WEIGHT["o"]],
                                               start=True, stop=True)
                    ins.then_inc(ao_ready, 1)
                if within(t, 2, NP + 2):
                    pe.wait_ge(h0T_done, t - 1)
                    wait(pe, n3T_done, t - 2)
                    for b in range(2):
                        ins = nc.tensor.transpose(h_bank[0:LH, D * b:D * b + D], h0T[:, LH * b:LH * b + LH], ident)
                    ins.then_inc(h0_ready, 1)
                if within(t, 1, NP + 1):
                    pe.wait_ge(fused_done, t)
                    wait(pe, yin_done, t - 1)
                    for j in range(4):
                        ins = nc.tensor.transpose(fu_bank[:, LH * j:LH * j + LH], fused[:, j, :], ident[0:LH, 0:LH])
                    ins.then_inc(fT_ready, 1)
                if within(t, 0, NP):
                    wait(pe, t2_done, t)
                    for j in range(4):
                        for k in range(4):
                            if j == 0:
                                pe.wait_ge(hid_done, 4 * t + k + 1)
                            ins = nc.tensor.matmul(f2_bank[0:LH, D * j:D * j + D], hid[:, k, LH * j:LH * j + LH],
                                                   w[:, WEIGHT["f2"].start + D * k:WEIGHT["f2"].start + D * k + D],
                                                   start=k == 0, stop=k == 3)
                    ins.then_inc(f2_ready, 1)
                if within(t, 2, NP + 2):
                    pe.wait_ge(norm[2], t - 1)
                    for b in range(2):
                        ins = nc.tensor.transpose(h_bank[:, 256 + LH * b:256 + LH * b + LH], n3[:, b, :], ident[0:LH, 0:LH])
                    ins.then_inc(n3T_ready, 1)
                if within(t, -1, NP - 1):
                    pe.wait_ge(norm[0], t + 2)
                    wait(pe, h1T_done, t + 1)
                    for j in range(4):
                        ins = nc.tensor.transpose(n1_bank[:, LH * j:LH * j + LH], n1[:, j, :], ident[0:LH, 0:LH])
                    ins.then_inc(n1T_ready, 1)
                if within(t, 1, NP + 1):
                    pe.wait_ge(yin_done, t)
                    wait(pe, max_done, t - 1)
                    for k in range(3):
                        ins = nc.tensor.matmul(cv_bank[:, 0:2 * L].rearrange("p (b l) -> p b l", b=2),
                                               w[:, WEIGHT["conv"].start + D * k:WEIGHT["conv"].start + D * k + D],
                                               yin[:, :, k:k + L], start=k == 0, stop=k == 2)
                    ins.then_inc(conv_ready, 1)

            steps(pe, slot, *RUN)

        @block.scalar
        def _(act):
            def root(i, count):
                act.wait_ge(aggr[i], count)
                wait(act, rs_done[i], count - 1)
                nc.scalar.activation(sd[i][:, :].unsqueeze(2), mv[i][:, :, 1:2], ACT.Sqrt, bias=c[0:LH, CONST["eps"]]).then_inc(sd_done[i], 1)

            def slot(h, p):
                t, _, _ = shift(h, p, 0)
                tm2, _, _ = shift(h, p, -2)
                _, _, pn = shift(h, p, 1)
                if within(t, 1, NP + 1):
                    root(1, t)
                if within(t, 2, NP + 2):
                    act.wait_ge(max_done, t - 1)
                    wait(act, h0_ready, t - 2)
                    nc.scalar.activation(h0T[:, :], ymax[:, :], ACT.Relu, bias=col("conv_b")).then_inc(h0T_done, 1)
                if within(t, 0, NP):
                    wait(act, f2_ready, t)
                    for k in range(4):
                        act.wait_ge(f1_ready, 4 * t + k + 1)
                        nc.scalar.activation(hid[:, k, :], f_bank[k % 2][:, 0:2 * L], ACT.Relu, bias=col(f"f1_{k}")).then_inc(hid_done, 1)
                if within(t, 1, NP + 1):
                    act.wait_ge(fT_ready, t)
                    if isinstance(t, int) and t == 1:
                        act.wait_ge(ready, 1)
                    wait(act, conv_ready, t - 1)
                    nc.scalar.activation(yin[:, :, 1:L + 1], fu_bank[:, 0:2 * L].rearrange("p (b l) -> p b l", b=2), ACT.Copy).then_inc(yin_done, 1)
                if within(t, 2, NP + 2):
                    root(2, t - 1)
                if within(t, -1, NP - 1):
                    root(0, t + 2)
                if within(t, 2, NP + 2):
                    act.wait_ge(n3T_ready, t - 1)
                    nc.scalar.activation(n3T_all[:, bass.ds(tm2 * 2 * LH, 2 * LH)], h_bank[:, 256:256 + 2 * LH], ACT.Copy).then_inc(n3T_done, 1)
                if within(t, -1, NP - 1):
                    act.wait_ge(n1T_ready, t + 2)
                    wait(act, f1_ready, 4 * t)
                    nc.scalar.activation(h1T[pn][:, :], n1_bank[:, 0:2 * L], ACT.Identity, scale=col("ln1_g"), bias=col("ln1_b")).then_inc(h1T_done, 1)

            steps(act, slot, *RUN)

        @block.vector
        def _(dve):
            nc.vector.memset(yin[:, :, 0:1], 0.0)
            nc.vector.memset(yin[:, :, L + 1:L + 2], 0.0).then_inc(ready, 1)

            def stats(i, src, n, count):
                wait(dve, sd_done[i], count - 1)
                wait(dve, norm[i], count - 1)
                for j in range(n):
                    ins = nc.vector.bn_stats(st[i][:, j, :], src[:, j, :])
                ins.then_inc(bn[i], 1)
                dve.wait_ge(bn[i], count)
                nc.vector.memset(gate[:, :], 0.0)
                for j in range(n):
                    ins = nc.vector.bn_aggr(mv[i][:, j, :], st[i][:, j, :])
                ins.then_inc(aggr[i], 1)

            def normalise(i, dst, src, n, count):
                dve.wait_ge(sd_done[i], count)
                nc.vector.reciprocal(rstd[i][:, :], sd[i][:, :]).then_inc(rs_done[i], 1)
                dve.wait_ge(rs_done[i], count)
                for j in range(n):
                    ins = nc.vector.tensor_scalar(dst[:, j, :], src[:, j, :], mv[i][:, j, 0:1], rstd[i][:, j:j + 1],
                                                  ALU.subtract, ALU.mult)
                ins.then_inc(norm[i], 1)

            def slot(h, p):
                t, _, _ = shift(h, p, 0)
                _, hn, pn = shift(h, p, 1)
                if within(t, 2, NP + 2):
                    dve.wait_ge(conv_ready, t - 1)
                    wait(dve, h0T_done, t - 2)
                    nc.vector.tensor_reduce(ymax[:, :], cv_bank[:, 0:2 * L].rearrange("p (l two) -> p l two", two=2), AX, ALU.max).then_inc(max_done, 1)
                if within(t, 1, NP + 1):
                    wait(dve, fused_done, t - 1)
                    normalise(1, n2, t2, 4, t)
                if within(t, -1, NP - 1):
                    dve.wait_ge(ao_ready, t + 2)
                    wait(dve, aob_done, t)
                    nc.vector.tensor_tensor(ao[pn][:, :, :], tok(ao_bank), row("o_b", 4), ALU.add).then_inc(ao_done, 1)
                if within(t, 2, NP + 2):
                    dve.wait_ge(h0_ready, t - 1)
                    wait(dve, h0b_done, t - 2)
                    wait(dve, norm[2], t - 2)
                    nc.vector.tensor_copy(h0[:, :, :], tok(h_bank, 2)).then_inc(h0_done, 1)
                    dve.wait_ge(h0_done, t - 1)
                    stats(2, h0, 2, t - 1)
                if within(t, -1, NP - 1):
                    dve.wait_ge(t1_done, t + 2)
                    stats(0, t1, 4, t + 2)
                if within(t, 2, NP + 2):
                    wait(dve, n3T_ready, t - 2)
                    normalise(2, n3, h0, 2, t - 1)
                if within(t, -1, NP - 1):
                    wait(dve, n1T_ready, t + 1)
                    wait(dve, hb_mul, t + 1)
                    normalise(0, n1, t1, 4, t + 2)
                if within(t, 0, NP):
                    dve.wait_ge(f2_ready, t + 1)
                    dve.wait_ge(hb_done, t + 1)
                    wait(dve, norm[1], t)
                    nc.vector.tensor_tensor(t2[:, :, :], tok(f2_bank), hb[p][:, :, :], ALU.add).then_inc(t2_done, 1)
                    dve.wait_ge(t2_done, t + 1)
                    stats(1, t2, 4, t + 1)

            steps(dve, slot, *RUN)

        @block.gpsimd
        def _(pool):
            nc.gpsimd.tensor_tensor(biases[:, :], rows[0:LH, RWS.index("ln1_b"), :], rows[0:LH, RWS.index("f2_b"), :], ALU.add).then_inc(hb_mul, 1)

            def slot(h, p):
                t, _, _ = shift(h, p, 0)
                tm2, _, _ = shift(h, p, -2)
                _, hn, pn = shift(h, p, 1)
                pm = pn
                if within(t, 1, NP + 1):
                    pool.wait_ge(norm[1], t)
                    wait(pool, fT_ready, t - 1)
                    nc.gpsimd.tensor_tensor(fused[:, :, :], n2[:, :, :], row("ln2_g", 4), ALU.mult).then_inc(fu_mul, 1)
                    pool.wait_ge(fu_mul, t)
                    pool.wait_ge(aob_done, t)
                    nc.gpsimd.tensor_tensor(fused[:, :, :], fused[:, :, :], aob[pm][:, :, :], ALU.add).then_inc(fused_done, 1)
                if within(t, -1, NP - 1):
                    pool.wait_ge(ao_done, t + 2)
                    pool.wait_ge(x_in[pn], 16 * hn + 16)
                    wait(pool, norm[0], t + 1)
                    nc.gpsimd.tensor_tensor(t1[:, :, :], ao[pn][:, :, :], xt[pn][:, :, :], ALU.add).then_inc(t1_done, 1)
                    wait(pool, fused_done, t)
                    nc.gpsimd.tensor_tensor(aob[pn][:, :, :], ao[pn][:, :, :], row("ln2_b", 4), ALU.add).then_inc(aob_done, 1)
                if within(t, 2, NP + 2):
                    pool.wait_ge(h0_done, t - 1)
                    nc.gpsimd.tensor_tensor(z_all[:, bass.ds(tm2 * 2, 2), :], h0[:, :, :], row("wp_b", 2), ALU.add).then_inc(h0b_done, 1)
                if within(t, -1, NP - 1):
                    pool.wait_ge(norm[0], t + 2)
                    wait(pool, t2_done, t)
                    nc.gpsimd.tensor_tensor(hb[pn][:, :, :], n1[:, :, :], row("ln1_g", 4), ALU.mult).then_inc(hb_mul, 1)
                    pool.wait_ge(hb_mul, t + 3)
                    nc.gpsimd.tensor_tensor(hb[pn][:, :, :], hb[pn][:, :, :], biases[:, :].unsqueeze(1).to_broadcast([LH, 4, D]), ALU.add).then_inc(hb_done, 1)

            steps(pool, slot, *RUN)


def window_attention(S):
    nc, w, c, cols, rows, banks = (S[k] for k in ("nc", "w", "c", "cols", "rows", "banks"))
    n3T_all, z_all = S["n3T_all"], S["z_all"]
    with ExitStack() as ctx:
        def sb(name, shape, dt=F32):
            return ctx.enter_context(nc.sbuf_tensor(name, shape, dt))

        def sem(name):
            return ctx.enter_context(nc.semaphore(name))

        def pair(name, shape, dt=F32):
            return [sb(f"{name}{p}", shape, dt) for p in range(2)]

        n3 = pair("n3T_", [128, LH])
        qT = pair("wqT_", [128, LH])
        kT = sb("wkT", [128, LH])
        kbd = pair("kbd_", [128, 4, LH])
        v = pair("wv_", [LH, D])
        negmax = pair("wmax_", [LH, H])
        probs = pair("wprobs_", [LH, H, LH])
        probsT = sb("wprobsT", [LH, H, LH])
        rinv = sb("wrinv", [128, 2 * LH])
        o2 = sb("o2", [128, 2, LH])
        wp = sb("wp2", [128, 2, D])
        ident16 = sb("ident16", [128, LH], BF16)
        band16 = sb("band16", [128, 4 * LH], BF16)
        st = sb("st_all", [LH, B, 6])
        mean = sb("mean_z", [LH, B])
        var = sb("var_z", [LH, B])
        tmp = sb("tmp_z", [LH, B])
        sdz = sb("sd_z", [LH, B])
        rs = sb("rstd_z", [LH, B])
        gain = sb("gain_z", [LH, B])
        offs = sb("offs_z", [LH, B])
        o = sb("o_all", [LH, B, D])

        n_in = [sem(f"w_n_in{p}") for p in range(2)]
        ready, kT_done, qT_done, kbd_done, v_done = sem("w_ready"), sem("w_kT_done"), sem("w_qT_done"), sem("w_kbd_done"), sem("w_v_done")
        qkv_ready, scores, max_done, exp_done = sem("w_qkv_ready"), sem("w_scores"), sem("w_max_done"), sem("w_exp_done")
        pT_ready, pT0_done, pT1_done = sem("w_pT_ready"), sem("w_pT0_done"), sem("w_pT1_done")
        pv_ready, rinv_done, o_done, proj_ready, z_done = sem("w_pv_ready"), sem("w_rinv_done"), sem("w_o_done"), sem("w_proj_ready"), sem("w_z_done")
        stat, chain, root_done, out_done, stored = sem("w_stat"), sem("w_chain"), sem("w_root_done"), [sem(f"w_out{i}") for i in range(2)], sem("w_stored")

        s_bank, t_bank, q_bank, o_bank, p_bank = banks[0:2], banks[2:4], banks[4], banks[5], banks[6]
        ident = c[:, CONST["ident"]]
        RUN = (-1, 4, B - 3, B + 1)

        def col(name):
            i = COLS.index(name)
            return cols[:, i:i + 1]

        block = ctx.enter_context(nc.Block())

        @block.sync
        def _(sp):
            def slot(h, p):
                u, _, _ = shift(h, p, 0)
                wait(sp, qkv_ready, u)
                sp.dma_start(n3[p][:, :], n3T_all[:, bass.ds(u * LH, LH)]).then_inc(n_in[p], 16)

            steps(sp, slot, 0, 4, B - 1, B - 1)
            for g in range(4):
                sp.wait_ge(out_done[0], 4 * g + 4)
                sp.wait_ge(out_done[1], 4 * g + 4)
                sp.dma_start(S["out"].rearrange("b l d -> l b d")[:, 8 * g:8 * g + 8, :], o[:, 8 * g:8 * g + 8, :]).then_inc(stored, 16)
            sp.wait_ge(stored, 64)

        @block.tensor
        def _(pe):
            pe.wait_ge(ready, 4)

            def slot(h, p):
                u, _, _ = shift(h, p, 0)
                _, hn, pn = shift(h, p, 1)
                _, _, pm = shift(h, p, -1)
                if within(u, 1, B + 1):
                    wait(pe, pT0_done, u - 1)
                    wait(pe, pT1_done, u - 1)
                    for r in range(2):
                        pe.wait_ge(exp_done, 2 * u - 1 + r)
                        for j in range(4):
                            ins = nc.tensor.transpose(t_bank[r][0:LH, LH * j:LH * j + LH], probs[pm][:, 4 * r + j, :], ident[0:LH, 0:LH])
                        ins.then_inc(pT_ready, 1)
                if within(u, -1, B):
                    wait(pe, kT_done, u + 1)
                    wait(pe, v_done, u)
                    if within(u, -1, B - 1):
                        pe.wait_ge(n_in[pn], 16 * hn + 16)
                        for i, name in enumerate(("wq", "wk")):
                            ins = nc.tensor.matmul(q_bank[:, 128 * i:128 * i + LH], w[:, WEIGHT[name]], n3[pn][:, :], start=True, stop=True)
                    if within(u, 0, B):
                        ins = nc.tensor.matmul(q_bank[0:LH, 256:256 + D], n3[p][:, :], w[:, WEIGHT["wv"]], start=True, stop=True)
                    ins.then_inc(qkv_ready, 1)
                if within(u, 0, B):
                    pe.wait_ge(qT_done, u + 1)
                    pe.wait_ge(kbd_done, u + 1)
                    wait(pe, exp_done, 2 * u)
                    for r in range(2):
                        nc.tensor.matmul(s_bank[r][0:LH, 0:4 * LH], qT[p][64 * r:64 * r + 64, :],
                                         kbd[p][64 * r:64 * r + 64, :, :].rearrange("p h l -> p (h l)"), start=True, stop=False)
                        nc.tensor.matmul(s_bank[r][0:LH, 0:4 * LH], ident16[0:LH, :], band16[0:LH, :], start=False, stop=True).then_inc(scores, 1)
                if within(u, 2, B + 2):
                    pe.wait_ge(o_done, u - 1)
                    wait(pe, z_done, u - 2)
                    for hh in range(2):
                        ins = nc.tensor.matmul(p_bank[0:LH, 0:D], o2[:, hh, :], wp[:, hh, :], start=hh == 0, stop=hh == 1)
                    ins.then_inc(proj_ready, 1)
                if within(u, 1, B + 1):
                    pe.wait_ge(pT0_done, u)
                    pe.wait_ge(pT1_done, u)
                    pe.wait_ge(v_done, u)
                    wait(pe, o_done, u - 1)
                    for src, at in ((None, 0), (c[0:LH, CONST["ones"]], 2 * LH)):
                        for ch in range(HC):
                            ins = nc.tensor.matmul(o_bank[CW * ch:CW * ch + CW, at:at + 2 * LH],
                                                   v[pm][:, CW * ch:CW * ch + CW] if src is None else src,
                                                   probsT[:, 2 * ch:2 * ch + 2, :].rearrange("p h l -> p (h l)"), start=True, stop=True)
                    ins.then_inc(pv_ready, 1)

            steps(pe, slot, *RUN)

        @block.scalar
        def _(act):
            def slot(h, p):
                u, _, _ = shift(h, p, 0)
                _, _, pn = shift(h, p, 1)
                if within(u, 1, B + 1):
                    act.wait_ge(pT_ready, 2 * u)
                    wait(act, pv_ready, u - 1)
                    nc.scalar.activation(probsT[:, 4:8, :].rearrange("p h l -> p (h l)"), t_bank[1][0:LH, 0:4 * LH], ACT.Copy).then_inc(pT1_done, 1)
                if within(u, -1, B - 1):
                    act.wait_ge(qkv_ready, u + 2)
                    wait(act, scores, 2 * u)
                    wait(act, kbd_done, u + 1)
                    nc.scalar.activation(qT[pn][:, :], q_bank[:, 0:LH], ACT.Identity, bias=col("wq_b")).then_inc(qT_done, 1)
                    nc.scalar.activation(kT[:, :], q_bank[:, 128:128 + LH], ACT.Identity, bias=col("wk_b")).then_inc(kT_done, 1)
                if within(u, 0, B):
                    wait(act, pT_ready, 2 * u - 2)
                    for r in range(2):
                        act.wait_ge(max_done, 2 * u + r + 1)
                        for j in range(4):
                            ins = nc.scalar.activation(probs[p][:, 4 * r + j, :], s_bank[r][0:LH, LH * j:LH * j + LH], ACT.Exp,
                                                       bias=negmax[p][:, 4 * r + j:4 * r + j + 1])
                        ins.then_inc(exp_done, 1)

            steps(act, slot, *RUN)
            act.wait_ge(chain, 6)
            nc.scalar.activation(sdz[:, :], var[:, :], ACT.Sqrt, bias=c[0:LH, CONST["eps"]]).then_inc(root_done, 1)
            act.wait_ge(chain, 9)
            for b in range(1, B, 2):
                nc.scalar.activation(o[:, b, :], z_all[:, b, :], ACT.Identity, scale=gain[:, b:b + 1], bias=offs[:, b:b + 1]).then_inc(out_done[1], 1)

        @block.gpsimd
        def _(pool):
            def slot(h, p):
                u, _, _ = shift(h, p, 0)
                pool.wait_ge(kT_done, u + 1)
                wait(pool, scores, 2 * u - 2)
                nc.gpsimd.tensor_tensor(kbd[p][:, :, :], kT[:, :].unsqueeze(1).to_broadcast([128, 4, LH]),
                                        c[:, CONST["kmask"]].unsqueeze(2).to_broadcast([128, 4, LH]), ALU.mult).then_inc(kbd_done, 1)

            steps(pool, slot, 0, 4, B - 1, B - 1)

        @block.vector
        def _(dve):
            nc.vector.tensor_copy(ident16[:, :], ident[:, 0:LH]).then_inc(ready, 1)
            nc.vector.tensor_copy(band16[:, :], c[:, CONST["band"]]).then_inc(ready, 1)
            for hh in range(2):
                nc.vector.tensor_scalar(wp[:, hh, :], w[:, WEIGHT["wp"]], c[:, CONST["parity"].start + hh:CONST["parity"].start + hh + 1],
                                        None, ALU.mult).then_inc(ready, 1)

            def slot(h, p):
                u, _, _ = shift(h, p, 0)
                um2, _, _ = shift(h, p, -2)
                if within(u, 1, B + 1):
                    dve.wait_ge(pT_ready, 2 * u - 1)
                    wait(dve, pv_ready, u - 1)
                    nc.vector.tensor_copy(probsT[:, 0:4, :].rearrange("p h l -> p (h l)"), t_bank[0][0:LH, 0:4 * LH]).then_inc(pT0_done, 1)
                if within(u, 0, B):
                    dve.wait_ge(qkv_ready, u + 2)
                    wait(dve, kT_done, min(u + 2, B) if isinstance(u, int) else u + 2)
                    wait(dve, pv_ready, u - 1)
                    nc.vector.tensor_tensor(v[p][:, :], q_bank[0:LH, 256:256 + D], rows[0:LH, RWS.index("wv_b"), :], ALU.add).then_inc(v_done, 1)
                    for r in range(2):
                        dve.wait_ge(scores, 2 * u + r + 1)
                        nc.vector.tensor_reduce(negmax[p][:, 4 * r:4 * r + 4], s_bank[r][0:LH, 0:4 * LH].rearrange("p (h l) -> p h l", h=4),
                                                AX, ALU.max, negate=True).then_inc(max_done, 1)
                if within(u, 2, B + 2):
                    dve.wait_ge(proj_ready, u - 1)
                    nc.vector.tensor_tensor(z_all[:, bass.ds(um2, 1), :], p_bank[0:LH, 0:D].unsqueeze(1), z_all[:, bass.ds(um2, 1), :], ALU.add).then_inc(z_done, 1)
                    dve.wait_ge(z_done, u - 1)
                    nc.vector.bn_stats(st[:, bass.ds(um2, 1), :].rearrange("p a b -> p (a b)"), z_all[:, bass.ds(um2, 1), :].rearrange("p a b -> p (a b)")).then_inc(stat, 1)
                if within(u, 1, B + 1):
                    dve.wait_ge(pv_ready, u)
                    nc.vector.reciprocal(rinv[:, :], o_bank[:, 2 * LH:4 * LH]).then_inc(rinv_done, 1)
                    dve.wait_ge(rinv_done, u)
                    wait(dve, proj_ready, u - 1)
                    nc.vector.tensor_tensor(o2[:, :, :].rearrange("p h l -> p (h l)"), o_bank[:, 0:2 * LH], rinv[:, :], ALU.mult).then_inc(o_done, 1)

            steps(dve, slot, *RUN)

            dve.wait_ge(stat, B)
            m0, m1, q0, q1 = (st[:, :, i] for i in (1, 4, 2, 5))
            nc.vector.tensor_tensor(mean[:, :], m0, m1, ALU.add).then_inc(chain, 1)
            nc.vector.tensor_tensor(tmp[:, :], m0, m1, ALU.subtract).then_inc(chain, 1)
            nc.vector.tensor_tensor(var[:, :], q0, q1, ALU.add).then_inc(chain, 1)
            dve.wait_ge(chain, 3)
            nc.vector.tensor_tensor(tmp[:, :], tmp[:, :], tmp[:, :], ALU.mult).then_inc(chain, 1)
            dve.wait_ge(chain, 4)
            nc.vector.scalar_tensor_tensor(var[:, :], var[:, :], 4.0 / D, tmp[:, :], ALU.mult, ALU.add).then_inc(chain, 1)
            dve.wait_ge(chain, 5)
            nc.vector.tensor_scalar_mul(var[:, :], var[:, :], 0.25).then_inc(chain, 1)
            dve.wait_ge(root_done, 1)
            nc.vector.reciprocal(rs[:, :], sdz[:, :]).then_inc(chain, 1)
            dve.wait_ge(chain, 7)
            nc.vector.tensor_scalar(gain[:, :], rs[:, :], 1.0, None, ALU.add).then_inc(chain, 1)
            nc.vector.scalar_tensor_tensor(offs[:, :], mean[:, :], -0.5, rs[:, :], ALU.mult, ALU.mult).then_inc(chain, 1)
            dve.wait_ge(chain, 9)
            for b in range(0, B, 2):
                nc.vector.tensor_scalar(o[:, b, :], z_all[:, b, :], gain[:, b:b + 1], offs[:, b:b + 1], ALU.mult, ALU.add).then_inc(out_done[0], 1)


def kernel(**inputs):
    import numpy as _np
    import concourse.bacc as _bacc
    from concourse.bass_utils import run_bass_kernel_spmd as _run

    a = {k.removeprefix("L0_"): _np.asarray(v) for k, v in inputs.items()}
    x = a["x"]
    f1_b = a["tok_f1_b"].reshape(4, 128)
    bq, bk, bv = a["attn_b_qkv"].reshape(3, D)
    arrays = {
        "xT": _np.ascontiguousarray(x.transpose(2, 0, 1).reshape(D, B * L)),
        "xtok": _np.ascontiguousarray(x.reshape(B * 2, LH, D).transpose(1, 0, 2)),
        "weights": _np.ascontiguousarray(_np.concatenate([
            a["tok_q_w"], a["tok_k_w"], a["tok_v_w"], a["tok_o_w"], a["tok_f1_w"],
            a["tok_f2_w"].reshape(4, 128, D).transpose(1, 0, 2).reshape(128, F),
            a["tok_conv_w"].transpose(1, 2, 0).reshape(D, 3 * D), a["attn_W_qkv"], a["attn_W_proj"]], axis=1)),
        "consts": constants(),
        "cols": _np.ascontiguousarray(_np.stack([
            a["tok_k_b"], a["tok_v_b"], a["tok_ln1_g"], a["tok_ln1_b"], *f1_b, a["tok_conv_b"], bq, bk], axis=1)),
        "rows": _np.ascontiguousarray(_np.concatenate([
            a["tok_q_b"], a["tok_o_b"], a["tok_ln1_g"], a["tok_ln1_b"], a["tok_f2_b"], a["tok_ln2_g"], a["tok_ln2_b"],
            bv, a["attn_b_proj"]])),
    }
    nc = _bacc.Bacc("TRN2", target_bir_lowering=False, num_devices=1)
    args = [nc.dram_tensor(n, v.shape, mybir.dt.from_np(v.dtype), kind="ExternalInput").ap() for n, v in arrays.items()]
    key_dram = nc.dram_tensor("key_scratch", (B * H, L), BF16, kind="Internal").ap()
    out = nc.dram_tensor("out", (B, LH, D), F32, kind="ExternalOutput").ap()
    program(nc, *args, key_dram, out)
    return _run(nc, [arrays], core_ids=[0]).results[0]["out"]
```

```python
from contextlib import ExitStack

import numpy as np
import concourse.bass as bass
from concourse import mybir

F32 = mybir.dt.float32
BF16 = mybir.dt.bfloat16
ALU = mybir.AluOpType
ACT = mybir.ActivationFunctionType
AX = mybir.AxisListType.X

B, L, D, H, F = 32, 250, 128, 8, 512
HD = D // H
LH = L // 2
KTOP = L // 5
NPAIR = B // 2
HC = H // 2
CW = 2 * HD
ROWS = 2 * KTOP
HALF = 32
EPS = 1e-5
SCALE = HD ** -0.5
OFF = 3.0e38

CONST = {}
WEIGHT = {}


def _columns(table, *sizes):
    at = 0
    for name, n in sizes:
        table[name] = slice(at, at + n)
        at += n
    return at


NCONST = _columns(CONST, ("ident", 128), ("qmask", HC * ROWS), ("omask", ROWS), ("kmask", 4), ("sidx", 1),
                  ("siota", KTOP * H), ("band", LH), ("eps", 1))
NWEIGHT = _columns(WEIGHT, ("q", D), ("k", D), ("v", D), ("o", D), ("f1", F), ("f2", F), ("conv", 3 * D),
                   ("wq", D), ("wk", D), ("wv", D), ("wp", D))
COLS = ["k_b", "v_b", "ln1_g", "ln1_b", "f1_0", "f1_1", "f1_2", "f1_3", "conv_b", "wq_b", "wk_b", "wv_b"]
RWS = ["q_b", "o_b", "ln1_g", "ln1_b", "f2_b", "ln2_g", "ln2_b", "wp_b"]


def constants():
    c = np.zeros((128, NCONST), np.float32)
    p = np.arange(128)
    c[:, CONST["ident"]] = np.eye(128)
    j = np.arange(ROWS)
    own = (p[:, None] % CW) // HD == j[None, :] % 2
    qm = np.stack([own & (p[:, None] // CW == cc) for cc in range(HC)], 1)
    c[:, CONST["qmask"]] = (qm * SCALE).reshape(128, -1)
    c[:, CONST["omask"]] = own
    c[:, CONST["kmask"]] = ((p[:, None] % 64) // HD == np.arange(4)[None, :]) * -SCALE
    c[:, CONST["sidx"]] = (p // 2 + 1)[:, None]
    c[:, CONST["siota"]] = np.repeat(np.arange(1, KTOP + 1), H)[None, :]
    away = np.abs(p[:, None] - np.arange(LH)[None, :]) > HALF
    c[:, CONST["band"]] = np.where(away, OFF, 0.0)
    c[:, CONST["eps"]] = EPS
    return c


def wait(eng, sem, value):
    if isinstance(value, int) and value <= 0:
        return
    eng.wait_ge(sem, value)


def within(u, lo, hi):
    return not isinstance(u, int) or lo <= u < hi


UNROLL = 4


def steps(eng, slot, first, lo, hi, last):
    turns = (hi + 1 - lo) // UNROLL
    for u in range(first, lo):
        slot(u // 2, u % 2)
    if turns:
        with eng.Fori(0, turns) as i:
            for k in range(UNROLL):
                slot(i * (UNROLL // 2) + (lo + k) // 2, k % 2)
    for u in range(lo + UNROLL * turns, last + 1):
        slot(u // 2, u % 2)


def shift(h, p, k):
    h, p = h + (p + k) // 2, (p + k) % 2
    return 2 * h + p, h, p


def program(nc, xT, xtok, weights, consts, cols, rows, key_dram, out):
    with ExitStack() as ctx:
        def sb(name, shape, dt=F32):
            return ctx.enter_context(nc.sbuf_tensor(name, shape, dt))

        S = {
            "nc": nc, "xT": xT, "xtok": xtok, "key_dram": key_dram, "out": out,
            "weights_dram": weights, "consts_dram": consts, "cols_dram": cols, "rows_dram": rows,
            "w": sb("w", [128, NWEIGHT]), "c": sb("c", [128, NCONST]),
            "cols": sb("vec_cols", [128, len(COLS)]), "rows": sb("vec_rows", [128, len(RWS), D]),
            "banks": [ctx.enter_context(nc.psum_tensor(f"bank{i}", [128, 512], F32)) for i in range(8)],
            "meanv": sb("meanv", [128, B]),
        }
        S["attn_all"] = sb("attn_all", [128, B * L])
        with ExitStack() as early:
            for name, shape in (("q_all", [LH, B * 2 * D]), ("k_all", [128, B * L]), ("v_all", [LH, B * 2 * D]),
                                ("key_all", [LH, 2, B, H])):
                S[name] = early.enter_context(nc.sbuf_tensor(name, shape, F32))
            measure_and_select(S)
            topk_attention(S)
        S["n3T_all"] = sb("n3T_all", [128, B * LH])
        S["z_all"] = sb("z_all", [LH, B, D])
        ffn_conv(S)
        window_attention(S)


def measure_and_select(S):
    nc, w, c, cols, rows, banks = (S[k] for k in ("nc", "w", "c", "cols", "rows", "banks"))
    q_all, k_all, v_all, key_all, meanv = (S[k] for k in ("q_all", "k_all", "v_all", "key_all", "meanv"))
    W = L + 8
    NQ = B // 4
    with ExitStack() as ctx:
        def sb(name, shape, dt=F32):
            return ctx.enter_context(nc.sbuf_tensor(name, shape, dt))

        def sem(name):
            return ctx.enter_context(nc.semaphore(name))

        xa = [sb(f"xa{p}", [128, 4 * L]) for p in range(2)]
        x_all = S["attn_all"]
        xc = [sb(f"xc{p}", [128, 4 * L]) for p in range(2)]
        sq = [sb(f"sq{i}", [LH, 4 * D]) for i in range(2)]
        norm_all = sb("norm_all", [LH, 2, B, H])
        xsum = sb("xsum", [128, B])
        xneg = sb("xneg", [128, B])
        work = [[sb(f"work{g}{i}", [128, W]) for i in range(2)] for g in range(2)]
        top8 = [sb(f"top8_{g}", [128, 8]) for g in range(2)]
        chosen = [sb(f"chosen{g}", [128, L]) for g in range(2)]
        prefix = [sb(f"prefix{g}", [128, L]) for g in range(2)]
        zeros = sb("zeros", [128, L])
        key = [sb(f"key{g}", [128, L]) for g in range(2)]
        key16 = [sb(f"key16_{g}", [128, L], BF16) for g in range(2)]

        params_in = [sem(f"m_params{i}") for i in range(5)]
        x_in = [sem(f"m_x_in{p}") for p in range(2)]
        x_kept = sem("m_x_kept")
        q_ready, q_done, xsum_done, xneg_done, xc_done = sem("m_q_ready"), sem("m_q_done"), sem("m_xsum_done"), sem("m_xneg_done"), sem("m_xc_done")
        k_ready, k_done, v_ready, v_done = sem("m_k_ready"), sem("m_k_done"), sem("m_v_ready"), sem("m_v_done")
        sq_done, norm_done = sem("m_sq_done"), sem("m_norm_done")
        mean_ready, norm_t_ready, key_t_ready = sem("m_mean_ready"), sem("m_norm_t_ready"), sem("m_key_t_ready")
        setup, select, key_stored, key_ready, key_t_done = sem("m_setup"), sem("m_select"), sem("m_key_stored"), sem("m_key_ready"), sem("m_key_t_done")
        ident = c[:, CONST["ident"]]
        q_bank, k_bank, v_bank, n_bank = banks[0:2], banks[2:4], banks[4:6], banks[6:8]
        block = ctx.enter_context(nc.Block())

        @block.sync
        def _(sp):
            def slot(h, p):
                t, _, _ = shift(h, p, 0)
                wait(sp, k_ready, 2 * t - 2)
                wait(sp, xsum_done, t - 1)
                wait(sp, x_kept, t - 1)
                sp.dma_start(xa[p][:, :], S["xT"][:, bass.ds(t * 4 * L, 4 * L)]).then_inc(x_in[p], 16)

            steps(sp, slot, 0, 4, NQ - 1, NQ - 1)
            sp.dma_start(rows[:, 1:, :].rearrange("p a b -> p (a b)"),
                         S["rows_dram"][D:].partition_broadcast(128)).then_inc(params_in[1], 16)
            sp.dma_start(w[:, 3 * D:], S["weights_dram"][:, 3 * D:]).then_inc(params_in[4], 16)
            for g in range(2):
                sp.wait_ge(key_ready, g + 1)
                sp.dma_start(S["key_dram"][128 * g:128 * g + 128, :], key16[g][:, :]).then_inc(key_stored, 16)
            sp.wait_ge(key_stored, 32)
            sp.wait_ge(params_in[1], 32)
            sp.wait_ge(params_in[4], 16)

        @block.scalar
        def _(act):
            act.dma_start(w[:, 0:3 * D], S["weights_dram"][:, 0:3 * D]).then_inc(params_in[0], 16)
            act.dma_start(rows[:, 0, :], S["rows_dram"][0:D].partition_broadcast(128)).then_inc(params_in[1], 16)
            act.dma_start(cols[:, :], S["cols_dram"]).then_inc(params_in[3], 16)
            act.dma_start(c[:, :], S["consts_dram"]).then_inc(params_in[2], 16)
            act.wait_ge(params_in[3], 16)

            def slot(h, p):
                t, half, _ = shift(h, p, 0)
                act.wait_ge(x_in[p], 16 * half + 16)
                nc.scalar.activation(x_all[:, bass.ds(t * 4 * L, 4 * L)], xa[p][:, :], ACT.Copy).then_inc(x_kept, 1)
                for i in range(2):
                    wait(act, q_done, 2 * t + i + 1)
                    wait(act, norm_done, 2 * t + i - 1)
                    nc.scalar.activation(sq[i][:, :], q_all[:, bass.ds(t * 8 * D + 4 * D * i, 4 * D)], ACT.Square).then_inc(sq_done, 1)
                for i in range(2):
                    act.wait_ge(k_ready, 2 * t + i + 1)
                    nc.scalar.activation(k_all[:, bass.ds(t * 4 * L + 2 * L * i, 2 * L)], k_bank[i][:, 0:2 * L], ACT.Identity,
                                         bias=cols[:, COLS.index("k_b"):COLS.index("k_b") + 1]).then_inc(k_done, 1)

            def slot_again(h, p):
                t, _, _ = shift(h, p, 0)
                for i in range(2):
                    act.wait_ge(v_ready, 2 * t + i + 1)
                    nc.scalar.activation(v_all[:, bass.ds(t * 8 * D + 4 * D * i, 4 * D)], v_bank[i][0:LH, :], ACT.Copy).then_inc(v_done, 1)

            steps(act, slot, 0, 4, NQ - 1, NQ - 1)
            steps(act, slot_again, 0, 4, NQ - 1, NQ - 1)

        @block.gpsimd
        def _(pool):
            def slot_again(h, p):
                t, _, _ = shift(h, p, 0)
                if isinstance(t, int) and t == 0:
                    pool.wait_ge(xneg_done, 1)
                    pool.wait_ge(x_kept, NQ)
                wait(pool, v_ready, 2 * t - 2)
                nc.gpsimd.tensor_tensor(xc[p][:, :].rearrange("p (b l) -> p b l", b=4), x_all[:, bass.ds(t * 4 * L, 4 * L)].rearrange("p (b l) -> p b l", b=4),
                                        xneg[:, bass.ds(t * 4, 4)].unsqueeze(2).to_broadcast([128, 4, L]), ALU.add).then_inc(xc_done, 1)

            steps(pool, slot_again, 0, 4, NQ - 1, NQ - 1)

        @block.tensor
        def _(pe):
            pe.wait_ge(params_in[0], 16)

            def slot(h, p):
                t, half, _ = shift(h, p, 0)
                pe.wait_ge(x_in[p], 16 * half + 16)
                for i in range(2):
                    wait(pe, q_done, 2 * t + i - 1)
                    for j in range(4):
                        last = nc.tensor.matmul(q_bank[i][0:LH, D * j:D * j + D], xa[p][:, 2 * L * i + LH * j:2 * L * i + LH * j + LH],
                                                w[:, WEIGHT["q"]], start=True, stop=True)
                    last.then_inc(q_ready, 1)
                for i in range(2):
                    wait(pe, k_done, 2 * t + i - 1)
                    nc.tensor.matmul(k_bank[i][:, 0:2 * L], w[:, WEIGHT["k"]], xa[p][:, 2 * L * i:2 * L * i + 2 * L],
                                     start=True, stop=True).then_inc(k_ready, 1)

            def slot_again(h, p):
                t, _, _ = shift(h, p, 0)
                pe.wait_ge(xc_done, t + 1)
                for i in range(2):
                    wait(pe, v_done, 2 * t + i - 1)
                    for j in range(4):
                        last = nc.tensor.matmul(v_bank[i][0:LH, D * j:D * j + D], xc[p][:, 2 * L * i + LH * j:2 * L * i + LH * j + LH],
                                                w[:, WEIGHT["v"]], start=True, stop=True)
                    last.then_inc(v_ready, 1)

            def norms_to_rows(g):
                pe.wait_ge(norm_done, 2 * NQ if g else NQ)
                for lt in range(2):
                    last = nc.tensor.transpose(n_bank[g][:, LH * lt:LH * lt + LH],
                                               norm_all[:, lt, 16 * g:16 * g + 16, :].rearrange("p b h -> p (b h)"),
                                               ident[0:LH, 0:LH])
                last.then_inc(norm_t_ready, 1)

            steps(pe, slot, 0, 4, NQ - 1, NQ - 1)
            pe.wait_ge(params_in[2], 16)
            for g in range(2):
                norms_to_rows(g)
            steps(pe, slot_again, 0, 4, NQ - 1, NQ - 1)
            pe.wait_ge(xsum_done, NQ)
            pe.wait_ge(q_done, 2 * NQ)
            nc.tensor.matmul(q_bank[0][:, 0:B], w[:, WEIGHT["v"]], xsum[:, :], start=True, stop=True).then_inc(mean_ready, 1)
            for g in range(2):
                pe.wait_ge(key_ready, g + 1)
                for lt in range(2):
                    last = nc.tensor.transpose(n_bank[g][0:LH, D * lt:D * lt + D], key[g][:, LH * lt:LH * lt + LH], ident)
                last.then_inc(key_t_ready, 1)

        @block.vector
        def _(dve):
            nc.vector.memset(zeros[:, :], 0.0).then_inc(setup, 1)
            for g in range(2):
                nc.vector.memset(work[g][0][:, L:W], -2.0).then_inc(setup, 1)
            dve.wait_ge(params_in[1], 16)

            def slot(h, p):
                t, half, _ = shift(h, p, 0)
                dve.wait_ge(x_in[p], 16 * half + 16)
                for i in range(2):
                    dve.wait_ge(q_ready, 2 * t + i + 1)
                    nc.vector.tensor_tensor(q_all[:, bass.ds(t * 8 * D + 4 * D * i, 4 * D)].rearrange("p (a b) -> p a b", b=D),
                                            q_bank[i][0:LH, :].rearrange("p (a b) -> p a b", b=D),
                                            rows[0:LH, RWS.index("q_b"):RWS.index("q_b") + 1, :].to_broadcast([LH, 4, D]),
                                            ALU.add).then_inc(q_done, 1)
                nc.vector.reduce_sum(xsum[:, bass.ds(t * 4, 4)], xa[p][:, :].rearrange("p (b l) -> p b l", b=4),
                                     axis=AX).then_inc(xsum_done, 1)
                for i in range(2):
                    wait(dve, sq_done, 2 * t + i + 1)
                    nc.vector.reduce_sum(norm_all[:, :, bass.ds(t * 4 + 2 * i, 2), :].rearrange("p l b h -> p b l h"),
                                         sq[i][:, :].rearrange("p (b l h d) -> p b l h d", b=2, l=2, h=H),
                                         axis=AX).then_inc(norm_done, 1)

            steps(dve, slot, 0, 4, NQ - 1, NQ - 1)
            dve.wait_ge(xsum_done, NQ)
            nc.vector.tensor_scalar_mul(xneg[:, :], xsum[:, :], -1.0 / L).then_inc(xneg_done, 1)
            n = [0]

            def link(ins):
                n[0] += 1
                ins.then_inc(select, 1)

            def joined():
                dve.wait_ge(select, n[0])

            dve.wait_ge(setup, 3)
            for g in range(2):
                dve.wait_ge(norm_t_ready, g + 1)
                link(nc.vector.tensor_copy(work[g][0][:, 0:L], n_bank[g][:, 0:L]))
            joined()
            rounds = (KTOP + 7) // 8

            for r in range(rounds):
                for g in range(2):
                    link(nc.vector.max(top8[g][:, :], work[g][r % 2][:, 0:L]))
                joined()
                if r == rounds - 1:
                    for g in range(2):
                        link(nc.vector.memset(top8[g][:, KTOP - 8 * r:8], -2.0))
                    joined()
                for g in range(2):
                    link(nc.vector.match_replace(work[g][(r + 1) % 2][:, :], top8[g][:, :], work[g][r % 2][:, :], -1.0))
                joined()
            for g in range(2):
                link(nc.vector.tensor_scalar(chosen[g][:, :], work[g][rounds % 2][:, 0:L], -1.0, None, ALU.is_equal))
            joined()
            for g in range(2):
                link(nc.vector.tensor_tensor_scan(prefix[g][:, :], chosen[g][:, :], zeros[:, :], 0.0, ALU.add, ALU.add))
            joined()
            for g in range(2):
                link(nc.vector.tensor_tensor(key[g][:, :], prefix[g][:, :], chosen[g][:, :], ALU.mult))
            joined()
            for g in range(2):
                nc.vector.tensor_copy(key16[g][:, :], key[g][:, :]).then_inc(key_ready, 1)
            dve.wait_ge(mean_ready, 1)
            dve.wait_ge(params_in[3], 16)
            nc.vector.tensor_scalar(meanv[:, :], q_bank[0][:, 0:B], 1.0 / L, cols[:, COLS.index("v_b"):COLS.index("v_b") + 1],
                                    ALU.mult, ALU.add)
            for g in range(2):
                dve.wait_ge(key_t_ready, g + 1)
                nc.vector.tensor_copy(key_all[:, :, 16 * g:16 * g + 16, :],
                                      n_bank[g][0:LH, 0:2 * D].rearrange("p (l b h) -> p l b h", l=2, h=H)).then_inc(key_t_done, 1)


def topk_attention(S):
    nc, c, banks = (S[k] for k in ("nc", "c", "banks"))
    q_all, k_all, v_all, key_all, meanv, attn_all = (S[k] for k in ("q_all", "k_all", "v_all", "key_all", "meanv", "attn_all"))
    with ExitStack() as ctx:
        def sb(name, shape, dt=F32):
            return ctx.enter_context(nc.sbuf_tensor(name, shape, dt))

        def sem(name):
            return ctx.enter_context(nc.semaphore(name))

        def pair(name, shape, dt=F32):
            return [sb(f"{name}{p}", shape, dt) for p in range(2)]

        q1 = pair("q1_", [LH, 2, D])
        k1 = pair("k1_", [128, L])
        v1 = pair("v1_", [LH, 2, D])
        keyb = pair("keyb_", [ROWS, HC, L], BF16)
        pick = pair("pick_", [LH, 2, KTOP, H])
        put = pair("put_", [ROWS, HC, L])
        qsel = pair("qsel_", [128, HC, ROWS])
        negmax = pair("negmax_", [ROWS, HC])
        rowsum = pair("rowsum_", [ROWS, HC])
        rinv = pair("rinv_", [ROWS, HC])
        probs = pair("probs_", [ROWS, HC, L])
        probsT = sb("probsT", [LH, 2, HC, ROWS])
        oT = sb("oT", [128, ROWS])
        gate = sb("gate_pool", [1, 1])
        osel = pair("osel_", [ROWS, HC, CW])

        q_in, k_in, v_in, key_in = ([sem(f"a_{k}_in{p}") for p in range(2)] for k in ("q", "k", "v", "key"))
        pick_done, gathered, qsel_done = sem("a_pick_done"), sem("a_gathered"), sem("a_qsel_done")
        scores0, scores1, max_done, exp_done = sem("a_scores0"), sem("a_scores1"), sem("a_max_done"), sem("a_exp_done")
        rinv_done, pT_ready, pT0_done, pT1_done = sem("a_rinv_done"), sem("a_pT_ready"), sem("a_pT0_done"), sem("a_pT1_done")
        pv_ready, oT_done, o_ready, osel_done = sem("a_pv_ready"), sem("a_oT_done"), sem("a_o_ready"), sem("a_osel_done")
        put_done, scattered, attn_done = sem("a_put_done"), sem("a_scattered"), sem("a_attn_done")

        s_bank, t_bank, ot_bank, g_bank, o_bank, a_bank = banks[0:2], banks[2:4], banks[4], banks[5], banks[6], banks[7]
        ident = c[:, CONST["ident"]]
        RUN = (-2, 4, B - 3, B + 1)
        block = ctx.enter_context(nc.Block())

        @block.sync
        def _(sp):
            def slot(h, p):
                v, _, _ = shift(h, p, 0)
                vn, _, pn = shift(h, p, 1)
                vm, _, pm = shift(h, p, -1)
                if within(v, 0, B):
                    wait(sp, scores0, v - 1)
                    wait(sp, scores1, v - 1)
                if within(v, -1, B - 1):
                    wait(sp, gathered, v)
                    sp.dma_start(q1[pn][:, :, :].rearrange("p a b -> p (a b)"),
                                 q_all[:, bass.ds(vn * 2 * D, 2 * D)]).then_inc(q_in[pn], 16)
                if within(v, 0, B):
                    sp.dma_start(k1[p][:, :], k_all[:, bass.ds(v * L, L)]).then_inc(k_in[p], 16)
                wait(sp, pv_ready, v - 2)
                if within(v, 0, B):
                    wait(sp, put_done, v - 1)
                    for hh in range(2):
                        src = S["key_dram"].rearrange("(b c hh) l -> b hh c l", c=HC, hh=2)[bass.ds(v, 1), hh, :, :]
                        sp.dma_start(keyb[p][hh:ROWS:2, :, :], src.to_broadcast([KTOP, HC, L])).then_inc(key_in[p], 16)
                if within(v, 1, B + 1):
                    sp.dma_start(v1[pm][:, :, :].rearrange("p a b -> p (a b)"),
                                 v_all[:, bass.ds(vm * 2 * D, 2 * D)]).then_inc(v_in[pm], 16)

            steps(sp, slot, -1, 4, B - 3, B)

        @block.gpsimd
        def _(pool):
            def slot(h, p):
                u, half, _ = shift(h, p, 0)
                pool.wait_ge(key_in[p], 32 * half + 32)
                wait(pool, scattered, u - 1)
                wait(pool, put_done, u)
                nc.gpsimd.tensor_tensor(gate[:, :], c[0:1, 0:1], c[0:1, 0:1], ALU.add)
                nc.gpsimd.tensor_scalar(put[p][:, :, :], keyb[p][:, :, :], c[0:ROWS, CONST["sidx"]], None,
                                        ALU.is_equal).then_inc(put_done, 1)

            steps(pool, slot, 0, 4, B - 1, B - 1)

        @block.tensor
        def _(pe):
            def slot(h, p):
                u, hu, _ = shift(h, p, 0)
                u1, h1, p1 = shift(h, p, 1)
                um, hm, pm = shift(h, p, -1)
                if within(u, 0, B):
                    pe.wait_ge(qsel_done, u + 1)
                    pe.wait_ge(k_in[p], 16 * hu + 16)
                    wait(pe, exp_done, 4 * u)
                    for ch in range(HC):
                        r, cc = ch // 2, ch % 2
                        ins = nc.tensor.matmul(s_bank[r][0:ROWS, L * cc:L * cc + L], qsel[p][:, ch, :], k1[p][:, :], start=True, stop=True)
                        if cc:
                            ins.then_inc((scores0, scores1)[r], 1)
                if within(u, 2, B + 2):
                    wait(pe, oT_done, u - 1)
                    wait(pe, osel_done, u - 2)
                    nc.tensor.transpose(ot_bank[0:ROWS, 0:128], oT[:, :], ident).then_inc(o_ready, 1)
                if within(u, 1, B + 1):
                    wait(pe, exp_done, 4 * u)
                    wait(pe, pT0_done, u - 1)
                    wait(pe, pT1_done, u - 1)
                    for lt in range(2):
                        for ch in range(HC):
                            ins = nc.tensor.transpose(t_bank[lt][0:LH, ROWS * ch:ROWS * ch + ROWS],
                                                      probs[pm][:, ch, LH * lt:LH * lt + LH], ident[0:ROWS, 0:ROWS])
                        ins.then_inc(pT_ready, 1)
                if within(u, -1, B - 1):
                    pe.wait_ge(q_in[p1], 16 * h1 + 16)
                    pe.wait_ge(pick_done, u + 2)
                    wait(pe, qsel_done, u + 1)
                    for lt in range(2):
                        for ch in range(HC):
                            ins = nc.tensor.matmul(g_bank[CW * ch:CW * ch + CW, 0:ROWS], q1[p1][:, lt, CW * ch:CW * ch + CW],
                                                   pick[p1][:, lt, :, 2 * ch:2 * ch + 2], start=lt == 0, stop=lt == 1)
                    ins.then_inc(gathered, 1)
                if within(u, 2, B + 2):
                    wait(pe, osel_done, u - 1)
                    wait(pe, put_done, u - 1)
                    wait(pe, attn_done, u - 2)
                    for ch in range(HC):
                        ins = nc.tensor.matmul(a_bank[CW * ch:CW * ch + CW, 0:L], osel[p][:, ch, :], put[p][:, ch, :],
                                               start=True, stop=True)
                    ins.then_inc(scattered, 1)
                if within(u, 1, B + 1):
                    pe.wait_ge(pT0_done, u)
                    pe.wait_ge(pT1_done, u)
                    pe.wait_ge(v_in[pm], 16 * hm + 16)
                    wait(pe, oT_done, u - 1)
                    for lt in range(2):
                        for ch in range(HC):
                            ins = nc.tensor.matmul(o_bank[CW * ch:CW * ch + CW, 0:ROWS], v1[pm][:, lt, CW * ch:CW * ch + CW],
                                                   probsT[:, lt, ch, :], start=lt == 0, stop=lt == 1)
                    ins.then_inc(pv_ready, 1)

            steps(pe, slot, *RUN)

        @block.vector
        def _(dve):
            def slot(h, p):
                u, _, _ = shift(h, p, 0)
                u2, _, p2 = shift(h, p, 2)
                _, _, p1 = shift(h, p, 1)
                _, _, pm = shift(h, p, -1)
                if within(u, 0, B):
                    for r in range(2):
                        dve.wait_ge((scores0, scores1)[r], u + 1)
                        nc.vector.tensor_reduce(negmax[p][:, 2 * r:2 * r + 2],
                                                s_bank[r][0:ROWS, 0:2 * L].rearrange("p (c l) -> p c l", c=2),
                                                AX, ALU.max, negate=True).then_inc(max_done, 1)
                if within(u, 1, B + 1):
                    dve.wait_ge(exp_done, 4 * u)
                    wait(dve, osel_done, u - 2)
                    nc.vector.reciprocal(rinv[pm][:, :], rowsum[pm][:, :]).then_inc(rinv_done, 1)
                if within(u, 2, B + 2):
                    dve.wait_ge(o_ready, u - 1)
                    dve.wait_ge(rinv_done, u - 1)
                    wait(dve, scattered, u - 3)
                    nc.vector.tensor_tensor(osel[p][:, :, :], ot_bank[0:ROWS, 0:128].rearrange("p (c f) -> p c f", c=HC),
                                            rinv[p][:, :].unsqueeze(2).to_broadcast([ROWS, HC, CW]), ALU.mult).then_inc(osel_done, 1)
                if within(u, 1, B + 1):
                    dve.wait_ge(pT_ready, 2 * u - 1)
                    wait(dve, pv_ready, u - 1)
                    nc.vector.tensor_copy(probsT[:, 0, :, :].rearrange("p c s -> p (c s)"), t_bank[0][0:LH, 0:HC * ROWS]).then_inc(pT0_done, 1)
                if within(u, -1, B - 1):
                    dve.wait_ge(gathered, u + 2)
                    wait(dve, scores1, u)
                    nc.vector.tensor_tensor(qsel[p1][:, :, :], g_bank[:, 0:ROWS].unsqueeze(1).to_broadcast([128, HC, ROWS]),
                                            c[:, CONST["qmask"]].rearrange("p (c s) -> p c s", c=HC), ALU.mult).then_inc(qsel_done, 1)
                if within(u, -2, B - 2):
                    wait(dve, gathered, u + 1)
                    nc.vector.tensor_tensor(pick[p2][:, :, :, :],
                                            c[0:LH, CONST["siota"]].rearrange("p (s h) -> p s h", h=H).unsqueeze(1).to_broadcast([LH, 2, KTOP, H]),
                                            key_all[:, :, bass.ds(u2, 1), :].to_broadcast([LH, 2, KTOP, H]),
                                            ALU.is_equal).then_inc(pick_done, 1)
                if within(u, 1, B + 1):
                    dve.wait_ge(pv_ready, u)
                    wait(dve, o_ready, u - 1)
                    nc.vector.tensor_tensor(oT[:, :], o_bank[:, 0:ROWS], c[:, CONST["omask"]], ALU.mult).then_inc(oT_done, 1)

            steps(dve, slot, *RUN)

        @block.scalar
        def _(act):
            def slot(h, p):
                u, _, _ = shift(h, p, 0)
                um2, _, _ = shift(h, p, -2)
                for ch in range(HC):
                    if within(u, 0, B):
                        if ch == 0:
                            wait(act, rinv_done, u - 1)
                            wait(act, pT_ready, 2 * u - 2)
                        if ch % 2 == 0:
                            act.wait_ge(max_done, 2 * u + 1 + ch // 2)
                        nc.scalar.activation(probs[p][:, ch, :], s_bank[ch // 2][0:ROWS, L * (ch % 2):L * (ch % 2) + L], ACT.Exp,
                                             bias=negmax[p][:, ch:ch + 1], accum_out=rowsum[p][:, ch:ch + 1]).then_inc(exp_done, 1)
                    if ch == 1 and within(u, 1, B + 1):
                        act.wait_ge(pT_ready, 2 * u)
                        wait(act, pv_ready, u - 1)
                        nc.scalar.activation(probsT[:, 1, :, :].rearrange("p c s -> p (c s)"), t_bank[1][0:LH, 0:HC * ROWS], ACT.Copy).then_inc(pT1_done, 1)
                if within(u, 2, B + 2):
                    act.wait_ge(scattered, u - 1)
                    nc.scalar.activation(attn_all[:, bass.ds(um2 * L, L)], a_bank[:, 0:L], ACT.Identity,
                                         bias=meanv[:, bass.ds(um2, 1)]).then_inc(attn_done, 1)

            steps(act, slot, *RUN)


def ffn_conv(S):
    nc, w, c, cols, rows, banks = (S[k] for k in ("nc", "w", "c", "cols", "rows", "banks"))
    attn_all, n3T_all, z_all = (S[k] for k in ("attn_all", "n3T_all", "z_all"))
    with ExitStack() as ctx:
        def sb(name, shape, dt=F32):
            return ctx.enter_context(nc.sbuf_tensor(name, shape, dt))

        def sem(name):
            return ctx.enter_context(nc.semaphore(name))

        def pair(name, shape, dt=F32):
            return [sb(f"{name}{p}", shape, dt) for p in range(2)]

        attn = pair("attn_", [128, 2 * L])
        xt = pair("xt_", [LH, 4, D])
        ao = sb("ao", [LH, 4, D])
        aob = pair("aob_", [LH, 4, D])
        xb = pair("xb_", [LH, 4, D])
        t1 = sb("t1", [LH, 4, D])
        n1 = sb("n1", [LH, 4, D])
        hb = pair("hb_", [LH, 4, D])
        h1T = pair("h1T_", [128, 2 * L])
        hid = sb("hid", [128, 4, 2 * L])
        t2 = sb("t2", [LH, 4, D])
        n2 = sb("n2", [LH, 4, D])
        fused = sb("fused", [LH, 4, D])
        yin = sb("yin", [128, 2, L + 2])
        ymax = sb("ymax", [128, 2 * LH])
        h0T = sb("h0T", [128, 2 * LH])
        h0 = sb("h0", [LH, 2, D])
        n3 = sb("n3", [LH, 2, D])
        gate = sb("gate", [1, 1])
        hbias = sb("hbias", [LH, D])
        obias = sb("obias", [LH, D])
        st = [sb(f"st{i}", [LH, n, 6]) for i, n in enumerate((4, 4, 2))]
        mv = [sb(f"mv{i}", [LH, n, 2]) for i, n in enumerate((4, 4, 2))]
        sd = [sb(f"sd{i}", [LH, n]) for i, n in enumerate((4, 4, 2))]
        rstd = [sb(f"rstd{i}", [LH, n]) for i, n in enumerate((4, 4, 2))]

        at_in = [sem(f"f_attn_in{p}") for p in range(2)]
        x_in = [sem(f"f_x_in{p}") for p in range(2)]
        ready = sem("f_ready")
        ao_ready, ao_done, t1_done, aob_done = sem("f_ao_ready"), sem("f_ao_done"), sem("f_t1_done"), sem("f_aob_done")
        bias_done, xb_done = sem("f_bias_done"), sem("f_xb_done")
        bn, aggr, sd_done, rs_done, norm = ([sem(f"f_{k}{i}") for i in range(3)] for k in ("bn", "aggr", "sd", "rstd", "norm"))
        n1T_ready, h1T_done, hb_mul, hb_done = sem("f_n1T_ready"), sem("f_h1T_done"), sem("f_hb_mul"), sem("f_hb_done")
        f1_ready, hid_done, f2_ready, t2_done = sem("f_f1_ready"), sem("f_hid_done"), sem("f_f2_ready"), sem("f_t2_done")
        fu_mul, fused_done, fT_ready, yin_done = sem("f_fu_mul"), sem("f_fused_done"), sem("f_fT_ready"), sem("f_yin_done")
        conv_ready, max_done, h0T_done, h0_ready = sem("f_conv_ready"), sem("f_max_done"), sem("f_h0T_done"), sem("f_h0_ready")
        h0_done, h0b_done, n3T_ready, n3T_done = sem("f_h0_done"), sem("f_h0b_done"), sem("f_n3T_ready"), sem("f_n3T_done")

        f_bank, ao_bank, f2_bank, n1_bank, fu_bank, cv_bank, h_bank = banks[0:2], banks[2], banks[3], banks[4], banks[5], banks[6], banks[7]
        ident = c[:, CONST["ident"]]
        NP = NPAIR
        RUN = (-2, 4, NP - 3, NP + 1)

        def row(name, n):
            i = RWS.index(name)
            return rows[0:LH, i:i + 1, :].to_broadcast([LH, n, D])

        def col(name):
            i = COLS.index(name)
            return cols[:, i:i + 1]

        def tok(bank, n=4):
            return bank[0:LH, 0:n * D].rearrange("p (a b) -> p a b", b=D)

        block = ctx.enter_context(nc.Block())

        @block.sync
        def _(sp):
            def slot(h, p):
                t, _, _ = shift(h, p, 0)
                wait(sp, ao_ready, t - 1)
                sp.dma_start(attn[p][:, :], attn_all[:, bass.ds(t * 2 * L, 2 * L)]).then_inc(at_in[p], 16)
                wait(sp, xb_done, t - 1)
                sp.dma_start(xt[p][:, :, :], S["xtok"][:, bass.ds(t * 4, 4), :]).then_inc(x_in[p], 16)

            steps(sp, slot, 0, 2, NP - 1, NP - 1)

        @block.tensor
        def _(pe):
            def slot(h, p):
                t, _, _ = shift(h, p, 0)
                _, hn, pn = shift(h, p, 1)
                if within(t, -1, NP - 1):
                    pe.wait_ge(at_in[pn], 16 * hn + 16)
                    wait(pe, ao_done, t + 1)
                    for j in range(4):
                        ins = nc.tensor.matmul(ao_bank[0:LH, D * j:D * j + D], attn[pn][:, LH * j:LH * j + LH], w[:, WEIGHT["o"]],
                                               start=True, stop=True)
                    ins.then_inc(ao_ready, 1)
                if within(t, 0, NP):
                    pe.wait_ge(h1T_done, t + 1)
                    for k in range(4):
                        wait(pe, hid_done, 4 * t + k - 1)
                        nc.tensor.matmul(f_bank[k % 2][:, 0:2 * L], w[:, WEIGHT["f1"].start + 128 * k:WEIGHT["f1"].start + 128 * k + 128],
                                         h1T[p][:, :], start=True, stop=True).then_inc(f1_ready, 1)
                if within(t, 2, NP + 2):
                    pe.wait_ge(h0T_done, t - 1)
                    wait(pe, n3T_done, t - 2)
                    for b in range(2):
                        ins = nc.tensor.transpose(h_bank[0:LH, D * b:D * b + D], h0T[:, LH * b:LH * b + LH], ident)
                    ins.then_inc(h0_ready, 1)
                if within(t, 1, NP + 1):
                    pe.wait_ge(fused_done, t)
                    wait(pe, yin_done, t - 1)
                    for j in range(4):
                        ins = nc.tensor.transpose(fu_bank[:, LH * j:LH * j + LH], fused[:, j, :], ident[0:LH, 0:LH])
                    ins.then_inc(fT_ready, 1)
                if within(t, 0, NP):
                    wait(pe, t2_done, t)
                    for j in range(4):
                        for k in range(4):
                            if j == 0:
                                pe.wait_ge(hid_done, 4 * t + k + 1)
                            ins = nc.tensor.matmul(f2_bank[0:LH, D * j:D * j + D], hid[:, k, LH * j:LH * j + LH],
                                                   w[:, WEIGHT["f2"].start + D * k:WEIGHT["f2"].start + D * k + D],
                                                   start=k == 0, stop=k == 3)
                    ins.then_inc(f2_ready, 1)
                if within(t, 2, NP + 2):
                    pe.wait_ge(norm[2], t - 1)
                    for b in range(2):
                        ins = nc.tensor.transpose(h_bank[:, 256 + LH * b:256 + LH * b + LH], n3[:, b, :], ident[0:LH, 0:LH])
                    ins.then_inc(n3T_ready, 1)
                if within(t, -1, NP - 1):
                    pe.wait_ge(norm[0], t + 2)
                    wait(pe, h1T_done, t + 1)
                    for j in range(4):
                        ins = nc.tensor.transpose(n1_bank[:, LH * j:LH * j + LH], n1[:, j, :], ident[0:LH, 0:LH])
                    ins.then_inc(n1T_ready, 1)
                if within(t, 1, NP + 1):
                    pe.wait_ge(yin_done, t)
                    wait(pe, max_done, t - 1)
                    for k in range(3):
                        ins = nc.tensor.matmul(cv_bank[:, 0:2 * L].rearrange("p (b l) -> p b l", b=2),
                                               w[:, WEIGHT["conv"].start + D * k:WEIGHT["conv"].start + D * k + D],
                                               yin[:, :, k:k + L], start=k == 0, stop=k == 2)
                    ins.then_inc(conv_ready, 1)

            steps(pe, slot, *RUN)

        @block.scalar
        def _(act):
            def root(i, count):
                act.wait_ge(aggr[i], count)
                wait(act, rs_done[i], count - 1)
                nc.scalar.activation(sd[i][:, :].unsqueeze(2), mv[i][:, :, 1:2], ACT.Sqrt, bias=c[0:LH, CONST["eps"]]).then_inc(sd_done[i], 1)

            def slot(h, p):
                t, _, _ = shift(h, p, 0)
                tm2, _, _ = shift(h, p, -2)
                _, _, pn = shift(h, p, 1)
                if within(t, 2, NP + 2):
                    act.wait_ge(max_done, t - 1)
                    wait(act, h0_ready, t - 2)
                    nc.scalar.activation(h0T[:, :], ymax[:, :], ACT.Relu, bias=col("conv_b")).then_inc(h0T_done, 1)
                for k in range(4):
                    if k == 2 and within(t, -1, NP - 1):
                        act.wait_ge(t1_done, t + 2)
                        wait(act, aob_done, t + 1)
                        nc.scalar.activation(ao[:, :, :], tok(ao_bank), ACT.Copy).then_inc(ao_done, 1)
                        root(0, t + 2)
                    if within(t, 0, NP):
                        if k == 0:
                            wait(act, f2_ready, t)
                        act.wait_ge(f1_ready, 4 * t + k + 1)
                        nc.scalar.activation(hid[:, k, :], f_bank[k % 2][:, 0:2 * L], ACT.Relu, bias=col(f"f1_{k}")).then_inc(hid_done, 1)
                if within(t, 1, NP + 1):
                    act.wait_ge(fT_ready, t)
                    if isinstance(t, int) and t == 1:
                        act.wait_ge(ready, 1)
                    wait(act, conv_ready, t - 1)
                    nc.scalar.activation(yin[:, :, 1:L + 1], fu_bank[:, 0:2 * L].rearrange("p (b l) -> p b l", b=2), ACT.Copy).then_inc(yin_done, 1)
                if within(t, 2, NP + 2):
                    root(2, t - 1)
                    act.wait_ge(n3T_ready, t - 1)
                    nc.scalar.activation(n3T_all[:, bass.ds(tm2 * 2 * LH, 2 * LH)], h_bank[:, 256:256 + 2 * LH], ACT.Copy).then_inc(n3T_done, 1)
                if within(t, -1, NP - 1):
                    act.wait_ge(n1T_ready, t + 2)
                    wait(act, f1_ready, 4 * t)
                    nc.scalar.activation(h1T[pn][:, :], n1_bank[:, 0:2 * L], ACT.Identity, scale=col("ln1_g"), bias=col("ln1_b")).then_inc(h1T_done, 1)
                if within(t, 0, NP):
                    root(1, t + 1)

            steps(act, slot, *RUN)

        @block.vector
        def _(dve):
            nc.vector.memset(yin[:, :, 0:1], 0.0)
            nc.vector.memset(yin[:, :, L + 1:L + 2], 0.0).then_inc(ready, 1)

            def stats(i, src, n, count):
                wait(dve, sd_done[i], count - 1)
                wait(dve, norm[i], count - 1)
                for j in range(n):
                    ins = nc.vector.bn_stats(st[i][:, j, :], src[:, j, :])
                ins.then_inc(bn[i], 1)
                dve.wait_ge(bn[i], count)
                nc.vector.memset(gate[:, :], 0.0)
                for j in range(n):
                    ins = nc.vector.bn_aggr(mv[i][:, j, :], st[i][:, j, :])
                ins.then_inc(aggr[i], 1)

            def normalise(i, dst, src, n, count):
                dve.wait_ge(sd_done[i], count)
                nc.vector.reciprocal(rstd[i][:, :], sd[i][:, :]).then_inc(rs_done[i], 1)
                dve.wait_ge(rs_done[i], count)
                for j in range(n):
                    ins = nc.vector.tensor_scalar(dst[:, j, :], src[:, j, :], mv[i][:, j, 0:1], rstd[i][:, j:j + 1],
                                                  ALU.subtract, ALU.mult)
                ins.then_inc(norm[i], 1)

            def slot(h, p):
                t, _, _ = shift(h, p, 0)
                _, hn, pn = shift(h, p, 1)
                if within(t, 1, NP + 1):
                    wait(dve, fused_done, t - 1)
                    normalise(1, n2, t2, 4, t)
                if within(t, 2, NP + 2):
                    dve.wait_ge(conv_ready, t - 1)
                    wait(dve, h0T_done, t - 2)
                    nc.vector.tensor_reduce(ymax[:, :], cv_bank[:, 0:2 * L].rearrange("p (l two) -> p l two", two=2), AX, ALU.max).then_inc(max_done, 1)
                if within(t, -1, NP - 1):
                    dve.wait_ge(ao_ready, t + 2)
                    dve.wait_ge(xb_done, t + 2)
                    wait(dve, norm[0], t + 1)
                    nc.vector.tensor_tensor(t1[:, :, :], tok(ao_bank), xb[pn][:, :, :], ALU.add).then_inc(t1_done, 1)
                    dve.wait_ge(t1_done, t + 2)
                    stats(0, t1, 4, t + 2)
                    wait(dve, n1T_ready, t + 1)
                    wait(dve, hb_mul, t + 1)
                    normalise(0, n1, t1, 4, t + 2)
                if within(t, 2, NP + 2):
                    dve.wait_ge(h0_ready, t - 1)
                    wait(dve, h0b_done, t - 2)
                    wait(dve, norm[2], t - 2)
                    nc.vector.tensor_copy(h0[:, :, :], tok(h_bank, 2)).then_inc(h0_done, 1)
                    dve.wait_ge(h0_done, t - 1)
                    stats(2, h0, 2, t - 1)
                    wait(dve, n3T_ready, t - 2)
                    normalise(2, n3, h0, 2, t - 1)
                if within(t, 0, NP):
                    dve.wait_ge(f2_ready, t + 1)
                    dve.wait_ge(hb_done, t + 1)
                    wait(dve, norm[1], t)
                    nc.vector.tensor_tensor(t2[:, :, :], tok(f2_bank), hb[p][:, :, :], ALU.add).then_inc(t2_done, 1)
                    dve.wait_ge(t2_done, t + 1)
                    stats(1, t2, 4, t + 1)

            steps(dve, slot, *RUN)

        @block.gpsimd
        def _(pool):
            for dst, one, other in ((hbias, "ln1_b", "f2_b"), (obias, "o_b", "ln2_b")):
                nc.gpsimd.tensor_tensor(dst[:, :], rows[0:LH, RWS.index(one), :], rows[0:LH, RWS.index(other), :], ALU.add).then_inc(bias_done, 1)
            pool.wait_ge(bias_done, 2)

            def slot(h, p):
                t, _, _ = shift(h, p, 0)
                tm2, _, _ = shift(h, p, -2)
                _, h2, _ = shift(h, p, 2)
                _, _, pn = shift(h, p, 1)
                pm = pn
                if within(t, 1, NP + 1):
                    pool.wait_ge(norm[1], t)
                    wait(pool, fT_ready, t - 1)
                    nc.gpsimd.tensor_tensor(fused[:, :, :], n2[:, :, :], row("ln2_g", 4), ALU.mult).then_inc(fu_mul, 1)
                    pool.wait_ge(fu_mul, t)
                    pool.wait_ge(aob_done, t)
                    nc.gpsimd.tensor_tensor(fused[:, :, :], fused[:, :, :], aob[pm][:, :, :], ALU.add).then_inc(fused_done, 1)
                if within(t, -1, NP - 1):
                    pool.wait_ge(ao_done, t + 2)
                    wait(pool, fused_done, t)
                    nc.gpsimd.tensor_tensor(aob[pn][:, :, :], ao[:, :, :], obias[:, :].unsqueeze(1).to_broadcast([LH, 4, D]), ALU.add).then_inc(aob_done, 1)
                if within(t, -1, NP - 1):
                    pool.wait_ge(norm[0], t + 2)
                    wait(pool, t2_done, t)
                    nc.gpsimd.tensor_tensor(hb[pn][:, :, :], n1[:, :, :], row("ln1_g", 4), ALU.mult).then_inc(hb_mul, 1)
                    pool.wait_ge(hb_mul, t + 2)
                    nc.gpsimd.tensor_tensor(hb[pn][:, :, :], hb[pn][:, :, :], hbias[:, :].unsqueeze(1).to_broadcast([LH, 4, D]), ALU.add).then_inc(hb_done, 1)
                if within(t, 2, NP + 2):
                    pool.wait_ge(h0_done, t - 1)
                    nc.gpsimd.tensor_tensor(z_all[:, bass.ds(tm2 * 2, 2), :], h0[:, :, :], row("wp_b", 2), ALU.add).then_inc(h0b_done, 1)
                if within(t, -2, NP - 2):
                    pool.wait_ge(x_in[p], 16 * h2 + 16)
                    wait(pool, t1_done, t + 1)
                    nc.gpsimd.tensor_tensor(xb[p][:, :, :], xt[p][:, :, :], row("o_b", 4), ALU.add).then_inc(xb_done, 1)

            steps(pool, slot, *RUN)


def window_attention(S):
    nc, w, c, cols, rows, banks = (S[k] for k in ("nc", "w", "c", "cols", "rows", "banks"))
    n3T_all, z_all = S["n3T_all"], S["z_all"]
    with ExitStack() as ctx:
        def sb(name, shape, dt=F32):
            return ctx.enter_context(nc.sbuf_tensor(name, shape, dt))

        def sem(name):
            return ctx.enter_context(nc.semaphore(name))

        def pair(name, shape, dt=F32):
            return [sb(f"{name}{p}", shape, dt) for p in range(2)]

        n3 = pair("n3T_", [128, LH])
        qT = pair("wqT_", [128, LH])
        kT = sb("wkT", [128, LH])
        kbd = pair("kbd_", [128, 4, LH])
        vo = pair("vo_", [LH, H, CW])
        negmax = pair("wmax_", [LH, H])
        probs = pair("wprobs_", [LH, H, LH])
        probsT = sb("wprobsT", [LH, H, LH])
        oT = sb("woT", [128, 2 * LH])
        rinv = sb("wrinv", [LH, H])
        otok = sb("otok", [LH, D])
        oF = sb("oF", [128, LH])
        gate = sb("wgate", [1, 2])
        st = sb("st_all", [LH, B, 6])
        mean = sb("mean_z", [LH, B])
        var = sb("var_z", [LH, B])
        tmp = sb("tmp_z", [LH, B])
        sdz = sb("sd_z", [LH, B])
        rs = sb("rstd_z", [LH, B])
        gain = sb("gain_z", [LH, B])
        offs = sb("offs_z", [LH, B])
        o = sb("o_all", [LH, B, D])

        n_in = [sem(f"w_n_in{p}") for p in range(2)]
        ready, kT_done, qT_done, kbd_done, v_done = sem("w_ready"), sem("w_kT_done"), sem("w_qT_done"), sem("w_kbd_done"), sem("w_v_done")
        qk_ready, v_ready, scores, max_done, exp_done = sem("w_qk_ready"), sem("w_v_ready"), sem("w_scores"), sem("w_max_done"), sem("w_exp_done")
        pT_ready, pT0_done, pT1_done = sem("w_pT_ready"), sem("w_pT0_done"), sem("w_pT1_done")
        pv_ready, oT_done, otok_ready, rinv_done, otok_done = sem("w_pv_ready"), sem("w_oT_done"), sem("w_otok_ready"), sem("w_rinv_done"), sem("w_otok_done")
        oF_ready, oF_done, proj_ready, z_done = sem("w_oF_ready"), sem("w_oF_done"), sem("w_proj_ready"), sem("w_z_done")
        stat, chain, root_done, out_done, stored = sem("w_stat"), sem("w_chain"), sem("w_root_done"), [sem(f"w_out{i}") for i in range(2)], sem("w_stored")

        s_bank, t_bank, q_bank, o_bank, a_bank, f_bank = banks[0:2], banks[2:4], banks[4], banks[5], banks[6], banks[7]
        ident = c[:, CONST["ident"]]
        RUN = (-1, 4, B - 3, B + 2)

        def col(name):
            i = COLS.index(name)
            return cols[:, i:i + 1]

        block = ctx.enter_context(nc.Block())

        @block.sync
        def _(sp):
            def slot(h, p):
                u, _, _ = shift(h, p, 0)
                wait(sp, v_ready, u - 1)
                sp.dma_start(n3[p][:, :], n3T_all[:, bass.ds(u * LH, LH)]).then_inc(n_in[p], 16)

            steps(sp, slot, 0, 4, B - 1, B - 1)
            for g in range(4):
                sp.wait_ge(out_done[0], 4 * g + 4)
                sp.wait_ge(out_done[1], 4 * g + 4)
                sp.dma_start(S["out"].rearrange("b l d -> l b d")[:, 8 * g:8 * g + 8, :], o[:, 8 * g:8 * g + 8, :]).then_inc(stored, 16)
            sp.wait_ge(stored, 64)

        @block.tensor
        def _(pe):
            pe.wait_ge(ready, 2)

            def slot(h, p):
                u, hu, _ = shift(h, p, 0)
                un, _, _ = shift(h, p, 1)
                _, _, pm = shift(h, p, -1)

                def scores_of(r):
                    if r == 0:
                        pe.wait_ge(qT_done, u + 1)
                        pe.wait_ge(kbd_done, u + 1)
                    wait(pe, exp_done, 2 * u - 1 + r)
                    nc.tensor.matmul(s_bank[r][0:LH, 0:4 * LH], qT[p][64 * r:64 * r + 64, :],
                                     kbd[p][64 * r:64 * r + 64, :, :].rearrange("p h l -> p (h l)"), start=True, stop=True).then_inc(scores, 1)

                def turn(r):
                    wait(pe, (pT0_done, pT1_done)[r], u - 1)
                    pe.wait_ge(exp_done, 2 * u - 1 + r)
                    for j in range(4):
                        ins = nc.tensor.transpose(t_bank[r][0:LH, LH * j:LH * j + LH], probs[pm][:, 4 * r + j, :], ident[0:LH, 0:LH])
                    ins.then_inc(pT_ready, 1)

                if within(u, 0, B):
                    scores_of(0)
                if within(u, -1, B - 1):
                    wait(pe, qT_done, u + 1)
                    for i, name in enumerate(("wk", "wq")):
                        ins = nc.tensor.matmul(q_bank[:, 128 * i:128 * i + LH], w[:, WEIGHT[name]], n3T_all[:, bass.ds(un * LH, LH)], start=True, stop=True)
                    ins.then_inc(qk_ready, 1)
                if within(u, 3, B + 3):
                    pe.wait_ge(otok_done, u - 2)
                    wait(pe, z_done, u - 3)
                    nc.tensor.transpose(f_bank[:, 0:LH], otok[:, :], ident[0:LH, 0:LH]).then_inc(oF_ready, 1)
                if within(u, 1, B + 1):
                    turn(0)
                if within(u, 0, B):
                    scores_of(1)
                if within(u, 3, B + 3):
                    pe.wait_ge(oF_done, u - 2)
                    nc.tensor.matmul(f_bank[0:LH, 256:256 + D], oF[:, :], w[:, WEIGHT["wp"]], start=True, stop=True).then_inc(proj_ready, 1)
                if within(u, 1, B + 1):
                    turn(1)
                if within(u, 2, B + 2):
                    pe.wait_ge(oT_done, u - 1)
                    wait(pe, otok_done, u - 2)
                    for i in range(2):
                        ins = nc.tensor.transpose(a_bank[0:LH, 128 * i:128 * i + 128], oT[:, LH * i:LH * i + LH], ident)
                    ins.then_inc(otok_ready, 1)
                if within(u, 0, B):
                    pe.wait_ge(n_in[p], 16 * hu + 16)
                    wait(pe, v_done, u)
                    wait(pe, oT_done, u - 1)
                    nc.tensor.matmul(o_bank[0:LH, 256:256 + D], n3[p][:, :], w[:, WEIGHT["wv"]], start=True, stop=True).then_inc(v_ready, 1)
                if within(u, 1, B + 1):
                    pe.wait_ge(v_done, u)
                    for j in range(H):
                        if j % 4 == 0:
                            pe.wait_ge((pT0_done, pT1_done)[j // 4], u)
                        ins = nc.tensor.matmul(o_bank[CW * (j % 4):CW * (j % 4) + CW, LH * (j // 4):LH * (j // 4) + LH],
                                               vo[pm][:, j, :], probsT[:, j, :], start=True, stop=True)
                    ins.then_inc(pv_ready, 1)

            steps(pe, slot, *RUN)

        @block.scalar
        def _(act):
            def slot(h, p):
                u, _, _ = shift(h, p, 0)
                _, _, pn = shift(h, p, 1)

                def exponents(r):
                    act.wait_ge(max_done, 2 * u + 1 + r)
                    for j in range(4 * r, 4 * r + 4):
                        ins = nc.scalar.activation(probs[p][:, j, :], s_bank[r][0:LH, LH * (j % 4):LH * (j % 4) + LH], ACT.Exp,
                                                   bias=negmax[p][:, j:j + 1], scale=-1.0)
                    ins.then_inc(exp_done, 1)

                if within(u, -1, B - 1):
                    act.wait_ge(qk_ready, u + 2)
                    wait(act, kbd_done, u + 1)
                    nc.scalar.activation(kT[:, :], q_bank[:, 0:LH], ACT.Identity, bias=col("wk_b")).then_inc(kT_done, 1)
                    wait(act, scores, 2 * u)
                    nc.scalar.activation(qT[pn][:, :], q_bank[:, 128:128 + LH], ACT.Identity, bias=col("wq_b")).then_inc(qT_done, 1)
                if within(u, 3, B + 3):
                    act.wait_ge(oF_ready, u - 2)
                    wait(act, proj_ready, u - 3)
                    nc.scalar.activation(oF[:, :], f_bank[:, 0:LH], ACT.Identity, bias=col("wv_b")).then_inc(oF_done, 1)
                if within(u, 0, B):
                    wait(act, pT_ready, 2 * u - 2)
                    exponents(0)
                if within(u, 1, B + 1):
                    act.wait_ge(pT_ready, 2 * u)
                    wait(act, pv_ready, u - 1)
                    nc.scalar.activation(probsT[:, 4:8, :].rearrange("p h l -> p (h l)"), t_bank[1][0:LH, 0:4 * LH], ACT.Copy).then_inc(pT1_done, 1)
                if within(u, 0, B):
                    exponents(1)
                if within(u, 1, B + 1):
                    act.wait_ge(pv_ready, u)
                    wait(act, otok_ready, u - 1)
                    nc.scalar.activation(oT[:, :], o_bank[:, 0:2 * LH], ACT.Copy).then_inc(oT_done, 1)
                if within(u, 0, B):
                    act.wait_ge(v_ready, u + 1)
                    nc.scalar.activation(vo[p][:, :, 0:HD], o_bank[0:LH, 256:256 + D].rearrange("p (h f) -> p h f", h=H), ACT.Copy).then_inc(v_done, 1)

            steps(act, slot, *RUN)
            act.wait_ge(chain, 6)
            nc.scalar.activation(sdz[:, :], var[:, :], ACT.Sqrt, bias=c[0:LH, CONST["eps"]]).then_inc(root_done, 1)
            act.wait_ge(chain, 9)
            for b in range(1, B, 2):
                nc.scalar.activation(o[:, b, :], z_all[:, b, :], ACT.Identity, scale=gain[:, b:b + 1], bias=offs[:, b:b + 1]).then_inc(out_done[1], 1)

        @block.gpsimd
        def _(pool):
            def slot(h, p):
                u, _, _ = shift(h, p, 0)
                pool.wait_ge(kT_done, u + 1)
                wait(pool, scores, 2 * u - 2)
                nc.gpsimd.tensor_tensor(kbd[p][:, :, :], kT[:, :].unsqueeze(1).to_broadcast([128, 4, LH]),
                                        c[:, CONST["kmask"]].unsqueeze(2).to_broadcast([128, 4, LH]), ALU.mult).then_inc(kbd_done, 1)

            steps(pool, slot, 0, 4, B - 1, B - 1)

        @block.vector
        def _(dve):
            for i in range(2):
                nc.vector.memset(vo[i][:, :, HD:CW], 1.0).then_inc(ready, 1)

            def slot(h, p):
                u, _, _ = shift(h, p, 0)
                um3, _, _ = shift(h, p, -3)

                def mask_and_max(r):
                    dve.wait_ge(scores, 2 * u + 1 + r)
                    nc.vector.memset(gate[:, r:r + 1], 0.0)
                    for j in range(4 * r, 4 * r + 4):
                        s = s_bank[r][0:LH, LH * (j % 4):LH * (j % 4) + LH]
                        ins = nc.vector.tensor_tensor_reduce(s, s, c[0:LH, CONST["band"]], 1.0, OFF, ALU.add, ALU.min, negmax[p][:, j:j + 1])
                    ins.then_inc(max_done, 1)

                if within(u, 0, B):
                    mask_and_max(0)
                if within(u, 1, B + 1):
                    dve.wait_ge(pT_ready, 2 * u - 1)
                    wait(dve, pv_ready, u - 1)
                    nc.vector.tensor_copy(probsT[:, 0:4, :].rearrange("p h l -> p (h l)"), t_bank[0][0:LH, 0:4 * LH]).then_inc(pT0_done, 1)
                if within(u, 0, B):
                    mask_and_max(1)
                if within(u, 2, B + 2):
                    dve.wait_ge(otok_ready, u - 1)
                    wait(dve, otok_done, u - 2)
                    nc.vector.reciprocal(rinv[:, :], a_bank[0:LH, 0:2 * 128].rearrange("p (h f) -> p h f", h=H)[:, :, HD]).then_inc(rinv_done, 1)
                if within(u, 3, B + 3):
                    dve.wait_ge(proj_ready, u - 2)
                    nc.vector.tensor_tensor(z_all[:, bass.ds(um3, 1), :], f_bank[0:LH, 256:256 + D].unsqueeze(1), z_all[:, bass.ds(um3, 1), :], ALU.add).then_inc(z_done, 1)
                if within(u, 2, B + 2):
                    dve.wait_ge(rinv_done, u - 1)
                    wait(dve, oF_ready, u - 2)
                    nc.vector.tensor_tensor(otok[:, :].rearrange("p (h f) -> p h f", h=H),
                                            a_bank[0:LH, 0:2 * 128].rearrange("p (h f) -> p h f", h=H)[:, :, 0:HD],
                                            rinv[:, :].unsqueeze(2).to_broadcast([LH, H, HD]), ALU.mult).then_inc(otok_done, 1)
                if within(u, 3, B + 3):
                    dve.wait_ge(z_done, u - 2)
                    nc.vector.bn_stats(st[:, bass.ds(um3, 1), :].rearrange("p a b -> p (a b)"), z_all[:, bass.ds(um3, 1), :].rearrange("p a b -> p (a b)")).then_inc(stat, 1)

            steps(dve, slot, *RUN)

            dve.wait_ge(stat, B)
            m0, m1, q0, q1 = (st[:, :, i] for i in (1, 4, 2, 5))
            nc.vector.tensor_tensor(mean[:, :], m0, m1, ALU.add).then_inc(chain, 1)
            nc.vector.tensor_tensor(tmp[:, :], m0, m1, ALU.subtract).then_inc(chain, 1)
            nc.vector.tensor_tensor(var[:, :], q0, q1, ALU.add).then_inc(chain, 1)
            dve.wait_ge(chain, 3)
            nc.vector.tensor_tensor(tmp[:, :], tmp[:, :], tmp[:, :], ALU.mult).then_inc(chain, 1)
            dve.wait_ge(chain, 4)
            nc.vector.scalar_tensor_tensor(var[:, :], var[:, :], 4.0 / D, tmp[:, :], ALU.mult, ALU.add).then_inc(chain, 1)
            dve.wait_ge(chain, 5)
            nc.vector.tensor_scalar_mul(var[:, :], var[:, :], 0.25).then_inc(chain, 1)
            dve.wait_ge(root_done, 1)
            nc.vector.reciprocal(rs[:, :], sdz[:, :]).then_inc(chain, 1)
            dve.wait_ge(chain, 7)
            nc.vector.tensor_scalar(gain[:, :], rs[:, :], 1.0, None, ALU.add).then_inc(chain, 1)
            nc.vector.scalar_tensor_tensor(offs[:, :], mean[:, :], -0.5, rs[:, :], ALU.mult, ALU.mult).then_inc(chain, 1)
            dve.wait_ge(chain, 9)
            for b in range(0, B, 2):
                nc.vector.tensor_scalar(o[:, b, :], z_all[:, b, :], gain[:, b:b + 1], offs[:, b:b + 1], ALU.mult, ALU.add).then_inc(out_done[0], 1)


def kernel(**inputs):
    import numpy as _np
    import concourse.bacc as _bacc
    from concourse.bass_utils import run_bass_kernel_spmd as _run

    a = {k.removeprefix("L0_"): _np.asarray(v) for k, v in inputs.items()}
    x = a["x"]
    f1_b = a["tok_f1_b"].reshape(4, 128)
    bq, bk, bv = a["attn_b_qkv"].reshape(3, D)
    arrays = {
        "xT": _np.ascontiguousarray(x.transpose(2, 0, 1).reshape(D, B * L)),
        "xtok": _np.ascontiguousarray(x.reshape(B * 2, LH, D).transpose(1, 0, 2)),
        "weights": _np.ascontiguousarray(_np.concatenate([
            a["tok_q_w"], a["tok_k_w"], a["tok_v_w"], a["tok_o_w"], a["tok_f1_w"],
            a["tok_f2_w"].reshape(4, 128, D).transpose(1, 0, 2).reshape(128, F),
            a["tok_conv_w"].transpose(1, 2, 0).reshape(D, 3 * D), a["attn_W_qkv"], a["attn_W_proj"]], axis=1)),
        "consts": constants(),
        "cols": _np.ascontiguousarray(_np.stack([
            a["tok_k_b"], a["tok_v_b"], a["tok_ln1_g"], a["tok_ln1_b"], *f1_b, a["tok_conv_b"], bq, bk, bv], axis=1)),
        "rows": _np.ascontiguousarray(_np.concatenate([
            a["tok_q_b"], a["tok_o_b"], a["tok_ln1_g"], a["tok_ln1_b"], a["tok_f2_b"], a["tok_ln2_g"], a["tok_ln2_b"],
            a["attn_b_proj"]])),
    }
    nc = _bacc.Bacc("TRN2", target_bir_lowering=False, num_devices=1)
    args = [nc.dram_tensor(n, v.shape, mybir.dt.from_np(v.dtype), kind="ExternalInput").ap() for n, v in arrays.items()]
    key_dram = nc.dram_tensor("key_scratch", (B * H, L), BF16, kind="Internal").ap()
    out = nc.dram_tensor("out", (B, LH, D), F32, kind="ExternalOutput").ap()
    program(nc, *args, key_dram, out)
    return _run(nc, [arrays], core_ids=[0]).results[0]["out"]
```

```python
from contextlib import ExitStack

import numpy as np
import concourse.bass as bass
from concourse import mybir

F32 = mybir.dt.float32
BF16 = mybir.dt.bfloat16
ALU = mybir.AluOpType
ACT = mybir.ActivationFunctionType
AX = mybir.AxisListType.X

B, L, D, H, F = 32, 250, 128, 8, 512
HD = D // H
LH = L // 2
KTOP = L // 5
NPAIR = B // 2
HC = H // 2
CW = 2 * HD
ROWS = 2 * KTOP
HALF = 32
EPS = 1e-5
SCALE = HD ** -0.5
OFF = 3.0e38

CONST = {}
WEIGHT = {}


def _columns(table, *sizes):
    at = 0
    for name, n in sizes:
        table[name] = slice(at, at + n)
        at += n
    return at


NCONST = _columns(CONST, ("ident", 128), ("qmask", HC * ROWS), ("omask", ROWS), ("kmask", 4), ("sidx", 1),
                  ("siota", KTOP * H), ("band", LH), ("eps", 1))
NWEIGHT = _columns(WEIGHT, ("q", D), ("k", D), ("v", D), ("o", D), ("f1", F), ("f2", F), ("conv", 3 * D),
                   ("wq", D), ("wk", D), ("wv", D), ("wp", D))
COLS = ["k_b", "v_b", "ln1_g", "ln1_b", "f1_0", "f1_1", "f1_2", "f1_3", "conv_b", "wq_b", "wk_b", "wv_b"]
RWS = ["q_b", "o_b", "ln1_g", "ln1_b", "f2_b", "ln2_g", "ln2_b", "wp_b"]


def constants():
    c = np.zeros((128, NCONST), np.float32)
    p = np.arange(128)
    c[:, CONST["ident"]] = np.eye(128)
    j = np.arange(ROWS)
    own = (p[:, None] % CW) // HD == j[None, :] % 2
    qm = np.stack([own & (p[:, None] // CW == cc) for cc in range(HC)], 1)
    c[:, CONST["qmask"]] = (qm * SCALE).reshape(128, -1)
    c[:, CONST["omask"]] = own
    c[:, CONST["kmask"]] = ((p[:, None] % 64) // HD == np.arange(4)[None, :]) * -SCALE
    c[:, CONST["sidx"]] = (p // 2 + 1)[:, None]
    c[:, CONST["siota"]] = np.repeat(np.arange(1, KTOP + 1), H)[None, :]
    away = np.abs(p[:, None] - np.arange(LH)[None, :]) > HALF
    c[:, CONST["band"]] = np.where(away, OFF, 0.0)
    c[:, CONST["eps"]] = EPS
    return c


def wait(eng, sem, value):
    if isinstance(value, int) and value <= 0:
        return
    eng.wait_ge(sem, value)


def within(u, lo, hi):
    return not isinstance(u, int) or lo <= u < hi


UNROLL = 4


def steps(eng, slot, first, lo, hi, last):
    turns = (hi + 1 - lo) // UNROLL
    for u in range(first, lo):
        slot(u // 2, u % 2)
    if turns:
        with eng.Fori(0, turns) as i:
            for k in range(UNROLL):
                slot(i * (UNROLL // 2) + (lo + k) // 2, k % 2)
    for u in range(lo + UNROLL * turns, last + 1):
        slot(u // 2, u % 2)


def shift(h, p, k):
    h, p = h + (p + k) // 2, (p + k) % 2
    return 2 * h + p, h, p


def program(nc, xT, xtok, weights, consts, cols, rows, key_dram, out):
    with ExitStack() as ctx:
        def sb(name, shape, dt=F32):
            return ctx.enter_context(nc.sbuf_tensor(name, shape, dt))

        S = {
            "nc": nc, "xT": xT, "xtok": xtok, "key_dram": key_dram, "out": out,
            "weights_dram": weights, "consts_dram": consts, "cols_dram": cols, "rows_dram": rows,
            "w": sb("w", [128, NWEIGHT]), "c": sb("c", [128, NCONST]),
            "cols": sb("vec_cols", [128, len(COLS)]), "rows": sb("vec_rows", [128, len(RWS), D]),
            "banks": [ctx.enter_context(nc.psum_tensor(f"bank{i}", [128, 512], F32)) for i in range(8)],
            "meanv": sb("meanv", [128, B]),
        }
        S["attn_all"] = sb("attn_all", [128, B * L])
        for name, shape in (("q1", [LH, 2, D]), ("k1", [128, L]), ("attn", [128, 2 * L]), ("xt", [LH, 4, D])):
            S[name] = [sb(f"{name}_{p}", shape) for p in range(2)]
            S[name + "_in"] = [ctx.enter_context(nc.semaphore(f"{name}_in{p}")) for p in range(2)]
        with ExitStack() as early:
            for name, shape in (("q_all", [LH, B * 2 * D]), ("k_all", [128, B * L]), ("v_all", [LH, B * 2 * D]),
                                ("key_all", [LH, 2, B, H])):
                S[name] = early.enter_context(nc.sbuf_tensor(name, shape, F32))
            measure_and_select(S)
            topk_attention(S)
        S["n3T_all"] = sb("n3T_all", [128, B * LH])
        S["z_all"] = sb("z_all", [LH, B, D])
        ffn_and_window(S)


def measure_and_select(S):
    nc, w, c, cols, rows, banks = (S[k] for k in ("nc", "w", "c", "cols", "rows", "banks"))
    q_all, k_all, v_all, key_all, meanv = (S[k] for k in ("q_all", "k_all", "v_all", "key_all", "meanv"))
    W = L + 8
    NQ = B // 4
    with ExitStack() as ctx:
        def sb(name, shape, dt=F32):
            return ctx.enter_context(nc.sbuf_tensor(name, shape, dt))

        def sem(name):
            return ctx.enter_context(nc.semaphore(name))

        xa = [sb(f"xa{p}", [128, 4 * L]) for p in range(2)]
        x_all = S["attn_all"]
        sq = [sb(f"sq{i}", [LH, 4 * D]) for i in range(2)]
        norm_all = sb("norm_all", [LH, 2, B, H])
        xsum = sb("xsum", [128, B])
        xneg = sb("xneg", [128, B])
        work = [[sb(f"work{g}{i}", [128, W]) for i in range(2)] for g in range(2)]
        top8 = [sb(f"top8_{g}", [128, 8]) for g in range(2)]
        chosen = [sb(f"chosen{g}", [128, L]) for g in range(2)]
        prefix = [sb(f"prefix{g}", [128, L]) for g in range(2)]
        zeros = sb("zeros", [128, L])
        key = [sb(f"key{g}", [128, L]) for g in range(2)]
        key16 = [sb(f"key16_{g}", [128, L], BF16) for g in range(2)]

        params_in = [sem(f"m_params{i}") for i in range(5)]
        x_in = [sem(f"m_x_in{p}") for p in range(2)]
        x_kept = sem("m_x_kept")
        q_ready, q_done, xneg_done, xc_done = sem("m_q_ready"), sem("m_q_done"), sem("m_xneg_done"), sem("m_xc_done")
        k_ready, k_done, v_ready, v_done = sem("m_k_ready"), sem("m_k_done"), sem("m_v_ready"), sem("m_v_done")
        sq_done, norm_done = [sem(f"m_sq_done{i}") for i in range(2)], sem("m_norm_done")
        mean_ready, norm_t_ready, key_t_ready = sem("m_mean_ready"), sem("m_norm_t_ready"), sem("m_key_t_ready")
        setup, key_stored, key_ready, key_t_done = sem("m_setup"), sem("m_key_stored"), sem("m_key_ready"), sem("m_key_t_done")
        select = [sem(f"m_select{g}") for g in range(2)]
        ident = c[:, CONST["ident"]]
        q_bank, k_bank, v_bank, n_bank = banks[0:2], banks[2:4], banks[4:6], banks[6:8]
        block = ctx.enter_context(nc.Block())

        @block.sync
        def _(sp):
            def slot(h, p):
                t, _, _ = shift(h, p, 0)
                wait(sp, k_ready, 2 * t - 2)
                wait(sp, x_kept, 4 * t - 4)
                sp.dma_start(xa[p][:, :], S["xT"][:, bass.ds(t * 4 * L, 4 * L)]).then_inc(x_in[p], 16)

            steps(sp, slot, 0, 4, NQ - 1, NQ - 1)
            sp.dma_start(rows[:, 1:, :].rearrange("p a b -> p (a b)"),
                         S["rows_dram"][D:].partition_broadcast(128)).then_inc(params_in[1], 16)
            sp.dma_start(w[:, 3 * D:], S["weights_dram"][:, 3 * D:]).then_inc(params_in[4], 16)
            sp.wait_ge(q_done, 2)
            for b in range(2):
                sp.dma_start(S["q1"][b][:, :, :].rearrange("p a b -> p (a b)"), q_all[:, 2 * D * b:2 * D * b + 2 * D]).then_inc(S["q1_in"][b], 16)
            sp.wait_ge(k_done, 2)
            sp.dma_start(S["k1"][0][:, :], k_all[:, 0:L]).then_inc(S["k1_in"][0], 16)
            for g in range(2):
                sp.wait_ge(key_ready, g + 1)
                sp.dma_start(S["key_dram"][128 * g:128 * g + 128, :], key16[g][:, :]).then_inc(key_stored, 16)
            sp.wait_ge(key_stored, 32)
            sp.wait_ge(params_in[1], 32)
            sp.wait_ge(params_in[4], 16)

        @block.scalar
        def _(act):
            act.dma_start(w[:, 0:3 * D], S["weights_dram"][:, 0:3 * D]).then_inc(params_in[0], 16)
            act.dma_start(rows[:, 0, :], S["rows_dram"][0:D].partition_broadcast(128)).then_inc(params_in[1], 16)
            act.dma_start(cols[:, :], S["cols_dram"]).then_inc(params_in[3], 16)
            act.dma_start(c[:, :], S["consts_dram"]).then_inc(params_in[2], 16)
            act.wait_ge(params_in[3], 16)

            def slot(h, p):
                t, half, _ = shift(h, p, 0)
                act.wait_ge(x_in[p], 16 * half + 16)
                for j in range(4):
                    nc.scalar.activation(x_all[:, bass.ds(t * 4 * L + L * j, L)], xa[p][:, L * j:L * j + L], ACT.Copy,
                                         accum_out=xsum[:, bass.ds(t * 4 + j, 1)]).then_inc(x_kept, 1)
                wait(act, q_done, 2 * t + 1)
                wait(act, norm_done, 2 * t - 1)
                nc.scalar.activation(sq[0][:, :], q_all[:, bass.ds(t * 8 * D, 4 * D)], ACT.Square).then_inc(sq_done[0], 1)
                for i in range(2):
                    act.wait_ge(k_ready, 2 * t + i + 1)
                    nc.scalar.activation(k_all[:, bass.ds(t * 4 * L + 2 * L * i, 2 * L)], k_bank[i][:, 0:2 * L], ACT.Identity,
                                         bias=cols[:, COLS.index("k_b"):COLS.index("k_b") + 1]).then_inc(k_done, 1)

            def slot_again(h, p):
                t, _, _ = shift(h, p, 0)
                for i in range(2):
                    act.wait_ge(v_ready, 2 * t + i + 1)
                    nc.scalar.activation(v_all[:, bass.ds(t * 8 * D + 4 * D * i, 4 * D)], v_bank[i][0:LH, :], ACT.Copy).then_inc(v_done, 1)

            steps(act, slot, 0, 4, NQ - 1, NQ - 1)
            steps(act, slot_again, 0, 4, NQ - 1, NQ - 1)

        @block.gpsimd
        def _(pool):
            def slot(h, p):
                t, _, _ = shift(h, p, 0)
                pool.wait_ge(q_done, 2 * t + 2)
                wait(pool, norm_done, 2 * t)
                q = q_all[:, bass.ds(t * 8 * D + 4 * D, 4 * D)]
                nc.gpsimd.tensor_tensor(sq[1][:, :], q, q, ALU.mult).then_inc(sq_done[1], 1)
                pool.wait_ge(x_kept, 4 * t + 4)
                nc.gpsimd.tensor_scalar(xneg[:, bass.ds(t * 4, 4)], xsum[:, bass.ds(t * 4, 4)], -1.0 / L, None, ALU.mult).then_inc(xneg_done, 1)
                x4 = x_all[:, bass.ds(t * 4 * L, 4 * L)].rearrange("p (b l) -> p b l", b=4)
                pool.wait_ge(xneg_done, t + 1)
                nc.gpsimd.tensor_tensor(x4, x4, xneg[:, bass.ds(t * 4, 4)].unsqueeze(2).to_broadcast([128, 4, L]),
                                        ALU.add).then_inc(xc_done, 1)

            steps(pool, slot, 0, 4, NQ - 1, NQ - 1)

        @block.tensor
        def _(pe):
            pe.wait_ge(params_in[0], 16)

            def slot(h, p):
                t, half, _ = shift(h, p, 0)
                pe.wait_ge(x_in[p], 16 * half + 16)
                for i in range(2):
                    wait(pe, q_done, 2 * t + i - 1)
                    for j in range(4):
                        last = nc.tensor.matmul(q_bank[i][0:LH, D * j:D * j + D], xa[p][:, 2 * L * i + LH * j:2 * L * i + LH * j + LH],
                                                w[:, WEIGHT["q"]], start=True, stop=True)
                    last.then_inc(q_ready, 1)
                for i in range(2):
                    wait(pe, k_done, 2 * t + i - 1)
                    nc.tensor.matmul(k_bank[i][:, 0:2 * L], w[:, WEIGHT["k"]], xa[p][:, 2 * L * i:2 * L * i + 2 * L],
                                     start=True, stop=True).then_inc(k_ready, 1)
                if t == NQ // 2:
                    pe.wait_ge(params_in[2], 16)
                    norms_to_rows(0)

            def slot_again(h, p):
                t, _, _ = shift(h, p, 0)
                if isinstance(t, int) and t == 2:
                    norms_to_rows(1)
                    pe.wait_ge(x_kept, B)
                    pe.wait_ge(q_done, 2 * NQ)
                    nc.tensor.matmul(q_bank[0][:, 0:B], w[:, WEIGHT["v"]], xsum[:, :], start=True, stop=True).then_inc(mean_ready, 1)
                pe.wait_ge(xc_done, t + 1)
                for i in range(2):
                    wait(pe, v_done, 2 * t + i - 1)
                    for j in range(4):
                        last = nc.tensor.matmul(v_bank[i][0:LH, D * j:D * j + D], x_all[:, bass.ds(t * 4 * L + 2 * L * i + LH * j, LH)],
                                                w[:, WEIGHT["v"]], start=True, stop=True)
                    last.then_inc(v_ready, 1)

            def norms_to_rows(g):
                pe.wait_ge(norm_done, NQ * g + NQ)
                for lt in range(2):
                    last = nc.tensor.transpose(n_bank[g][:, LH * lt:LH * lt + LH],
                                               norm_all[:, lt, 16 * g:16 * g + 16, :].rearrange("p b h -> p (b h)"),
                                               ident[0:LH, 0:LH])
                last.then_inc(norm_t_ready, 1)

            for t in range(NQ):
                slot(t // 2, t % 2)
            steps(pe, slot_again, 0, 4, NQ - 1, NQ - 1)
            for g in range(2):
                pe.wait_ge(key_ready, g + 1)
                for lt in range(2):
                    last = nc.tensor.transpose(n_bank[g][0:LH, D * lt:D * lt + D], key[g][:, LH * lt:LH * lt + LH], ident)
                last.then_inc(key_t_ready, 1)

        @block.vector
        def _(dve):
            nc.vector.memset(zeros[:, :], 0.0).then_inc(setup, 1)
            for g in range(2):
                nc.vector.memset(work[g][0][:, L:W], -2.0).then_inc(setup, 1)
            dve.wait_ge(params_in[1], 16)

            chain = [0, 0]

            def link(g, ins):
                chain[g] += 1
                ins.then_inc(select[g], 1)

            rounds = (KTOP + 7) // 8

            def rows_in(g):
                dve.wait_ge(norm_t_ready, g + 1)
                link(g, nc.vector.tensor_copy(work[g][0][:, 0:L], n_bank[g][:, 0:L]))

            def largest(g, r):
                dve.wait_ge(select[g], chain[g])
                link(g, nc.vector.max(top8[g][:, :], work[g][r % 2][:, 0:L]))
                if r == rounds - 1:
                    dve.wait_ge(select[g], chain[g])
                    link(g, nc.vector.memset(top8[g][:, KTOP - 8 * r:8], -2.0))

            def strike(g, r):
                dve.wait_ge(select[g], chain[g])
                link(g, nc.vector.match_replace(work[g][(r + 1) % 2][:, :], top8[g][:, :], work[g][r % 2][:, :], -1.0))

            def mark_chosen(g):
                dve.wait_ge(select[g], chain[g])
                link(g, nc.vector.tensor_scalar(chosen[g][:, :], work[g][rounds % 2][:, 0:L], -1.0, None, ALU.is_equal))

            def count_chosen(g):
                dve.wait_ge(select[g], chain[g])
                link(g, nc.vector.tensor_tensor_scan(prefix[g][:, :], chosen[g][:, :], zeros[:, :], 0.0, ALU.add, ALU.add))

            def keep_counts(g):
                dve.wait_ge(select[g], chain[g])
                link(g, nc.vector.tensor_tensor(key[g][:, :], prefix[g][:, :], chosen[g][:, :], ALU.mult))

            def hand_over_key(g):
                dve.wait_ge(select[g], chain[g])
                nc.vector.tensor_copy(key16[g][:, :], key[g][:, :]).then_inc(key_ready, 1)

            def norms(n):
                dve.wait_ge(sq_done[n % 2], n // 2 + 1)
                nc.vector.reduce_sum(norm_all[:, :, 2 * n:2 * n + 2, :].rearrange("p l b h -> p b l h"),
                                     sq[n % 2][:, :].rearrange("p (b l h d) -> p b l h d", b=2, l=2, h=H),
                                     axis=AX).then_inc(norm_done, 1)

            for n in range(NPAIR):
                r = n - (NPAIR // 2 + 2)
                dve.wait_ge(q_ready, n + 1)
                nc.vector.tensor_tensor(q_all[:, 4 * D * n:4 * D * n + 4 * D].rearrange("p (a b) -> p a b", b=D),
                                        q_bank[n % 2][0:LH, :].rearrange("p (a b) -> p a b", b=D),
                                        rows[0:LH, RWS.index("q_b"):RWS.index("q_b") + 1, :].to_broadcast([LH, 4, D]),
                                        ALU.add).then_inc(q_done, 1)
                if r >= 0:
                    largest(0, r)
                if n >= 1:
                    norms(n - 1)
                if r == -1:
                    dve.wait_ge(setup, 3)
                    rows_in(0)
                if r >= 0:
                    strike(0, r)
            norms(NPAIR - 1)
            for r in range(NPAIR // 2 - 2, rounds):
                largest(0, r)
                strike(0, r)
            rows_in(1)
            for r in range(rounds):
                largest(1, r)
                if r == 0:
                    mark_chosen(0)
                if r == 1:
                    count_chosen(0)
                if r == 2:
                    keep_counts(0)
                if r == 3:
                    hand_over_key(0)
                strike(1, r)
            mark_chosen(1)
            count_chosen(1)
            keep_counts(1)
            hand_over_key(1)
            dve.wait_ge(mean_ready, 1)
            dve.wait_ge(params_in[3], 16)
            nc.vector.tensor_scalar(meanv[:, :], q_bank[0][:, 0:B], 1.0 / L, cols[:, COLS.index("v_b"):COLS.index("v_b") + 1],
                                    ALU.mult, ALU.add)
            for g in range(2):
                dve.wait_ge(key_t_ready, g + 1)
                nc.vector.tensor_copy(key_all[:, :, 16 * g:16 * g + 16, :],
                                      n_bank[g][0:LH, 0:2 * D].rearrange("p (l b h) -> p l b h", l=2, h=H)).then_inc(key_t_done, 1)


def topk_attention(S):
    nc, c, banks = (S[k] for k in ("nc", "c", "banks"))
    q_all, k_all, v_all, key_all, meanv, attn_all = (S[k] for k in ("q_all", "k_all", "v_all", "key_all", "meanv", "attn_all"))
    with ExitStack() as ctx:
        def sb(name, shape, dt=F32):
            return ctx.enter_context(nc.sbuf_tensor(name, shape, dt))

        def sem(name):
            return ctx.enter_context(nc.semaphore(name))

        def pair(name, shape, dt=F32):
            return [sb(f"{name}{p}", shape, dt) for p in range(2)]

        q1, k1 = S["q1"], S["k1"]
        v1 = pair("v1_", [LH, 2, D])
        keyb = pair("keyb_", [ROWS, HC, L], BF16)
        pick = pair("pick_", [LH, 2, KTOP, H])
        put = pair("put_", [ROWS, HC, L])
        qsel = pair("qsel_", [128, HC, ROWS])
        negmax = pair("negmax_", [ROWS, HC])
        rowsum = pair("rowsum_", [ROWS, HC])
        rinv = pair("rinv_", [ROWS, HC])
        probs = pair("probs_", [ROWS, HC, L])
        probsT = sb("probsT", [LH, 2, HC, ROWS])
        oT = sb("oT", [128, ROWS])
        gate = sb("gate_pool", [1, 1])
        osel = pair("osel_", [ROWS, HC, CW])

        q_in, k_in = S["q1_in"], S["k1_in"]
        v_in, key_in = ([sem(f"a_{k}_in{p}") for p in range(2)] for k in ("v", "key"))
        pick_done, gathered, qsel_done = sem("a_pick_done"), sem("a_gathered"), sem("a_qsel_done")
        scores0, scores1, max_done, exp_done = sem("a_scores0"), sem("a_scores1"), sem("a_max_done"), sem("a_exp_done")
        rinv_done, pT_ready, pT0_done, pT1_done = sem("a_rinv_done"), sem("a_pT_ready"), sem("a_pT0_done"), sem("a_pT1_done")
        pv_ready, oT_done, o_ready, osel_done = sem("a_pv_ready"), sem("a_oT_done"), sem("a_o_ready"), sem("a_osel_done")
        put_done, scattered, attn_done = sem("a_put_done"), sem("a_scattered"), sem("a_attn_done")

        s_bank, t_bank, ot_bank, g_bank, o_bank, a_bank = banks[0:2], banks[2:4], banks[4], banks[5], banks[6], banks[7]
        ident = c[:, CONST["ident"]]
        RUN = (-2, 4, B - 3, B + 1)
        block = ctx.enter_context(nc.Block())

        @block.sync
        def _(sp):
            def slot(h, p):
                v, _, _ = shift(h, p, 0)
                vn, _, pn = shift(h, p, 1)
                vm, _, pm = shift(h, p, -1)
                if within(v, 0, B):
                    wait(sp, scores0, v - 1)
                    wait(sp, scores1, v - 1)
                if within(v, 1, B - 1):
                    wait(sp, gathered, v)
                    sp.dma_start(q1[pn][:, :, :].rearrange("p a b -> p (a b)"),
                                 q_all[:, bass.ds(vn * 2 * D, 2 * D)]).then_inc(q_in[pn], 16)
                if within(v, 1, B):
                    sp.dma_start(k1[p][:, :], k_all[:, bass.ds(v * L, L)]).then_inc(k_in[p], 16)
                wait(sp, pv_ready, v - 2)
                if within(v, 0, B):
                    wait(sp, put_done, v - 1)
                    for hh in range(2):
                        src = S["key_dram"].rearrange("(b c hh) l -> b hh c l", c=HC, hh=2)[bass.ds(v, 1), hh, :, :]
                        sp.dma_start(keyb[p][hh:ROWS:2, :, :], src.to_broadcast([KTOP, HC, L])).then_inc(key_in[p], 16)
                if within(v, 1, B + 1):
                    sp.dma_start(v1[pm][:, :, :].rearrange("p a b -> p (a b)"),
                                 v_all[:, bass.ds(vm * 2 * D, 2 * D)]).then_inc(v_in[pm], 16)

            steps(sp, slot, 0, 4, B - 3, B)
            for t in range(2):
                sp.dma_start(S["xt"][t][:, :, :], S["xtok"][:, 4 * t:4 * t + 4, :]).then_inc(S["xt_in"][t], 16)
                sp.wait_ge(attn_done, 2 * t + 2)
                sp.dma_start(S["attn"][t][:, :], attn_all[:, 2 * L * t:2 * L * t + 2 * L]).then_inc(S["attn_in"][t], 16)

        @block.gpsimd
        def _(pool):
            def slot(h, p):
                u, half, _ = shift(h, p, 0)
                pool.wait_ge(key_in[p], 32 * half + 32)
                wait(pool, scattered, u - 1)
                wait(pool, put_done, u)
                nc.gpsimd.tensor_tensor(gate[:, :], c[0:1, 0:1], c[0:1, 0:1], ALU.add)
                nc.gpsimd.tensor_scalar(put[p][:, :, :], keyb[p][:, :, :], c[0:ROWS, CONST["sidx"]], None,
                                        ALU.is_equal).then_inc(put_done, 1)

            steps(pool, slot, 0, 4, B - 1, B - 1)

        @block.tensor
        def _(pe):
            def slot(h, p):
                u, hu, _ = shift(h, p, 0)
                u1, h1, p1 = shift(h, p, 1)
                um, hm, pm = shift(h, p, -1)
                if within(u, 0, B):
                    pe.wait_ge(qsel_done, u + 1)
                    pe.wait_ge(k_in[p], 16 * hu + 16)
                    wait(pe, exp_done, 4 * u)
                    for ch in range(HC):
                        r, cc = ch // 2, ch % 2
                        ins = nc.tensor.matmul(s_bank[r][0:ROWS, L * cc:L * cc + L], qsel[p][:, ch, :], k1[p][:, :], start=True, stop=True)
                        if cc:
                            ins.then_inc((scores0, scores1)[r], 1)
                if within(u, 2, B + 2):
                    wait(pe, oT_done, u - 1)
                    wait(pe, osel_done, u - 2)
                    nc.tensor.transpose(ot_bank[0:ROWS, 0:128], oT[:, :], ident).then_inc(o_ready, 1)
                if within(u, 1, B + 1):
                    wait(pe, exp_done, 4 * u)
                    wait(pe, pT0_done, u - 1)
                    wait(pe, pT1_done, u - 1)
                    for lt in range(2):
                        for ch in range(HC):
                            ins = nc.tensor.transpose(t_bank[lt][0:LH, ROWS * ch:ROWS * ch + ROWS],
                                                      probs[pm][:, ch, LH * lt:LH * lt + LH], ident[0:ROWS, 0:ROWS])
                        ins.then_inc(pT_ready, 1)
                if within(u, -1, B - 1):
                    pe.wait_ge(q_in[p1], 16 * h1 + 16)
                    pe.wait_ge(pick_done, u + 2)
                    wait(pe, qsel_done, u + 1)
                    for lt in range(2):
                        for ch in range(HC):
                            ins = nc.tensor.matmul(g_bank[CW * ch:CW * ch + CW, 0:ROWS], q1[p1][:, lt, CW * ch:CW * ch + CW],
                                                   pick[p1][:, lt, :, 2 * ch:2 * ch + 2], start=lt == 0, stop=lt == 1)
                    ins.then_inc(gathered, 1)
                if within(u, 2, B + 2):
                    wait(pe, osel_done, u - 1)
                    wait(pe, put_done, u - 1)
                    wait(pe, attn_done, u - 2)
                    for ch in range(HC):
                        ins = nc.tensor.matmul(a_bank[CW * ch:CW * ch + CW, 0:L], osel[p][:, ch, :], put[p][:, ch, :],
                                               start=True, stop=True)
                    ins.then_inc(scattered, 1)
                if within(u, 1, B + 1):
                    pe.wait_ge(pT0_done, u)
                    pe.wait_ge(pT1_done, u)
                    pe.wait_ge(v_in[pm], 16 * hm + 16)
                    wait(pe, oT_done, u - 1)
                    for lt in range(2):
                        for ch in range(HC):
                            ins = nc.tensor.matmul(o_bank[CW * ch:CW * ch + CW, 0:ROWS], v1[pm][:, lt, CW * ch:CW * ch + CW],
                                                   probsT[:, lt, ch, :], start=lt == 0, stop=lt == 1)
                    ins.then_inc(pv_ready, 1)

            steps(pe, slot, *RUN)

        @block.vector
        def _(dve):
            def slot(h, p):
                u, _, _ = shift(h, p, 0)
                u2, _, p2 = shift(h, p, 2)
                _, _, p1 = shift(h, p, 1)
                _, _, pm = shift(h, p, -1)
                if within(u, 0, B):
                    for r in range(2):
                        dve.wait_ge((scores0, scores1)[r], u + 1)
                        nc.vector.tensor_reduce(negmax[p][:, 2 * r:2 * r + 2],
                                                s_bank[r][0:ROWS, 0:2 * L].rearrange("p (c l) -> p c l", c=2),
                                                AX, ALU.max, negate=True).then_inc(max_done, 1)
                if within(u, 1, B + 1):
                    dve.wait_ge(exp_done, 4 * u)
                    wait(dve, osel_done, u - 2)
                    nc.vector.reciprocal(rinv[pm][:, :], rowsum[pm][:, :]).then_inc(rinv_done, 1)
                if within(u, 2, B + 2):
                    dve.wait_ge(o_ready, u - 1)
                    dve.wait_ge(rinv_done, u - 1)
                    wait(dve, scattered, u - 3)
                    nc.vector.tensor_tensor(osel[p][:, :, :], ot_bank[0:ROWS, 0:128].rearrange("p (c f) -> p c f", c=HC),
                                            rinv[p][:, :].unsqueeze(2).to_broadcast([ROWS, HC, CW]), ALU.mult).then_inc(osel_done, 1)
                if within(u, 1, B + 1):
                    dve.wait_ge(pT_ready, 2 * u - 1)
                    wait(dve, pv_ready, u - 1)
                    nc.vector.tensor_copy(probsT[:, 0, :, :].rearrange("p c s -> p (c s)"), t_bank[0][0:LH, 0:HC * ROWS]).then_inc(pT0_done, 1)
                if within(u, -1, B - 1):
                    dve.wait_ge(gathered, u + 2)
                    wait(dve, scores1, u)
                    nc.vector.tensor_tensor(qsel[p1][:, :, :], g_bank[:, 0:ROWS].unsqueeze(1).to_broadcast([128, HC, ROWS]),
                                            c[:, CONST["qmask"]].rearrange("p (c s) -> p c s", c=HC), ALU.mult).then_inc(qsel_done, 1)
                if within(u, -2, B - 2):
                    wait(dve, gathered, u + 1)
                    nc.vector.tensor_tensor(pick[p2][:, :, :, :],
                                            c[0:LH, CONST["siota"]].rearrange("p (s h) -> p s h", h=H).unsqueeze(1).to_broadcast([LH, 2, KTOP, H]),
                                            key_all[:, :, bass.ds(u2, 1), :].to_broadcast([LH, 2, KTOP, H]),
                                            ALU.is_equal).then_inc(pick_done, 1)
                if within(u, 1, B + 1):
                    dve.wait_ge(pv_ready, u)
                    wait(dve, o_ready, u - 1)
                    nc.vector.tensor_tensor(oT[:, :], o_bank[:, 0:ROWS], c[:, CONST["omask"]], ALU.mult).then_inc(oT_done, 1)

            steps(dve, slot, *RUN)

        @block.scalar
        def _(act):
            def slot(h, p):
                u, _, _ = shift(h, p, 0)
                um2, _, _ = shift(h, p, -2)
                for ch in range(HC):
                    if within(u, 0, B):
                        if ch == 0:
                            wait(act, rinv_done, u - 1)
                            wait(act, pT_ready, 2 * u - 2)
                        if ch % 2 == 0:
                            act.wait_ge(max_done, 2 * u + 1 + ch // 2)
                        nc.scalar.activation(probs[p][:, ch, :], s_bank[ch // 2][0:ROWS, L * (ch % 2):L * (ch % 2) + L], ACT.Exp,
                                             bias=negmax[p][:, ch:ch + 1], accum_out=rowsum[p][:, ch:ch + 1]).then_inc(exp_done, 1)
                    if ch == 1 and within(u, 1, B + 1):
                        act.wait_ge(pT_ready, 2 * u)
                        wait(act, pv_ready, u - 1)
                        nc.scalar.activation(probsT[:, 1, :, :].rearrange("p c s -> p (c s)"), t_bank[1][0:LH, 0:HC * ROWS], ACT.Copy).then_inc(pT1_done, 1)
                if within(u, 2, B + 2):
                    act.wait_ge(scattered, u - 1)
                    nc.scalar.activation(attn_all[:, bass.ds(um2 * L, L)], a_bank[:, 0:L], ACT.Identity,
                                         bias=meanv[:, bass.ds(um2, 1)]).then_inc(attn_done, 1)

            steps(act, slot, *RUN)


def ffn_and_window(S):
    nc, w, c, cols, rows, banks = (S[k] for k in ("nc", "w", "c", "cols", "rows", "banks"))
    attn_all, n3T_all, z_all = (S[k] for k in ("attn_all", "n3T_all", "z_all"))
    with ExitStack() as ctx:
        def sb(name, shape, dt=F32):
            return ctx.enter_context(nc.sbuf_tensor(name, shape, dt))

        def sem(name):
            return ctx.enter_context(nc.semaphore(name))

        def pair(name, shape, dt=F32):
            return [sb(f"{name}{p}", shape, dt) for p in range(2)]

        attn, xt = S["attn"], S["xt"]
        ao = sb("ao", [LH, 4, D])
        aob = pair("aob_", [LH, 4, D])
        xb = pair("xb_", [LH, 4, D])
        t1 = sb("t1", [LH, 4, D])
        n1 = sb("n1", [LH, 4, D])
        hb = pair("hb_", [LH, 4, D])
        h1T = pair("h1T_", [128, 2 * L])
        hid = sb("hid", [128, 4, 2 * L])
        t2 = sb("t2", [LH, 4, D])
        n2 = sb("n2", [LH, 4, D])
        fused = sb("fused", [LH, 4, D])
        yin = sb("yin", [128, 2, L + 2])
        ymax = sb("ymax", [128, 2 * LH])
        h0T = sb("h0T", [128, 2 * LH])
        h0 = sb("h0", [LH, 2, D])
        n3 = sb("n3", [LH, 2, D])
        gate = sb("gate", [1, 1])
        table_of = sb("table_of", [1, 3])
        hbias = sb("hbias", [LH, D])
        obias = sb("obias", [LH, D])
        st = [sb(f"st{i}", [LH, n, 6]) for i, n in enumerate((4, 4, 2))]
        mv = [sb(f"mv{i}", [LH, n, 2]) for i, n in enumerate((4, 4, 2))]
        sd = [sb(f"sd{i}", [LH, n]) for i, n in enumerate((4, 4, 2))]
        rstd = [sb(f"rstd{i}", [LH, n]) for i, n in enumerate((4, 4, 2))]

        at_in, x_in = S["attn_in"], S["xt_in"]
        ready = sem("f_ready")
        ao_ready, ao_done, t1_done, aob_done = sem("f_ao_ready"), sem("f_ao_done"), sem("f_t1_done"), sem("f_aob_done")
        bias_done, xb_done = sem("f_bias_done"), sem("f_xb_done")
        bn, aggr, sd_done, rs_done, norm = ([sem(f"f_{k}{i}") for i in range(3)] for k in ("bn", "aggr", "sd", "rstd", "norm"))
        n1T_ready, h1T_done, hb_mul, hb_done = sem("f_n1T_ready"), sem("f_h1T_done"), sem("f_hb_mul"), sem("f_hb_done")
        f1_ready, hid_done, f2_ready, t2_done = sem("f_f1_ready"), sem("f_hid_done"), sem("f_f2_ready"), sem("f_t2_done")
        fu_mul, fused_done, fT_ready, yin_done = sem("f_fu_mul"), sem("f_fused_done"), sem("f_fT_ready"), sem("f_yin_done")
        conv_ready, max_done, h0T_done, h0_ready = sem("f_conv_ready"), sem("f_max_done"), sem("f_h0T_done"), sem("f_h0_ready")
        h0_done, h0b_done, n3T_ready, n3T_done = sem("f_h0_done"), sem("f_h0b_done"), sem("f_n3T_ready"), sem("f_n3T_done")

        f_bank, ao_bank, f2_bank, n1_bank, fu_bank, cv_bank, h_bank = banks[0:2], banks[2], banks[3], banks[4], banks[5], banks[6], banks[7]
        ident = c[:, CONST["ident"]]
        NP = NPAIR

        def row(name, n):
            i = RWS.index(name)
            return rows[0:LH, i:i + 1, :].to_broadcast([LH, n, D])

        def col(name):
            i = COLS.index(name)
            return cols[:, i:i + 1]

        def tok(bank, n=4):
            return bank[0:LH, 0:n * D].rearrange("p (a b) -> p a b", b=D)

        wn3 = pair("n3T_", [128, LH])
        qT = pair("wqT_", [128, LH])
        kT = sb("wkT", [128, LH])
        kbd = pair("kbd_", [128, 4, LH])
        vo = pair("vo_", [LH, H, CW])
        negmax = pair("wmax_", [LH, H])
        probs = pair("wprobs_", [LH, H, LH])
        probsT = sb("wprobsT", [LH, H, LH])
        oT = sb("woT", [128, 2 * LH])
        rinv = sb("wrinv", [LH, H])
        otok = sb("otok", [LH, D])
        oF = sb("oF", [128, LH])
        wgate = sb("wgate", [1, 2])
        zst = sb("st_all", [LH, B, 6])
        mean = sb("mean_z", [LH, B])
        var = sb("var_z", [LH, B])
        tmp = sb("tmp_z", [LH, B])
        sdz = sb("sd_z", [LH, B])
        rs = sb("rstd_z", [LH, B])
        gain = sb("gain_z", [LH, B])
        offs = sb("offs_z", [LH, B])
        o = sb("o_all", [LH, B, D])

        n_in = [sem(f"w_n_in{p}") for p in range(2)]
        ones_in, kT_done, qT_done, kbd_done, v_done = sem("w_ready"), sem("w_kT_done"), sem("w_qT_done"), sem("w_kbd_done"), sem("w_v_done")
        qk_ready, v_ready, scores, min_done, exp_done = sem("w_qk_ready"), sem("w_v_ready"), sem("w_scores"), sem("w_max_done"), sem("w_exp_done")
        pT_ready, pT0_done, pT1_done = sem("w_pT_ready"), sem("w_pT0_done"), sem("w_pT1_done")
        pv_ready, oT_done, otok_ready, rinv_done, otok_done = sem("w_pv_ready"), sem("w_oT_done"), sem("w_otok_ready"), sem("w_rinv_done"), sem("w_otok_done")
        oF_ready, oF_done, proj_ready, z_done = sem("w_oF_ready"), sem("w_oF_done"), sem("w_proj_ready"), sem("w_z_done")
        stat, chain, root_done, out_done, stored = sem("w_stat"), sem("w_chain"), sem("w_root_done"), {who: sem(f"w_out{who}") for who in "PDA"}, sem("w_stored")

        s_bank, t_bank, q_bank, o_bank, a_bank, of_bank = banks[0:2], banks[2:4], banks[4], banks[5], banks[6], banks[7]
        def in_turn(eng, ffn, window):
            steps(eng, ffn, -2, 4, NP - 3, NP - 1)
            first = ((ffn, NP), (window, -1)) if eng is nc.gpsimd else ((window, -1), (ffn, NP))
            for slot, u in first + ((window, 0), (window, 1), (ffn, NP + 1)):
                slot(u // 2, u % 2)
            steps(eng, window, 2, 4, B - 3, B - 1)

        def at(window, u):
            window(u // 2, u % 2)

        EARLY = B - 4
        owner = "PDAPDAPD" * (B // 8)

        def own(who, lo, hi):
            return [b for b in range(lo, hi) if owner[b] == who]

        block = ctx.enter_context(nc.Block())

        @block.sync
        def _(sp):
            def ffn(h, p):
                t, _, _ = shift(h, p, 0)
                wait(sp, ao_ready, t - 1)
                sp.dma_start(attn[p][:, :], attn_all[:, bass.ds(t * 2 * L, 2 * L)]).then_inc(at_in[p], 16)
                wait(sp, xb_done, t - 1)
                sp.dma_start(xt[p][:, :, :], S["xtok"][:, bass.ds(t * 4, 4), :]).then_inc(x_in[p], 16)

            steps(sp, ffn, 2, 2, NP - 1, NP - 1)

            def window(h, p):
                u, _, _ = shift(h, p, 0)
                if isinstance(u, int) and u < 4:
                    sp.wait_ge(n3T_done, u // 2 + 1 if u < 3 else NP)
                wait(sp, v_ready, u - 1)
                sp.dma_start(wn3[p][:, :], n3T_all[:, bass.ds(u * LH, LH)]).then_inc(n_in[p], 16)

            steps(sp, window, 0, 4, B - 1, B - 1)
            for g in range(4):
                for who in "PDA":
                    sp.wait_ge(out_done[who], len(own(who, 0, 8 * g + 8)))
                sp.dma_start(S["out"].rearrange("b l d -> l b d")[:, 8 * g:8 * g + 8, :], o[:, 8 * g:8 * g + 8, :]).then_inc(stored, 16)
            sp.wait_ge(stored, 64)

        @block.tensor
        def _(pe):
            def ffn(h, p):
                t, _, _ = shift(h, p, 0)
                _, hn, pn = shift(h, p, 1)
                if within(t, -1, NP - 1):
                    pe.wait_ge(at_in[pn], 16 * hn + 16)
                    wait(pe, ao_done, t + 1)
                    for j in range(4):
                        ins = nc.tensor.matmul(ao_bank[0:LH, D * j:D * j + D], attn[pn][:, LH * j:LH * j + LH], w[:, WEIGHT["o"]],
                                               start=True, stop=True)
                    ins.then_inc(ao_ready, 1)
                if within(t, 0, NP):
                    pe.wait_ge(h1T_done, t + 1)
                    for k in range(4):
                        wait(pe, hid_done, 4 * t + k - 1)
                        nc.tensor.matmul(f_bank[k % 2][:, 0:2 * L], w[:, WEIGHT["f1"].start + 128 * k:WEIGHT["f1"].start + 128 * k + 128],
                                         h1T[p][:, :], start=True, stop=True).then_inc(f1_ready, 1)
                if within(t, 2, NP + 2):
                    pe.wait_ge(h0T_done, t - 1)
                    wait(pe, n3T_done, t - 2)
                    for b in range(2):
                        ins = nc.tensor.transpose(h_bank[0:LH, D * b:D * b + D], h0T[:, LH * b:LH * b + LH], ident)
                    ins.then_inc(h0_ready, 1)
                if within(t, 1, NP + 1):
                    pe.wait_ge(fused_done, t)
                    wait(pe, yin_done, t - 1)
                    for j in range(4):
                        ins = nc.tensor.transpose(fu_bank[:, LH * j:LH * j + LH], fused[:, j, :], ident[0:LH, 0:LH])
                    ins.then_inc(fT_ready, 1)
                if within(t, 0, NP):
                    wait(pe, t2_done, t)
                    for j in range(4):
                        for k in range(4):
                            if j == 0:
                                pe.wait_ge(hid_done, 4 * t + k + 1)
                            ins = nc.tensor.matmul(f2_bank[0:LH, D * j:D * j + D], hid[:, k, LH * j:LH * j + LH],
                                                   w[:, WEIGHT["f2"].start + D * k:WEIGHT["f2"].start + D * k + D],
                                                   start=k == 0, stop=k == 3)
                    ins.then_inc(f2_ready, 1)
                if within(t, 2, NP + 2):
                    pe.wait_ge(norm[2], t - 1)
                    for b in range(2):
                        ins = nc.tensor.transpose(h_bank[:, 256 + LH * b:256 + LH * b + LH], n3[:, b, :], ident[0:LH, 0:LH])
                    ins.then_inc(n3T_ready, 1)
                if within(t, -1, NP - 1):
                    pe.wait_ge(norm[0], t + 2)
                    wait(pe, h1T_done, t + 1)
                    for j in range(4):
                        ins = nc.tensor.transpose(n1_bank[:, LH * j:LH * j + LH], n1[:, j, :], ident[0:LH, 0:LH])
                    ins.then_inc(n1T_ready, 1)
                if within(t, 1, NP + 1):
                    pe.wait_ge(yin_done, t)
                    wait(pe, max_done, t - 1)
                    for k in range(3):
                        ins = nc.tensor.matmul(cv_bank[:, 0:2 * L].rearrange("p (b l) -> p b l", b=2),
                                               w[:, WEIGHT["conv"].start + D * k:WEIGHT["conv"].start + D * k + D],
                                               yin[:, :, k:k + L], start=k == 0, stop=k == 2)
                    ins.then_inc(conv_ready, 1)

            pe.wait_ge(ones_in, 2)

            def window(h, p):
                u, hu, _ = shift(h, p, 0)
                un, _, _ = shift(h, p, 1)
                _, _, pm = shift(h, p, -1)

                def scores_of(r):
                    if r == 0:
                        pe.wait_ge(qT_done, u + 1)
                        pe.wait_ge(kbd_done, u + 1)
                    wait(pe, exp_done, 2 * u - 1 + r)
                    nc.tensor.matmul(s_bank[r][0:LH, 0:4 * LH], qT[p][64 * r:64 * r + 64, :],
                                     kbd[p][64 * r:64 * r + 64, :, :].rearrange("p h l -> p (h l)"), start=True, stop=True).then_inc(scores, 1)

                def turn(r):
                    wait(pe, (pT0_done, pT1_done)[r], u - 1)
                    pe.wait_ge(exp_done, 2 * u - 1 + r)
                    for j in range(4):
                        ins = nc.tensor.transpose(t_bank[r][0:LH, LH * j:LH * j + LH], probs[pm][:, 4 * r + j, :], ident[0:LH, 0:LH])
                    ins.then_inc(pT_ready, 1)

                if isinstance(u, int):
                    for first, done, count in ((-1, h1T_done, NP), (0, hid_done, 4 * NP), (0, yin_done, NP), (1, ao_done, NP),
                                               (1, t2_done, NP), (2, max_done, NP), (3, n3T_done, NP)):
                        if u == first:
                            pe.wait_ge(done, count)
                    if u < 3:
                        pe.wait_ge(n3T_done, un // 2 + 1)
                if within(u, 0, B):
                    scores_of(0)
                if within(u, -1, B - 1):
                    wait(pe, qT_done, u + 1)
                    for i, name in enumerate(("wk", "wq")):
                        ins = nc.tensor.matmul(q_bank[:, 128 * i:128 * i + LH], w[:, WEIGHT[name]], n3T_all[:, bass.ds(un * LH, LH)], start=True, stop=True)
                    ins.then_inc(qk_ready, 1)
                if within(u, 3, B + 3):
                    pe.wait_ge(otok_done, u - 2)
                    wait(pe, z_done, u - 3)
                    nc.tensor.transpose(of_bank[:, 0:LH], otok[:, :], ident[0:LH, 0:LH]).then_inc(oF_ready, 1)
                if within(u, 1, B + 1):
                    turn(0)
                if within(u, 0, B):
                    scores_of(1)
                if within(u, 3, B + 3):
                    pe.wait_ge(oF_done, u - 2)
                    nc.tensor.matmul(of_bank[0:LH, 256:256 + D], oF[:, :], w[:, WEIGHT["wp"]], start=True, stop=True).then_inc(proj_ready, 1)
                if within(u, 1, B + 1):
                    turn(1)
                if within(u, 2, B + 2):
                    pe.wait_ge(oT_done, u - 1)
                    wait(pe, otok_done, u - 2)
                    for i in range(2):
                        ins = nc.tensor.transpose(a_bank[0:LH, 128 * i:128 * i + 128], oT[:, LH * i:LH * i + LH], ident)
                    ins.then_inc(otok_ready, 1)
                if within(u, 0, B):
                    pe.wait_ge(n_in[p], 16 * hu + 16)
                    wait(pe, v_done, u)
                    wait(pe, oT_done, u - 1)
                    nc.tensor.matmul(o_bank[0:LH, 256:256 + D], wn3[p][:, :], w[:, WEIGHT["wv"]], start=True, stop=True).then_inc(v_ready, 1)
                if within(u, 1, B + 1):
                    pe.wait_ge(v_done, u)
                    for j in range(H):
                        if j % 4 == 0:
                            pe.wait_ge((pT0_done, pT1_done)[j // 4], u)
                        ins = nc.tensor.matmul(o_bank[CW * (j % 4):CW * (j % 4) + CW, LH * (j // 4):LH * (j // 4) + LH],
                                               vo[pm][:, j, :], probsT[:, j, :], start=True, stop=True)
                    ins.then_inc(pv_ready, 1)

            in_turn(pe, ffn, window)
            for u in range(B, B + 3):
                at(window, u)

        @block.scalar
        def _(act):
            def fetch_table(i, func):
                nc.scalar.activation(table_of[:, i:i + 1], c[0:1, CONST["eps"]], func)

            fetch_table(0, ACT.Sqrt)

            def root(i, count):
                act.wait_ge(aggr[i], count)
                wait(act, rs_done[i], count - 1)
                nc.scalar.activation(sd[i][:, :].unsqueeze(2), mv[i][:, :, 1:2], ACT.Sqrt, bias=c[0:LH, CONST["eps"]]).then_inc(sd_done[i], 1)

            def ffn(h, p):
                t, _, _ = shift(h, p, 0)
                tm2, _, _ = shift(h, p, -2)
                _, _, pn = shift(h, p, 1)
                if within(t, 2, NP + 2):
                    act.wait_ge(max_done, t - 1)
                    wait(act, h0_ready, t - 2)
                    nc.scalar.activation(h0T[:, :], ymax[:, :], ACT.Relu, bias=col("conv_b")).then_inc(h0T_done, 1)
                for k in range(4):
                    if k == 2 and within(t, -1, NP - 1):
                        act.wait_ge(t1_done, t + 2)
                        wait(act, aob_done, t + 1)
                        nc.scalar.activation(ao[:, :, :], tok(ao_bank), ACT.Copy).then_inc(ao_done, 1)
                        root(0, t + 2)
                    if within(t, 0, NP):
                        if k == 0:
                            wait(act, f2_ready, t)
                        act.wait_ge(f1_ready, 4 * t + k + 1)
                        nc.scalar.activation(hid[:, k, :], f_bank[k % 2][:, 0:2 * L], ACT.Relu, bias=col(f"f1_{k}")).then_inc(hid_done, 1)
                if within(t, 2, NP + 2):
                    root(2, t - 1)
                if within(t, 1, NP + 1):
                    act.wait_ge(fT_ready, t)
                    if isinstance(t, int) and t == 2:
                        act.wait_ge(ready, 1)
                    wait(act, conv_ready, t - 1)
                    nc.scalar.activation(yin[:, :, 1:L + 1], fu_bank[:, 0:2 * L].rearrange("p (b l) -> p b l", b=2), ACT.Copy).then_inc(yin_done, 1)
                if within(t, 2, NP + 2):
                    act.wait_ge(n3T_ready, t - 1)
                    nc.scalar.activation(n3T_all[:, bass.ds(tm2 * 2 * LH, 2 * LH)], h_bank[:, 256:256 + 2 * LH], ACT.Copy).then_inc(n3T_done, 1)
                if within(t, -1, NP - 1):
                    act.wait_ge(n1T_ready, t + 2)
                    wait(act, f1_ready, 4 * t)
                    nc.scalar.activation(h1T[pn][:, :], n1_bank[:, 0:2 * L], ACT.Identity, scale=col("ln1_g"), bias=col("ln1_b")).then_inc(h1T_done, 1)
                if within(t, 0, NP):
                    root(1, t + 1)
                if isinstance(t, int) and t >= NP:
                    fetch_table(1 + t - NP, ACT.Exp)

            def window(h, p):
                u, _, _ = shift(h, p, 0)
                _, _, pn = shift(h, p, 1)

                def exponents(r):
                    act.wait_ge(min_done, 2 * u + 1 + r)
                    for j in range(4 * r, 4 * r + 4):
                        ins = nc.scalar.activation(probs[p][:, j, :], s_bank[r][0:LH, LH * (j % 4):LH * (j % 4) + LH], ACT.Exp,
                                                   bias=negmax[p][:, j:j + 1], scale=-1.0)
                    ins.then_inc(exp_done, 1)

                if within(u, -1, B - 1):
                    act.wait_ge(qk_ready, u + 2)
                    wait(act, kbd_done, u + 1)
                    nc.scalar.activation(kT[:, :], q_bank[:, 0:LH], ACT.Identity, bias=col("wk_b")).then_inc(kT_done, 1)
                    wait(act, scores, 2 * u)
                    nc.scalar.activation(qT[pn][:, :], q_bank[:, 128:128 + LH], ACT.Identity, bias=col("wq_b")).then_inc(qT_done, 1)
                if within(u, 3, B + 3):
                    act.wait_ge(oF_ready, u - 2)
                    wait(act, proj_ready, u - 3)
                    nc.scalar.activation(oF[:, :], of_bank[:, 0:LH], ACT.Identity, bias=col("wv_b")).then_inc(oF_done, 1)
                if within(u, 0, B):
                    wait(act, pT_ready, 2 * u - 2)
                    exponents(0)
                if within(u, 1, B + 1):
                    act.wait_ge(pT_ready, 2 * u)
                    wait(act, pv_ready, u - 1)
                    nc.scalar.activation(probsT[:, 4:8, :].rearrange("p h l -> p (h l)"), t_bank[1][0:LH, 0:4 * LH], ACT.Copy).then_inc(pT1_done, 1)
                if within(u, 0, B):
                    exponents(1)
                if within(u, 1, B + 1):
                    act.wait_ge(pv_ready, u)
                    wait(act, otok_ready, u - 1)
                    nc.scalar.activation(oT[:, :], o_bank[:, 0:2 * LH], ACT.Copy).then_inc(oT_done, 1)
                if within(u, 0, B):
                    act.wait_ge(v_ready, u + 1)
                    nc.scalar.activation(vo[p][:, :, 0:HD], o_bank[0:LH, 256:256 + D].rearrange("p (h f) -> p h f", h=H), ACT.Copy).then_inc(v_done, 1)

            def root_z(lo, hi, count):
                act.wait_ge(chain, count)
                nc.scalar.activation(sdz[:, lo:hi], var[:, lo:hi], ACT.Sqrt, bias=c[0:LH, CONST["eps"]]).then_inc(root_done, 1)

            def output(clips, count):
                act.wait_ge(chain, count)
                for b in clips:
                    nc.scalar.activation(o[:, b, :], z_all[:, b, :], ACT.Identity, scale=gain[:, b:b + 1], bias=offs[:, b:b + 1]).then_inc(out_done["A"], 1)

            in_turn(act, ffn, window)
            root_z(0, EARLY, 6)
            at(window, B)
            at(window, B + 1)
            output(own("A", 0, EARLY)[:4], 9)
            at(window, B + 2)
            output(own("A", 0, EARLY)[4:], 9)
            root_z(EARLY, B, 15)
            output(own("A", EARLY, B), 18)

        @block.gpsimd
        def _(pool):
            for dst, one, other in ((hbias, "ln1_b", "f2_b"), (obias, "o_b", "ln2_b")):
                nc.gpsimd.tensor_tensor(dst[:, :], rows[0:LH, RWS.index(one), :], rows[0:LH, RWS.index(other), :], ALU.add).then_inc(bias_done, 1)
            pool.wait_ge(bias_done, 2)

            def ffn(h, p):
                t, _, _ = shift(h, p, 0)
                tm2, _, _ = shift(h, p, -2)
                _, h2, _ = shift(h, p, 2)
                _, _, pn = shift(h, p, 1)
                pm = pn
                if within(t, 1, NP + 1):
                    pool.wait_ge(norm[1], t)
                    wait(pool, fT_ready, t - 1)
                    nc.gpsimd.tensor_tensor(fused[:, :, :], n2[:, :, :], row("ln2_g", 4), ALU.mult).then_inc(fu_mul, 1)
                    pool.wait_ge(fu_mul, t)
                    pool.wait_ge(aob_done, t)
                    nc.gpsimd.tensor_tensor(fused[:, :, :], fused[:, :, :], aob[pm][:, :, :], ALU.add).then_inc(fused_done, 1)
                if within(t, -1, NP - 1):
                    pool.wait_ge(ao_done, t + 2)
                    wait(pool, fused_done, t)
                    nc.gpsimd.tensor_tensor(aob[pn][:, :, :], ao[:, :, :], obias[:, :].unsqueeze(1).to_broadcast([LH, 4, D]), ALU.add).then_inc(aob_done, 1)
                if within(t, -1, NP - 1):
                    pool.wait_ge(norm[0], t + 2)
                    wait(pool, t2_done, t)
                    nc.gpsimd.tensor_tensor(hb[pn][:, :, :], n1[:, :, :], row("ln1_g", 4), ALU.mult).then_inc(hb_mul, 1)
                    pool.wait_ge(hb_mul, t + 2)
                    nc.gpsimd.tensor_tensor(hb[pn][:, :, :], hb[pn][:, :, :], hbias[:, :].unsqueeze(1).to_broadcast([LH, 4, D]), ALU.add).then_inc(hb_done, 1)
                if within(t, 2, NP + 2):
                    pool.wait_ge(h0_done, t - 1)
                    nc.gpsimd.tensor_tensor(z_all[:, bass.ds(tm2 * 2, 2), :], h0[:, :, :], row("wp_b", 2), ALU.add).then_inc(h0b_done, 1)
                if within(t, -2, NP - 2):
                    pool.wait_ge(x_in[p], 16 * h2 + 16)
                    wait(pool, t1_done, t + 1)
                    nc.gpsimd.tensor_tensor(xb[p][:, :, :], xt[p][:, :, :], row("o_b", 4), ALU.add).then_inc(xb_done, 1)

            def window(h, p):
                u, _, _ = shift(h, p, 0)
                _, _, pn = shift(h, p, 1)
                if within(u, -1, B - 1):
                    pool.wait_ge(kT_done, u + 2)
                    wait(pool, scores, 2 * u)
                    nc.gpsimd.tensor_tensor(kbd[pn][:, :, :], kT[:, :].unsqueeze(1).to_broadcast([128, 4, LH]),
                                            c[:, CONST["kmask"]].unsqueeze(2).to_broadcast([128, 4, LH]), ALU.mult).then_inc(kbd_done, 1)

            in_turn(pool, ffn, window)
            for lo, hi, count in ((0, EARLY, 9), (EARLY, B, 18)):
                pool.wait_ge(chain, count)
                for b in own("P", lo, hi):
                    nc.gpsimd.tensor_scalar(o[:, b, :], z_all[:, b, :], gain[:, b:b + 1], offs[:, b:b + 1], ALU.mult, ALU.add).then_inc(out_done["P"], 1)

        @block.vector
        def _(dve):
            nc.vector.memset(yin[:, :, 0:1], 0.0)
            nc.vector.memset(yin[:, :, L + 1:L + 2], 0.0).then_inc(ready, 1)

            def stats(i, src, n, count):
                wait(dve, sd_done[i], count - 1)
                wait(dve, norm[i], count - 1)
                for j in range(n):
                    ins = nc.vector.bn_stats(st[i][:, j, :], src[:, j, :])
                ins.then_inc(bn[i], 1)
                dve.wait_ge(bn[i], count)
                nc.vector.memset(gate[:, :], 0.0)
                for j in range(n):
                    ins = nc.vector.bn_aggr(mv[i][:, j, :], st[i][:, j, :])
                ins.then_inc(aggr[i], 1)

            def normalise(i, dst, src, n, count):
                dve.wait_ge(sd_done[i], count)
                nc.vector.reciprocal(rstd[i][:, :], sd[i][:, :]).then_inc(rs_done[i], 1)
                dve.wait_ge(rs_done[i], count)
                for j in range(n):
                    ins = nc.vector.tensor_scalar(dst[:, j, :], src[:, j, :], mv[i][:, j, 0:1], rstd[i][:, j:j + 1],
                                                  ALU.subtract, ALU.mult)
                ins.then_inc(norm[i], 1)

            def ffn(h, p):
                t, _, _ = shift(h, p, 0)
                _, hn, pn = shift(h, p, 1)
                if within(t, 1, NP + 1):
                    wait(dve, fused_done, t - 1)
                    normalise(1, n2, t2, 4, t)
                if within(t, 2, NP + 2):
                    dve.wait_ge(conv_ready, t - 1)
                    wait(dve, h0T_done, t - 2)
                    nc.vector.tensor_reduce(ymax[:, :], cv_bank[:, 0:2 * L].rearrange("p (l two) -> p l two", two=2), AX, ALU.max).then_inc(max_done, 1)
                if within(t, -1, NP - 1):
                    dve.wait_ge(ao_ready, t + 2)
                    dve.wait_ge(xb_done, t + 2)
                    wait(dve, norm[0], t + 1)
                    nc.vector.tensor_tensor(t1[:, :, :], tok(ao_bank), xb[pn][:, :, :], ALU.add).then_inc(t1_done, 1)
                    dve.wait_ge(t1_done, t + 2)
                    stats(0, t1, 4, t + 2)
                    wait(dve, n1T_ready, t + 1)
                    wait(dve, hb_mul, t + 1)
                    normalise(0, n1, t1, 4, t + 2)
                if within(t, 2, NP + 2):
                    dve.wait_ge(h0_ready, t - 1)
                    wait(dve, h0b_done, t - 2)
                    wait(dve, norm[2], t - 2)
                    nc.vector.tensor_copy(h0[:, :, :], tok(h_bank, 2)).then_inc(h0_done, 1)
                    dve.wait_ge(h0_done, t - 1)
                    stats(2, h0, 2, t - 1)
                    wait(dve, n3T_ready, t - 2)
                    normalise(2, n3, h0, 2, t - 1)
                if within(t, 0, NP):
                    dve.wait_ge(f2_ready, t + 1)
                    dve.wait_ge(hb_done, t + 1)
                    wait(dve, norm[1], t)
                    nc.vector.tensor_tensor(t2[:, :, :], tok(f2_bank), hb[p][:, :, :], ALU.add).then_inc(t2_done, 1)
                    dve.wait_ge(t2_done, t + 1)
                    stats(1, t2, 4, t + 1)

            for i in range(2):
                nc.vector.memset(vo[i][:, :, HD:CW], 1.0).then_inc(ones_in, 1)

            def window(h, p):
                u, _, _ = shift(h, p, 0)
                um3, _, _ = shift(h, p, -3)

                def mask_and_max(r):
                    dve.wait_ge(scores, 2 * u + 1 + r)
                    nc.vector.memset(wgate[:, r:r + 1], 0.0)
                    for j in range(4 * r, 4 * r + 4):
                        s = s_bank[r][0:LH, LH * (j % 4):LH * (j % 4) + LH]
                        ins = nc.vector.tensor_tensor_reduce(s, s, c[0:LH, CONST["band"]], 1.0, OFF, ALU.add, ALU.min, negmax[p][:, j:j + 1])
                    ins.then_inc(min_done, 1)

                if within(u, 0, B):
                    mask_and_max(0)
                if within(u, 1, B + 1):
                    dve.wait_ge(pT_ready, 2 * u - 1)
                    wait(dve, pv_ready, u - 1)
                    nc.vector.tensor_copy(probsT[:, 0:4, :].rearrange("p h l -> p (h l)"), t_bank[0][0:LH, 0:4 * LH]).then_inc(pT0_done, 1)
                if within(u, 0, B):
                    mask_and_max(1)
                if within(u, 2, B + 2):
                    dve.wait_ge(otok_ready, u - 1)
                    wait(dve, otok_done, u - 2)
                    nc.vector.reciprocal(rinv[:, :], a_bank[0:LH, 0:2 * 128].rearrange("p (h f) -> p h f", h=H)[:, :, HD]).then_inc(rinv_done, 1)
                if within(u, 3, B + 3):
                    dve.wait_ge(proj_ready, u - 2)
                    if isinstance(u, int) and u == 3:
                        dve.wait_ge(h0b_done, NP)
                    nc.vector.tensor_tensor(z_all[:, bass.ds(um3, 1), :], of_bank[0:LH, 256:256 + D].unsqueeze(1), z_all[:, bass.ds(um3, 1), :], ALU.add).then_inc(z_done, 1)
                if within(u, 2, B + 2):
                    dve.wait_ge(rinv_done, u - 1)
                    wait(dve, oF_ready, u - 2)
                    nc.vector.tensor_tensor(otok[:, :].rearrange("p (h f) -> p h f", h=H),
                                            a_bank[0:LH, 0:2 * 128].rearrange("p (h f) -> p h f", h=H)[:, :, 0:HD],
                                            rinv[:, :].unsqueeze(2).to_broadcast([LH, H, HD]), ALU.mult).then_inc(otok_done, 1)
                if within(u, 3, B + 3):
                    dve.wait_ge(z_done, u - 2)
                    nc.vector.bn_stats(zst[:, bass.ds(um3, 1), :].rearrange("p a b -> p (a b)"), z_all[:, bass.ds(um3, 1), :].rearrange("p a b -> p (a b)")).then_inc(stat, 1)

            def spread(lo, hi, count):
                own_ = slice(lo, hi)
                dve.wait_ge(stat, hi)
                m0, m1, q0, q1 = (zst[:, own_, i] for i in (1, 4, 2, 5))
                nc.vector.tensor_tensor(mean[:, own_], m0, m1, ALU.add).then_inc(chain, 1)
                nc.vector.tensor_tensor(tmp[:, own_], m0, m1, ALU.subtract).then_inc(chain, 1)
                nc.vector.tensor_tensor(var[:, own_], q0, q1, ALU.add).then_inc(chain, 1)
                dve.wait_ge(chain, count + 3)
                nc.vector.tensor_tensor(tmp[:, own_], tmp[:, own_], tmp[:, own_], ALU.mult).then_inc(chain, 1)
                dve.wait_ge(chain, count + 4)
                nc.vector.scalar_tensor_tensor(var[:, own_], var[:, own_], 4.0 / D, tmp[:, own_], ALU.mult, ALU.add).then_inc(chain, 1)
                dve.wait_ge(chain, count + 5)
                nc.vector.tensor_scalar_mul(var[:, own_], var[:, own_], 0.25).then_inc(chain, 1)

            def factors(lo, hi, roots, count):
                own_ = slice(lo, hi)
                dve.wait_ge(root_done, roots)
                nc.vector.reciprocal(rs[:, own_], sdz[:, own_]).then_inc(chain, 1)
                dve.wait_ge(chain, count + 1)
                nc.vector.tensor_scalar(gain[:, own_], rs[:, own_], 1.0, None, ALU.add).then_inc(chain, 1)
                nc.vector.scalar_tensor_tensor(offs[:, own_], mean[:, own_], -0.5, rs[:, own_], ALU.mult, ALU.mult).then_inc(chain, 1)

            def output(clips, count):
                dve.wait_ge(chain, count)
                for b in clips:
                    nc.vector.tensor_scalar(o[:, b, :], z_all[:, b, :], gain[:, b:b + 1], offs[:, b:b + 1], ALU.mult, ALU.add).then_inc(out_done["D"], 1)

            in_turn(dve, ffn, window)
            early = own("D", 0, EARLY)
            spread(0, EARLY, 0)
            at(window, B)
            factors(0, EARLY, 1, 6)
            output(early[:3], 9)
            at(window, B + 1)
            output(early[3:7], 9)
            at(window, B + 2)
            spread(EARLY, B, 9)
            output(early[7:], 9)
            factors(EARLY, B, 2, 15)
            output(own("D", EARLY, B), 18)


def kernel(**inputs):
    import numpy as _np
    import concourse.bacc as _bacc
    from concourse.bass_utils import run_bass_kernel_spmd as _run

    a = {k.removeprefix("L0_"): _np.asarray(v) for k, v in inputs.items()}
    x = a["x"]
    f1_b = a["tok_f1_b"].reshape(4, 128)
    bq, bk, bv = a["attn_b_qkv"].reshape(3, D)
    arrays = {
        "xT": _np.ascontiguousarray(x.transpose(2, 0, 1).reshape(D, B * L)),
        "xtok": _np.ascontiguousarray(x.reshape(B * 2, LH, D).transpose(1, 0, 2)),
        "weights": _np.ascontiguousarray(_np.concatenate([
            a["tok_q_w"], a["tok_k_w"], a["tok_v_w"], a["tok_o_w"], a["tok_f1_w"],
            a["tok_f2_w"].reshape(4, 128, D).transpose(1, 0, 2).reshape(128, F),
            a["tok_conv_w"].transpose(1, 2, 0).reshape(D, 3 * D), a["attn_W_qkv"], a["attn_W_proj"]], axis=1)),
        "consts": constants(),
        "cols": _np.ascontiguousarray(_np.stack([
            a["tok_k_b"], a["tok_v_b"], a["tok_ln1_g"], a["tok_ln1_b"], *f1_b, a["tok_conv_b"], bq, bk, bv], axis=1)),
        "rows": _np.ascontiguousarray(_np.concatenate([
            a["tok_q_b"], a["tok_o_b"], a["tok_ln1_g"], a["tok_ln1_b"], a["tok_f2_b"], a["tok_ln2_g"], a["tok_ln2_b"],
            a["attn_b_proj"]])),
    }
    nc = _bacc.Bacc("TRN2", target_bir_lowering=False, num_devices=1)
    args = [nc.dram_tensor(n, v.shape, mybir.dt.from_np(v.dtype), kind="ExternalInput").ap() for n, v in arrays.items()]
    key_dram = nc.dram_tensor("key_scratch", (B * H, L), BF16, kind="Internal").ap()
    out = nc.dram_tensor("out", (B, LH, D), F32, kind="ExternalOutput").ap()
    program(nc, *args, key_dram, out)
    return _run(nc, [arrays], core_ids=[0]).results[0]["out"]
```
